# Optimizing a Trainium2 kernel written in Bass

```python
import numpy as np
import jax
import jax.numpy as jnp

def _softmax(x, axis=-1):
    return jax.nn.softmax(x, axis=axis)

def _gelu(x):
    return jax.nn.gelu(x, approximate=True)

def _silu(x):
    return jax.nn.silu(x)

def _sigmoid(x):
    return jax.nn.sigmoid(x)

def _layernorm(x, axis=-1, eps=1e-05):
    m = jnp.mean(x, axis=axis, keepdims=True)
    v = jnp.var(x, axis=axis, keepdims=True)
    return (x - m) / jnp.sqrt(v + eps)

def _scatter_add(tgt, idx, src, axis=0):
    return tgt.at[idx].add(src)

def _segment_sum(src, seg, n):
    return jax.ops.segment_sum(src, seg, n)
kernel_name = 'mk_conv_preact_d4_conv_nhwc768_r4_ed9d26'

def setup_inputs(seed: int=0):
    np.random.seed(seed)
    _w = jnp.asarray

    def _rec_inputs():
        import jax
        import jax.numpy as jnp
        _gk = jax.random.key(seed)
        x = -0.0005058 + 1 * jax.random.normal(jax.random.fold_in(_gk, 1), (2, 48, 48, 192), jnp.float32)
        return x
    x = _rec_inputs()

    def _L0_conv_setup():
        import jax, jax.numpy as jnp
        import numpy as np
        D_MODEL = 192
        D_HEAD = 16
        N_HEADS = D_MODEL // D_HEAD
        KERNEL = 7
        NEG_INF = -1e+30

        def make_neighbourhood_mask(kernel_h, kernel_w, canvas_h, canvas_w):
            h_ramp = jnp.arange(canvas_h)
            w_ramp = jnp.arange(canvas_w)
            h_pos, w_pos = jnp.meshgrid(h_ramp, w_ramp, indexing='ij')
            start_h = jnp.clip(h_pos - kernel_h // 2, 0, canvas_h - kernel_h)[..., None, None]
            end_h = start_h + kernel_h
            start_w = jnp.clip(w_pos - kernel_w // 2, 0, canvas_w - kernel_w)[..., None, None]
            end_w = start_w + kernel_w
            h_range = h_ramp.reshape(1, 1, canvas_h, 1)
            w_range = w_ramp.reshape(1, 1, 1, canvas_w)
            mask = (h_range >= start_h) & (h_range < end_h) & (w_range >= start_w) & (w_range < end_w)
            return mask.reshape(canvas_h * canvas_w, canvas_h * canvas_w)
        key = jax.random.key(seed)
        k1, k2, k3, k4, k5, k6 = jax.random.split(key, 6)
        x = jax.random.normal(k1, (2, 48, 48, D_MODEL), dtype=jnp.float32)
        registers = jax.random.normal(k2, (16, D_MODEL), dtype=jnp.float32)
        scale = 1.0 / np.sqrt(D_MODEL)
        qkv_w = jax.random.normal(k3, (3 * D_MODEL, D_MODEL), dtype=jnp.float32) * scale
        qkv_b = jax.random.normal(k4, (3 * D_MODEL,), dtype=jnp.float32) * 0.01
        out_w = jax.random.normal(k5, (D_MODEL, D_MODEL), dtype=jnp.float32) * scale
        out_b = jax.random.normal(k6, (D_MODEL,), dtype=jnp.float32) * 0.01
        return {'x': x, 'registers': registers, 'qkv_w': qkv_w, 'qkv_b': qkv_b, 'out_w': out_w, 'out_b': out_b}
    _L0_conv_all = _L0_conv_setup()
    _L0_conv_in = {k: v for k, v in _L0_conv_all.items() if k in ('registers', 'qkv_w', 'qkv_b', 'out_w', 'out_b')}
    del _L0_conv_all

    def _L1_conv_setup():
        import jax, jax.numpy as jnp
        import numpy as np
        B_, H_, W_, DM = (4, 16, 16, 192)
        DI = int(0.5 * DM)
        N = 16
        R = -(-DM // 16)
        K = 4

        def selective_scan(xs, dts, As, Bs, Cs, Dsk):
            u = jnp.moveaxis(xs, -1, 0)
            d = jnp.moveaxis(dts, -1, 0)
            Bt = jnp.moveaxis(Bs, -1, 0)
            Ct = jnp.moveaxis(Cs, -1, 0)

            def step(h, inp):
                u_t, d_t, B_t, C_t = inp
                dA = jnp.exp(d_t[..., None] * As)
                h = h * dA + (d_t * u_t)[..., None] * B_t[:, :, None, :]
                y = jnp.einsum('bkcn,bkn->bkc', h, C_t)
                return (h, y)
            h0 = jnp.zeros(u.shape[1:] + (As.shape[-1],), u.dtype)
            _, ys = jax.lax.scan(step, h0, (u, d, Bt, Ct))
            ys = jnp.moveaxis(ys, 0, -1)
            return ys + Dsk[None, :, :, None] * xs
        key = jax.random.key(seed)
        ks = jax.random.split(key, 8)
        s = lambda i, shape, sc=0.02: jax.random.normal(ks[i], shape, jnp.float32) * sc
        return dict(x=jax.random.normal(ks[0], (B_, H_, W_, DM), jnp.float32), in_proj_w=s(1, (2 * DI, DM)), conv_w=s(2, (DI, 1, 3, 3)), conv_b=jnp.zeros((DI,), jnp.float32), x_proj_w=s(3, (K, R + 2 * N, DI)), dt_projs_w=s(4, (K, DI, R)), dt_projs_b=s(5, (K, DI)), A_logs=jnp.log(jnp.tile(jnp.arange(1, N + 1, dtype=jnp.float32)[None, :], (K * DI, 1))), Ds=jnp.ones((K * DI,), jnp.float32), out_norm_g=jnp.ones((DI,), jnp.float32), out_norm_b=jnp.zeros((DI,), jnp.float32), out_proj_w=s(6, (DM, DI)))
    _L1_conv_all = _L1_conv_setup()
    _L1_conv_in = {k: v for k, v in _L1_conv_all.items() if k in ('in_proj_w', 'conv_w', 'conv_b', 'x_proj_w', 'dt_projs_w', 'dt_projs_b', 'A_logs', 'Ds', 'out_norm_g', 'out_norm_b', 'out_proj_w')}
    del _L1_conv_all

    def _L2_conv_setup():
        import jax, jax.numpy as jnp
        import numpy as np
        B_, H_, W_, DM = (4, 16, 16, 192)
        DI = int(0.5 * DM)
        N = 16
        R = -(-DM // 16)
        K = 4

        def selective_scan(xs, dts, As, Bs, Cs, Dsk):
            u = jnp.moveaxis(xs, -1, 0)
            d = jnp.moveaxis(dts, -1, 0)
            Bt = jnp.moveaxis(Bs, -1, 0)
            Ct = jnp.moveaxis(Cs, -1, 0)

            def step(h, inp):
                u_t, d_t, B_t, C_t = inp
                dA = jnp.exp(d_t[..., None] * As)
                h = h * dA + (d_t * u_t)[..., None] * B_t[:, :, None, :]
                y = jnp.einsum('bkcn,bkn->bkc', h, C_t)
                return (h, y)
            h0 = jnp.zeros(u.shape[1:] + (As.shape[-1],), u.dtype)
            _, ys = jax.lax.scan(step, h0, (u, d, Bt, Ct))
            ys = jnp.moveaxis(ys, 0, -1)
            return ys + Dsk[None, :, :, None] * xs
        key = jax.random.key(seed)
        ks = jax.random.split(key, 8)
        s = lambda i, shape, sc=0.02: jax.random.normal(ks[i], shape, jnp.float32) * sc
        return dict(x=jax.random.normal(ks[0], (B_, H_, W_, DM), jnp.float32), in_proj_w=s(1, (2 * DI, DM)), conv_w=s(2, (DI, 1, 3, 3)), conv_b=jnp.zeros((DI,), jnp.float32), x_proj_w=s(3, (K, R + 2 * N, DI)), dt_projs_w=s(4, (K, DI, R)), dt_projs_b=s(5, (K, DI)), A_logs=jnp.log(jnp.tile(jnp.arange(1, N + 1, dtype=jnp.float32)[None, :], (K * DI, 1))), Ds=jnp.ones((K * DI,), jnp.float32), out_norm_g=jnp.ones((DI,), jnp.float32), out_norm_b=jnp.zeros((DI,), jnp.float32), out_proj_w=s(6, (DM, DI)))
    _L2_conv_all = _L2_conv_setup()
    _L2_conv_in = {k: v for k, v in _L2_conv_all.items() if k in ('in_proj_w', 'conv_w', 'conv_b', 'x_proj_w', 'dt_projs_w', 'dt_projs_b', 'A_logs', 'Ds', 'out_norm_g', 'out_norm_b', 'out_proj_w')}
    del _L2_conv_all

    def _L3_conv_setup():
        import jax, jax.numpy as jnp
        import numpy as np
        B, H, W, C = (1, 16, 16, 192)
        NUM_HEADS = 12
        HEAD_DIM = C // NUM_HEADS
        key = jax.random.key(seed)
        ks = jax.random.split(key, 7)
        s = 0.02
        return {'imagelike_bhwc': jax.random.normal(ks[0], (B, H, W, C), dtype=jnp.float32), 'qkv_w': jax.random.normal(ks[1], (C, 3 * C), dtype=jnp.float32) * s, 'qkv_b': jax.random.normal(ks[2], (3 * C,), dtype=jnp.float32) * s, 'proj_w': jax.random.normal(ks[3], (C, C), dtype=jnp.float32) * s, 'proj_b': jax.random.normal(ks[4], (C,), dtype=jnp.float32) * s, 'rel_pos_h': jax.random.normal(ks[5], (2 * H - 1, HEAD_DIM), dtype=jnp.float32) * s, 'rel_pos_w': jax.random.normal(ks[6], (2 * W - 1, HEAD_DIM), dtype=jnp.float32) * s}
    _L3_conv_all = _L3_conv_setup()
    _L3_conv_in = {k: v for k, v in _L3_conv_all.items() if k in ('qkv_w', 'qkv_b', 'proj_w', 'proj_b', 'rel_pos_h', 'rel_pos_w')}
    del _L3_conv_all
    return {'x': x, 'L0_conv_registers': _L0_conv_in['registers'], 'L0_conv_qkv_w': _L0_conv_in['qkv_w'], 'L0_conv_qkv_b': _L0_conv_in['qkv_b'], 'L0_conv_out_w': _L0_conv_in['out_w'], 'L0_conv_out_b': _L0_conv_in['out_b'], 'L1_conv_in_proj_w': _L1_conv_in['in_proj_w'], 'L1_conv_conv_w': _L1_conv_in['conv_w'], 'L1_conv_conv_b': _L1_conv_in['conv_b'], 'L1_conv_x_proj_w': _L1_conv_in['x_proj_w'], 'L1_conv_dt_projs_w': _L1_conv_in['dt_projs_w'], 'L1_conv_dt_projs_b': _L1_conv_in['dt_projs_b'], 'L1_conv_A_logs': _L1_conv_in['A_logs'], 'L1_conv_Ds': _L1_conv_in['Ds'], 'L1_conv_out_norm_g': _L1_conv_in['out_norm_g'], 'L1_conv_out_norm_b': _L1_conv_in['out_norm_b'], 'L1_conv_out_proj_w': _L1_conv_in['out_proj_w'], 'L2_conv_in_proj_w': _L2_conv_in['in_proj_w'], 'L2_conv_conv_w': _L2_conv_in['conv_w'], 'L2_conv_conv_b': _L2_conv_in['conv_b'], 'L2_conv_x_proj_w': _L2_conv_in['x_proj_w'], 'L2_conv_dt_projs_w': _L2_conv_in['dt_projs_w'], 'L2_conv_dt_projs_b': _L2_conv_in['dt_projs_b'], 'L2_conv_A_logs': _L2_conv_in['A_logs'], 'L2_conv_Ds': _L2_conv_in['Ds'], 'L2_conv_out_norm_g': _L2_conv_in['out_norm_g'], 'L2_conv_out_norm_b': _L2_conv_in['out_norm_b'], 'L2_conv_out_proj_w': _L2_conv_in['out_proj_w'], 'L3_conv_qkv_w': _L3_conv_in['qkv_w'], 'L3_conv_qkv_b': _L3_conv_in['qkv_b'], 'L3_conv_proj_w': _L3_conv_in['proj_w'], 'L3_conv_proj_b': _L3_conv_in['proj_b'], 'L3_conv_rel_pos_h': _L3_conv_in['rel_pos_h'], 'L3_conv_rel_pos_w': _L3_conv_in['rel_pos_w']}

def reference(x, L0_conv_registers, L0_conv_qkv_w, L0_conv_qkv_b, L0_conv_out_w, L0_conv_out_b, L1_conv_in_proj_w, L1_conv_conv_w, L1_conv_conv_b, L1_conv_x_proj_w, L1_conv_dt_projs_w, L1_conv_dt_projs_b, L1_conv_A_logs, L1_conv_Ds, L1_conv_out_norm_g, L1_conv_out_norm_b, L1_conv_out_proj_w, L2_conv_in_proj_w, L2_conv_conv_w, L2_conv_conv_b, L2_conv_x_proj_w, L2_conv_dt_projs_w, L2_conv_dt_projs_b, L2_conv_A_logs, L2_conv_Ds, L2_conv_out_norm_g, L2_conv_out_norm_b, L2_conv_out_proj_w, L3_conv_qkv_w, L3_conv_qkv_b, L3_conv_proj_w, L3_conv_proj_b, L3_conv_rel_pos_h, L3_conv_rel_pos_w):
    import jax
    import jax.numpy as jnp

    def _L0_conv_ref(x, registers, qkv_w, qkv_b, out_w, out_b):
        import jax, jax.numpy as jnp
        import numpy as np
        D_MODEL = 192
        D_HEAD = 16
        N_HEADS = D_MODEL // D_HEAD
        KERNEL = 7
        NEG_INF = -1e+30

        def make_neighbourhood_mask(kernel_h, kernel_w, canvas_h, canvas_w):
            h_ramp = jnp.arange(canvas_h)
            w_ramp = jnp.arange(canvas_w)
            h_pos, w_pos = jnp.meshgrid(h_ramp, w_ramp, indexing='ij')
            start_h = jnp.clip(h_pos - kernel_h // 2, 0, canvas_h - kernel_h)[..., None, None]
            end_h = start_h + kernel_h
            start_w = jnp.clip(w_pos - kernel_w // 2, 0, canvas_w - kernel_w)[..., None, None]
            end_w = start_w + kernel_w
            h_range = h_ramp.reshape(1, 1, canvas_h, 1)
            w_range = w_ramp.reshape(1, 1, 1, canvas_w)
            mask = (h_range >= start_h) & (h_range < end_h) & (w_range >= start_w) & (w_range < end_w)
            return mask.reshape(canvas_h * canvas_w, canvas_h * canvas_w)
        n, h, w, _ = x.shape
        nh, e = (N_HEADS, D_HEAD)
        s = h * w
        r = registers.shape[0]
        qkv = x @ qkv_w.T + qkv_b
        qkv = qkv.reshape(n, h, w, 3, nh, e)
        qkv = qkv.transpose(3, 0, 4, 1, 2, 5).reshape(3, n, nh, s, e)
        q, k, v = (qkv[0], qkv[1], qkv[2])
        reg_kv = registers @ qkv_w[D_MODEL:].T + qkv_b[D_MODEL:]
        reg_kv = reg_kv.reshape(r, 2, nh, e).transpose(1, 2, 0, 3)
        reg_k = jnp.broadcast_to(reg_kv[0][None], (n, nh, r, e))
        reg_v = jnp.broadcast_to(reg_kv[1][None], (n, nh, r, e))
        k_cat = jnp.concatenate([k, reg_k], axis=-2)
        v_cat = jnp.concatenate([v, reg_v], axis=-2)
        mask = make_neighbourhood_mask(KERNEL, KERNEL, h, w)
        mask_cat = jnp.concatenate([mask, jnp.ones((s, r), dtype=bool)], axis=-1)
        scale = 1.0 / jnp.sqrt(jnp.asarray(e, dtype=x.dtype))
        scores = jnp.einsum('bnqe,bnke->bnqk', q, k_cat) * scale
        scores = jnp.where(mask_cat[None, None], scores, NEG_INF)
        attn = jax.nn.softmax(scores, axis=-1)
        o = jnp.einsum('bnqk,bnke->bnqe', attn, v_cat)
        o = o.transpose(0, 2, 1, 3).reshape(n, h, w, nh * e)
        return o @ out_w.T + out_b

    def _L1_conv_ref(x, in_proj_w, conv_w, conv_b, x_proj_w, dt_projs_w, dt_projs_b, A_logs, Ds, out_norm_g, out_norm_b, out_proj_w):
        import jax, jax.numpy as jnp
        import numpy as np
        B_, H_, W_, DM = (4, 16, 16, 192)
        DI = int(0.5 * DM)
        N = 16
        R = -(-DM // 16)
        K = 4

        def selective_scan(xs, dts, As, Bs, Cs, Dsk):
            u = jnp.moveaxis(xs, -1, 0)
            d = jnp.moveaxis(dts, -1, 0)
            Bt = jnp.moveaxis(Bs, -1, 0)
            Ct = jnp.moveaxis(Cs, -1, 0)

            def step(h, inp):
                u_t, d_t, B_t, C_t = inp
                dA = jnp.exp(d_t[..., None] * As)
                h = h * dA + (d_t * u_t)[..., None] * B_t[:, :, None, :]
                y = jnp.einsum('bkcn,bkn->bkc', h, C_t)
                return (h, y)
            h0 = jnp.zeros(u.shape[1:] + (As.shape[-1],), u.dtype)
            _, ys = jax.lax.scan(step, h0, (u, d, Bt, Ct))
            ys = jnp.moveaxis(ys, 0, -1)
            return ys + Dsk[None, :, :, None] * xs
        B, H, W, _ = x.shape
        L = H * W
        xz = x @ in_proj_w.T
        xh, z = jnp.split(xz, 2, axis=-1)
        xc = jnp.transpose(xh, (0, 3, 1, 2))
        xc = jax.lax.conv_general_dilated(xc, conv_w, (1, 1), 'SAME', feature_group_count=DI)
        xc = jax.nn.silu(xc + conv_b[None, :, None, None])
        x_flat = xc.reshape(B, DI, L)
        x_t = jnp.transpose(xc, (0, 1, 3, 2)).reshape(B, DI, L)
        x_hwwh = jnp.stack([x_flat, x_t], 1)
        xs = jnp.concatenate([x_hwwh, jnp.flip(x_hwwh, -1)], 1)
        x_dbl = jnp.einsum('bkdl,kcd->bkcl', xs, x_proj_w)
        dts, Bs, Cs = jnp.split(x_dbl, [R, R + N], axis=2)
        dts = jnp.einsum('bkrl,kdr->bkdl', dts, dt_projs_w)
        dts = jax.nn.softplus(dts + dt_projs_b[None, :, :, None])
        As = -jnp.exp(A_logs).reshape(K, DI, N)
        out_y = selective_scan(xs, dts, As, Bs, Cs, Ds.reshape(K, DI))
        inv_y = jnp.flip(out_y[:, 2:4], -1)
        wh_y = jnp.transpose(out_y[:, 1].reshape(B, DI, W, H), (0, 1, 3, 2)).reshape(B, DI, L)
        invwh_y = jnp.transpose(inv_y[:, 1].reshape(B, DI, W, H), (0, 1, 3, 2)).reshape(B, DI, L)
        y = out_y[:, 0] + inv_y[:, 0] + wh_y + invwh_y
        y = jnp.transpose(y, (0, 2, 1)).reshape(B, H, W, DI)
        mu = y.mean(-1, keepdims=True)
        var = y.var(-1, keepdims=True)
        y = (y - mu) / jnp.sqrt(var + 1e-05) * out_norm_g + out_norm_b
        y = y * jax.nn.silu(z)
        return y @ out_proj_w.T

    def _L2_conv_ref(x, in_proj_w, conv_w, conv_b, x_proj_w, dt_projs_w, dt_projs_b, A_logs, Ds, out_norm_g, out_norm_b, out_proj_w):
        import jax, jax.numpy as jnp
        import numpy as np
        B_, H_, W_, DM = (4, 16, 16, 192)
        DI = int(0.5 * DM)
        N = 16
        R = -(-DM // 16)
        K = 4

        def selective_scan(xs, dts, As, Bs, Cs, Dsk):
            u = jnp.moveaxis(xs, -1, 0)
            d = jnp.moveaxis(dts, -1, 0)
            Bt = jnp.moveaxis(Bs, -1, 0)
            Ct = jnp.moveaxis(Cs, -1, 0)

            def step(h, inp):
                u_t, d_t, B_t, C_t = inp
                dA = jnp.exp(d_t[..., None] * As)
                h = h * dA + (d_t * u_t)[..., None] * B_t[:, :, None, :]
                y = jnp.einsum('bkcn,bkn->bkc', h, C_t)
                return (h, y)
            h0 = jnp.zeros(u.shape[1:] + (As.shape[-1],), u.dtype)
            _, ys = jax.lax.scan(step, h0, (u, d, Bt, Ct))
            ys = jnp.moveaxis(ys, 0, -1)
            return ys + Dsk[None, :, :, None] * xs
        B, H, W, _ = x.shape
        L = H * W
        xz = x @ in_proj_w.T
        xh, z = jnp.split(xz, 2, axis=-1)
        xc = jnp.transpose(xh, (0, 3, 1, 2))
        xc = jax.lax.conv_general_dilated(xc, conv_w, (1, 1), 'SAME', feature_group_count=DI)
        xc = jax.nn.silu(xc + conv_b[None, :, None, None])
        x_flat = xc.reshape(B, DI, L)
        x_t = jnp.transpose(xc, (0, 1, 3, 2)).reshape(B, DI, L)
        x_hwwh = jnp.stack([x_flat, x_t], 1)
        xs = jnp.concatenate([x_hwwh, jnp.flip(x_hwwh, -1)], 1)
        x_dbl = jnp.einsum('bkdl,kcd->bkcl', xs, x_proj_w)
        dts, Bs, Cs = jnp.split(x_dbl, [R, R + N], axis=2)
        dts = jnp.einsum('bkrl,kdr->bkdl', dts, dt_projs_w)
        dts = jax.nn.softplus(dts + dt_projs_b[None, :, :, None])
        As = -jnp.exp(A_logs).reshape(K, DI, N)
        out_y = selective_scan(xs, dts, As, Bs, Cs, Ds.reshape(K, DI))
        inv_y = jnp.flip(out_y[:, 2:4], -1)
        wh_y = jnp.transpose(out_y[:, 1].reshape(B, DI, W, H), (0, 1, 3, 2)).reshape(B, DI, L)
        invwh_y = jnp.transpose(inv_y[:, 1].reshape(B, DI, W, H), (0, 1, 3, 2)).reshape(B, DI, L)
        y = out_y[:, 0] + inv_y[:, 0] + wh_y + invwh_y
        y = jnp.transpose(y, (0, 2, 1)).reshape(B, H, W, DI)
        mu = y.mean(-1, keepdims=True)
        var = y.var(-1, keepdims=True)
        y = (y - mu) / jnp.sqrt(var + 1e-05) * out_norm_g + out_norm_b
        y = y * jax.nn.silu(z)
        return y @ out_proj_w.T

    def _L3_conv_ref(imagelike_bhwc, qkv_w, qkv_b, proj_w, proj_b, rel_pos_h, rel_pos_w):
        import jax, jax.numpy as jnp
        import numpy as np
        B, H, W, C = (1, 16, 16, 192)
        NUM_HEADS = 12
        HEAD_DIM = C // NUM_HEADS
        b, h, w, c = imagelike_bhwc.shape
        n = h * w
        nh, hd = (NUM_HEADS, c // NUM_HEADS)
        scale = hd ** (-0.5)
        qkv = imagelike_bhwc @ qkv_w + qkv_b
        qkv = qkv.reshape(b, n, 3, nh, hd).transpose(2, 0, 3, 1, 4).reshape(3, b * nh, n, hd)
        q, k, v = (qkv[0], qkv[1], qkv[2])
        attn = jnp.einsum('bqd,bkd->bqk', q * scale, k)
        idx_h = jnp.arange(h)[:, None] - jnp.arange(h)[None, :] + (h - 1)
        idx_w = jnp.arange(w)[:, None] - jnp.arange(w)[None, :] + (w - 1)
        Rh = rel_pos_h[idx_h]
        Rw = rel_pos_w[idx_w]
        r_q = q.reshape(b * nh, h, w, hd)
        rel_h = jnp.einsum('bhwc,hkc->bhwk', r_q, Rh)
        rel_w = jnp.einsum('bhwc,wkc->bhwk', r_q, Rw)
        bias = (rel_h[:, :, :, :, None] + rel_w[:, :, :, None, :]).reshape(b * nh, n, n)
        attn = jax.nn.softmax(attn + bias, axis=-1)
        out = jnp.einsum('bqk,bkd->bqd', attn, v)
        out = out.reshape(b, nh, h, w, hd).transpose(0, 2, 3, 1, 4).reshape(b, h, w, c)
        return out @ proj_w + proj_b

    def _gn(v, G=32, eps=1e-05):
        B_, H_, W_, C_ = v.shape
        g = v.reshape(B_, H_, W_, G, C_ // G)
        m = jnp.mean(g, axis=(1, 2, 4), keepdims=True)
        s = jnp.var(g, axis=(1, 2, 4), keepdims=True)
        return ((g - m) / jnp.sqrt(s + eps)).reshape(v.shape)

    def _ln_c(v, eps=1e-06):
        m = jnp.mean(v, axis=-1, keepdims=True)
        s = jnp.var(v, axis=-1, keepdims=True)
        return (v - m) / jnp.sqrt(s + eps)

    def _ln_t(v, eps=1e-05):
        m = jnp.mean(v, axis=-1, keepdims=True)
        s = jnp.var(v, axis=-1, keepdims=True)
        return (v - m) / jnp.sqrt(s + eps)

    def _to_tokens(v):
        B_, H_, W_, C_ = v.shape
        return v.reshape(B_, H_ * W_, C_)

    def _from_tokens(t, like):
        return t.reshape(like.shape)
    x = x + _L0_conv_ref(_gn(x), L0_conv_registers, L0_conv_qkv_w, L0_conv_qkv_b, L0_conv_out_w, L0_conv_out_b)
    x = x + _L1_conv_ref(_gn(x), L1_conv_in_proj_w, L1_conv_conv_w, L1_conv_conv_b, L1_conv_x_proj_w, L1_conv_dt_projs_w, L1_conv_dt_projs_b, L1_conv_A_logs, L1_conv_Ds, L1_conv_out_norm_g, L1_conv_out_norm_b, L1_conv_out_proj_w)
    x = x + _L2_conv_ref(_gn(x), L2_conv_in_proj_w, L2_conv_conv_w, L2_conv_conv_b, L2_conv_x_proj_w, L2_conv_dt_projs_w, L2_conv_dt_projs_b, L2_conv_A_logs, L2_conv_Ds, L2_conv_out_norm_g, L2_conv_out_norm_b, L2_conv_out_proj_w)
    x = x + _L3_conv_ref(_gn(x), L3_conv_qkv_w, L3_conv_qkv_b, L3_conv_proj_w, L3_conv_proj_b, L3_conv_rel_pos_h, L3_conv_rel_pos_w)
    return x

_drawn_inputs = setup_inputs


def setup_inputs(seed=0):
    import zlib

    import numpy as np

    out = dict(_drawn_inputs(seed))
    spreads = {'L1_conv_conv_b': (0.0, 0.1),
     'L1_conv_Ds': (1.0, 0.6),
     'L1_conv_out_norm_g': (1.0, 0.6),
     'L1_conv_out_norm_b': (0.0, 0.8),
     'L2_conv_conv_b': (0.0, 0.1),
     'L2_conv_Ds': (1.0, 0.6),
     'L2_conv_out_norm_g': (1.0, 0.6),
     'L2_conv_out_norm_b': (0.0, 0.8)}
    factors = {'L0_conv_qkv_b': 5.777,
     'L0_conv_out_b': 5.459,
     'L1_conv_conv_w': 8.0,
     'L1_conv_x_proj_w': 64.0,
     'L1_conv_dt_projs_w': 64.0,
     'L1_conv_dt_projs_b': 64.0,
     'L1_conv_A_logs': 64.0,
     'L2_conv_conv_w': 8.0,
     'L2_conv_x_proj_w': 64.0,
     'L2_conv_dt_projs_w': 64.0,
     'L2_conv_dt_projs_b': 64.0,
     'L2_conv_A_logs': 64.0,
     'L3_conv_qkv_w': 8.0,
     'L3_conv_qkv_b': 8.0,
     'L3_conv_proj_w': 6.021,
     'L3_conv_proj_b': 3.006,
     'L3_conv_rel_pos_h': 8.0,
     'L3_conv_rel_pos_w': 8.0}
    for name, (base, spread) in spreads.items():
        noise = np.random.default_rng([zlib.crc32(name.encode()), seed]).standard_normal(out[name].shape)
        drawn = base * np.exp(spread * noise) if base else spread * noise
        out[name] = jnp.asarray(drawn.astype(out[name].dtype))
    for name, factor in factors.items():
        out[name] = (out[name] * factor).astype(out[name].dtype)
    return out
```

```python
from contextlib import ExitStack

import numpy as np

import concourse.bass as bass
from concourse import mybir

F32 = mybir.dt.float32
F16 = mybir.dt.float16
BF16 = mybir.dt.bfloat16
ALU = mybir.AluOpType
ACT = mybir.ActivationFunctionType
AX_X = mybir.AxisListType.X

B, H, W, C = 2, 48, 48, 192
L = H * W
TOK = B * L
CP, CC = 96, 2
NH, HD = 12, 16
HPC = CP // HD
BH = B * NH
GROUPS = 32
GC = C // GROUPS
CH = 512
LCH = [(s, min(CH, L - s)) for s in range(0, L, CH)]
TCH = [(s, CH) for s in range(0, TOK, CH)]
NREG = 16
WIN = 7
PH, PW = 8, 16
NPH, NPW = H // PH, W // PW
NPT = NPH * NPW
KH, KW = PH + WIN - 1, PW + WIN - 1
CUTS = [(0, 5), (5, 5), (10, 4)]
WK = KH * KW
LK = L + NREG
VE = HD + 1
DI, NS, DT_R, ND = 96, 16, 12, 4
QUARTER = HD ** -0.5
A_MOST, DT_LEAST = 2.0 ** 115, 2.0 ** -109


class Chain:

    def __init__(self, eng, sem, base=0):
        self.eng, self.sem, self.base, self.n = eng, sem, base, 0

    def __call__(self, ins):
        self.n += 1
        ins.then_inc(self.sem, 1)
        self.eng.wait_ge(self.sem, self.base + self.n)


class Scope:

    def __init__(self, nc, name):
        self.nc, self.name, self.stack, self.sems = nc, name, ExitStack(), []

    def __enter__(self):
        return self

    def __exit__(self, *a):
        if self.sems:
            self.nc.clear_and_free_semaphores(self.sems)
            self.nc.all_engine_barrier()
        return self.stack.__exit__(*a)

    def sb(self, name, shape, dtype=F32):
        return self.stack.enter_context(self.nc.sbuf_tensor(f"{self.name}_{name}", shape, dtype))

    def ps(self, name, shape, dtype=F32):
        return self.stack.enter_context(self.nc.psum_tensor(f"{self.name}_{name}", shape, dtype))

    def sem(self, name):
        self.sems.append(self.nc.alloc_semaphore(f"{self.name}_{name}"))
        return self.sems[-1]

    def block(self):
        return self.nc.Block()


def group_norm(nc, name, X, XN, group_mean, load=None):
    with Scope(nc, name) as s:
        stats = s.sb("stats", [CP, CC * B, len(LCH), 6])
        mv = s.sb("mv", [CP, CC * B, 2])
        gmean = s.sb("gmean", [CP, CC * B])
        dev = s.sb("dev", [CP, CC * B])
        spread = s.sb("spread", [CP, CC * B])
        sd = s.sb("sd", [CP, CC * B])
        rstd = s.sb("rstd", [CP, CC * B])
        shift = s.sb("shift", [CP, CC * B])
        gm_ps = s.ps("gm_ps", [CP, 512])
        gv_ps = s.ps("gv_ps", [CP, 512])
        loaded = s.sem("loaded")
        channel_ready, gm_ready, spread_ready, gv_ready = (
            s.sem(n) for n in ("channel", "gm", "spread", "gv"))
        var_ready, sd_ready, affine_ready, own = (s.sem(n) for n in ("var", "sd", "affine", "own"))
        xn_dve, xn_act = s.sem("xn_dve"), s.sem("xn_act")
        parts = [(c, b) for c in range(CC) for b in range(B)]
        with s.block() as block:
            if load is not None:
                @block.sync
                def _(sp):
                    load(sp, loaded)

            @block.vector
            def _(dve):
                link = Chain(dve, own)
                if load is not None:
                    dve.wait_ge(loaded, load.total)
                for n, (c, b) in enumerate(parts):
                    for k, (at, w) in enumerate(LCH):
                        last = dve.bn_stats(stats[:, n, k, :], X[:, c, b * L + at:b * L + at + w])
                link(last)
                for n in range(len(parts)):
                    last = dve.bn_aggr(mv[:, n, :], stats[:, n, :, :].rearrange("p k s -> p (k s)"))
                last.then_inc(channel_ready, 1)
                dve.wait_ge(gm_ready, 1)
                dve.tensor_copy(gmean[:], gm_ps[:, 0:CC * B]).then_inc(own, 1)
                link.n += 1
                link(dve.tensor_tensor(dev[:], mv[:, :, 0], gm_ps[:, 0:CC * B], ALU.subtract))
                link(dve.tensor_tensor(spread[:], dev[:], dev[:], ALU.mult))
                link(dve.tensor_tensor(spread[:], spread[:], mv[:, :, 1], ALU.add))
                dve.sem_inc(spread_ready, 1)
                dve.wait_ge(gv_ready, 1)
                dve.tensor_scalar(sd[:], gv_ps[:, 0:CC * B], 1e-5, None, ALU.add).then_inc(var_ready, 1)
                dve.wait_ge(sd_ready, 1)
                link(dve.reciprocal(rstd[:], sd[:]))
                dve.scalar_tensor_tensor(shift[:], gmean[:], -1.0, rstd[:], ALU.mult, ALU.mult)\
                   .then_inc(affine_ready, 1)
                dve.wait_ge(affine_ready, 1)
                for n, (c, b) in enumerate(parts):
                    if n % 2:
                        dve.tensor_scalar(XN[:, c, b * L:(b + 1) * L], X[:, c, b * L:(b + 1) * L],
                                          rstd[:, n:n + 1], shift[:, n:n + 1], ALU.mult, ALU.add)\
                           .then_inc(xn_dve, 1)
                dve.wait_ge(xn_dve, 2)

            @block.tensor
            def _(pe):
                pe.wait_ge(channel_ready, 1)
                pe.matmul(gm_ps[:, 0:CC * B], group_mean[:, :], mv[:, :, 0], start=True, stop=True)\
                  .then_inc(gm_ready, 1)
                pe.wait_ge(spread_ready, 1)
                pe.matmul(gv_ps[:, 0:CC * B], group_mean[:, :], spread[:], start=True, stop=True)\
                  .then_inc(gv_ready, 1)

            @block.scalar
            def _(act):
                act.wait_ge(var_ready, 1)
                act.activation(sd[:], sd[:], ACT.Sqrt).then_inc(sd_ready, 1)
                act.wait_ge(affine_ready, 1)
                for n, (c, b) in enumerate(parts):
                    if n % 2 == 0:
                        act.activation(XN[:, c, b * L:(b + 1) * L], X[:, c, b * L:(b + 1) * L],
                                       ACT.Identity, scale=rstd[:, n:n + 1], bias=shift[:, n:n + 1])\
                           .then_inc(xn_act, 1)
                act.wait_ge(xn_act, 2)


def out_projection(nc, name, X, OT, wT, bias_dram, rows, chunks):
    with Scope(nc, name) as s:
        w_sb = s.sb("w", [rows, chunks, C])
        b_sb = s.sb("b", [CP, CC])
        acc = [s.ps(f"acc{i}", [CP, CH]) for i in range(4)]
        loaded, ready, added = s.sem("loaded"), s.sem("ready"), s.sem("added")
        jobs = [(m, at, w) for m in range(CC) for at, w in TCH]
        with s.block() as block:
            @block.sync
            def _(sp):
                sp.dma_start(w_sb[:], wT.rearrange("(k p) n -> p k n", p=rows)).then_inc(loaded, 16)
                if bias_dram is not None:
                    with nc.allow_non_contiguous_dma(reason="a bias column"):
                        sp.dma_start(b_sb[:], bias_dram.rearrange("(c p) -> p c", p=CP)).then_inc(loaded, 16)
                sp.wait_ge(loaded, 32 if bias_dram is not None else 16)

            @block.tensor
            def _(pe):
                pe.wait_ge(loaded, 32 if bias_dram is not None else 16)
                for n, (m, at, w) in enumerate(jobs):
                    if n >= 4:
                        pe.wait_ge(added, n - 3)
                    for k in range(chunks):
                        mm = pe.matmul(acc[n % 4][:, 0:w], w_sb[:, k, m * CP:(m + 1) * CP],
                                       OT[:, k, at:at + w], start=k == 0, stop=k == chunks - 1)
                    mm.then_inc(ready, 1)

            @block.vector
            def _(dve):
                for n, (m, at, w) in enumerate(jobs):
                    dve.wait_ge(ready, n + 1)
                    x = X[:, m, at:at + w]
                    if bias_dram is not None:
                        dve.scalar_tensor_tensor(x, acc[n % 4][:, 0:w], b_sb[:, m:m + 1], x,
                                                 ALU.add, ALU.add).then_inc(added, 1)
                    else:
                        dve.tensor_tensor(x, acc[n % 4][:, 0:w], x, ALU.add).then_inc(added, 1)
                dve.wait_ge(added, len(jobs))


def qk_projection(nc, name, XN, wT, bias_dram, parts_dram, regs=None, q_keep=None, early=None,
                  patches=False):
    lch = [(at, PH * W) for at in range(0, L, PH * W)] if patches else LCH
    wide = L + (NREG if regs is not None else 0)
    with Scope(nc, name) as s:
        w_sb = s.sb("w", [CP, CC, 2 * C])
        b_sb = s.sb("b", [CP, 2 * CC])
        r_sb = s.sb("r", [CP, CC, NREG])
        val = s.sb("val", [CP, 4, CH])
        hi = s.sb("hi", [CP, 2, LK], F16)
        lo = s.sb("lo", [CP, 2, LK], F16)
        acc = [s.ps(f"acc{i}", [CP, CH]) for i in range(4)]
        loaded, ready, valued, rounded, split = (
            s.sem(n) for n in ("loaded", "ready", "valued", "rounded", "split"))
        stored = [s.sem(f"stored{i}") for i in range(2)]
        n_loads = 32 + (16 if regs is not None else 0)
        rows = [(q, c, b) for q in range(2) for c in range(CC) for b in range(B)]
        jobs = []
        for slot, (q, c, b) in enumerate(rows):
            for at, w in lch:
                jobs.append((slot, q, c, b, at, w, False))
            if regs is not None:
                jobs.append((slot, q, c, b, L, NREG, True))
        per = len(jobs) // len(rows)
        with s.block() as block:
            @block.sync
            def _(sp):
                sp.dma_start(w_sb[:], wT.rearrange("(k p) n -> p k n", p=CP)[:, :, 0:2 * C]).then_inc(loaded, 16)
                with nc.allow_non_contiguous_dma(reason="a bias column"):
                    sp.dma_start(b_sb[:], bias_dram[0:2 * C].rearrange("(c p) -> p c", p=CP))\
                      .then_inc(loaded, 16)
                if regs is not None:
                    sp.dma_start(r_sb[:], regs.rearrange("(k p) n -> p k n", p=CP)).then_inc(loaded, 16)
                if early is not None:
                    early(sp)
                for slot, (q, c, b) in enumerate(rows):
                    sp.wait_ge(split, per * (slot + 1))
                    at = b * C + c * CP
                    for part, t in enumerate((hi, lo)):
                        sp.dma_start(parts_dram[q][part][at:at + CP, :], t[:, slot % 2, 0:wide])\
                          .then_inc(stored[slot % 2], 16)
                for x in stored:
                    sp.wait_ge(x, 16 * len(rows))

            @block.tensor
            def _(pe):
                pe.wait_ge(loaded, n_loads)
                for n, (slot, q, c, b, at, w, is_reg) in enumerate(jobs):
                    if n >= 4:
                        pe.wait_ge(valued, n - 3)
                    for k in range(CC):
                        rhs = r_sb[:, k, :] if is_reg else XN[:, k, b * L + at:b * L + at + w]
                        mm = pe.matmul(acc[n % 4][:, 0:w], w_sb[:, k, q * C + c * CP:q * C + (c + 1) * CP],
                                       rhs, start=k == 0, stop=k == CC - 1)
                    mm.then_inc(ready, 1)

            def value(n):
                slot, q, c, b, at, w, is_reg = jobs[n]
                if q_keep is not None and q == 0:
                    return q_keep[:, c, b * L + at:b * L + at + w]
                return val[:, n % 4, 0:w]

            def home(n, ap):
                if patches and jobs[n][1] == 0 and not jobs[n][6]:
                    return ap.rearrange("p (h x w) -> p x h w", x=NPW, w=PW)
                return ap

            def stored_order(n, ap):
                if patches and jobs[n][1] == 0 and not jobs[n][6]:
                    return ap.rearrange("p (x h w) -> p x h w", h=PH, w=PW)
                return ap

            @block.vector
            def _(dve):
                dve.wait_ge(loaded, n_loads)
                for n in range(len(jobs) + 1):
                    if n < len(jobs):
                        slot, q, c, b, at, w, _ = jobs[n]
                        dve.wait_ge(ready, n + 1)
                        if n >= 4:
                            dve.wait_ge(rounded, n - 3)
                        dve.tensor_scalar(value(n), acc[n % 4][:, 0:w], b_sb[:, q * CC + c:q * CC + c + 1],
                                          QUARTER if q else 1.0, ALU.add, ALU.mult).then_inc(valued, 1)
                    if n >= 1:
                        slot, q, c, b, at, w, _ = jobs[n - 1]
                        dve.wait_ge(rounded, n)
                        dve.wait_ge(valued, n)
                        if slot >= 2:
                            dve.wait_ge(stored[slot % 2], 32 * (slot // 2))
                        dve.tensor_tensor(stored_order(n - 1, lo[:, slot % 2, at:at + w]), home(n - 1, value(n - 1)),
                                          stored_order(n - 1, hi[:, slot % 2, at:at + w]), ALU.subtract)\
                           .then_inc(split, 1)

            @block.scalar
            def _(act):
                for n, (slot, q, c, b, at, w, _) in enumerate(jobs):
                    act.wait_ge(valued, n + 1)
                    if slot >= 2:
                        act.wait_ge(stored[slot % 2], 32 * (slot // 2))
                    act.activation(stored_order(n, hi[:, slot % 2, at:at + w]), home(n, value(n)), ACT.Copy)\
                       .then_inc(rounded, 1)


def v_projection(nc, name, XN, wT, bias_dram, V, regs=None):
    with Scope(nc, name) as s:
        w_sb = s.sb("w", [CP, CC, C])
        bias = s.sb("bias", [128, C])
        r_sb = s.sb("r", [CP, CC, NREG])
        acc = [s.ps(f"acc{i}", [128, CH]) for i in range(4)]
        loaded, ready, done = s.sem("loaded"), s.sem("ready"), s.sem("done")
        n_loads = 32 + (16 if regs is not None else 0)
        jobs = [(n, 128) for n in range(TOK // 128)] + ([(TOK // 128, NREG)] if regs is not None else [])
        with s.block() as block:
            @block.sync
            def _(sp):
                sp.dma_start(w_sb[:], wT.rearrange("(k p) n -> p k n", p=CP)[:, :, 2 * C:3 * C]).then_inc(loaded, 16)
                sp.dma_start(bias[:], bias_dram[2 * C:3 * C].rearrange("(a n) -> a n", a=1).to_broadcast([128, C]))\
                  .then_inc(loaded, 16)
                if regs is not None:
                    sp.dma_start(r_sb[:], regs.rearrange("(k p) n -> p k n", p=CP)).then_inc(loaded, 16)
                sp.wait_ge(loaded, n_loads)

            @block.tensor
            def _(pe):
                pe.wait_ge(loaded, n_loads)
                for n, (tile, rows) in enumerate(jobs):
                    if n >= 4:
                        pe.wait_ge(done, n - 3)
                    for k in range(CC):
                        src = XN[:, k, tile * 128:(tile + 1) * 128] if rows == 128 else r_sb[:, k, :]
                        mm = pe.matmul(acc[n % 4][0:rows, 0:C], src, w_sb[:, k, :], start=k == 0, stop=k == CC - 1)
                    mm.then_inc(ready, 1)

            @block.vector
            def _(dve):
                dve.wait_ge(loaded, n_loads)
                for n, (tile, rows) in enumerate(jobs):
                    dve.wait_ge(ready, n + 1)
                    dve.tensor_tensor(V[0:rows, tile, :, 0:HD], acc[n % 4][0:rows, 0:C].rearrange("p (h d) -> p h d", d=HD),
                                      bias[0:rows, :].rearrange("p (h d) -> p h d", d=HD), ALU.add)\
                       .then_inc(done, 1)
                dve.wait_ge(done, len(jobs))


def window_of(p):
    r, c = divmod(p, NPW)
    kr = min(max(r * PH - WIN // 2, 0), H - KH)
    kc = min(max(c * PW - WIN // 2, 0), W - KW)
    kind = 3 * (0 if r == 0 else 2 if r == NPH - 1 else 1) + (0 if c == 0 else 2 if c == NPW - 1 else 1)
    return (r * PH, c * PW), (kr, kc), kind


def image_of(ap, n=1):
    return ap.rearrange("p (h w) -> p h w", w=W)


def layer0_attention(nc, parts_dram, O, V, mask_d, eye_bf_d, eye):
    NU = NPT // 2
    HPB = 2
    U = NU * HPB
    WKR = WK + NREG
    PQ = PH * PW
    ROWS = [n * KW + (NREG if k == len(CUTS) - 1 else 0) for k, (_, n) in enumerate(CUTS)]
    LEAD = 16
    JB = NH // HPB
    with Scope(nc, "l0a") as s:
        Q = [s.sb(f"q{i}", [3 * HD, L], F16) for i in range(HPB)]
        K = [s.sb(f"k{i}", [3 * HD, LK], F16) for i in range(HPB)]
        mask = s.sb("mask", [PQ, 9, WKR], BF16)
        eye_b = s.sb("eye_b", [PQ, PQ], BF16)
        nmax = s.sb("nmax", [PQ, 2, 2])
        P = s.sb("p", [PQ, 2, 2, WKR])
        PT = s.sb("pt", [128, 2, 2, len(CUTS), PQ])
        rec = s.sb("rec", [PQ, 2, 2])
        s_ps = [s.ps(f"s{i}", [PQ, 2, CH]) for i in range(2)]
        t_ps = s.ps("t", [128, 2, 4, PQ])
        o_ps = [s.ps(f"o{i}", [PQ, CH]) for i in range(2)]
        consts = s.sem("consts")
        loaded = [s.sem(f"loaded{i}") for i in range(HPB)]
        scored, maxed, exped, turned, evac_dve, evac_act, summed, inverted, normed = (
            s.sem(n) for n in ("scored", "maxed", "exped", "turned", "evac_dve", "evac_act", "summed",
                               "inverted", "normed"))
        LOADS = 6 * 16

        def lead(eng, *sems):
            for x in sems:
                eng.sem_inc(x, LEAD)

        def unit(u):
            return u // NU, 2 * (u % NU)

        def evacuate(copy, u, x):
            copy(PT[0:ROWS[0], u % 2, x, 0:2, :], t_ps[0:ROWS[0], x, 0:2, :])
            return copy(PT[0:ROWS[2], u % 2, x, 2, :], t_ps[0:ROWS[2], x, 2, :])

        with s.block() as block:
            @block.sync
            def _(sp):
                sp.dma_start(mask[:], mask_d.rearrange("k q w -> q k w")).then_inc(consts, 16)
                sp.dma_start(eye_b[:], eye_bf_d[0:PQ, 0:PQ]).then_inc(consts, 16)
                with sp.Fori(0, B * JB) as i:
                    for e in range(HPB):
                        sp.wait_ge(scored, i * U + LEAD - (NU if e == 0 else 0))
                        row = i * (HPB * HD) + e * HD
                        for j, part in enumerate((0, 0, 1)):
                            sp.dma_start(Q[e][j * HD:(j + 1) * HD, :],
                                         parts_dram[0][part][bass.ds(row, HD), 0:L]).then_inc(loaded[e], 16)
                        for j, part in enumerate((0, 1, 0)):
                            sp.dma_start(K[e][j * HD:(j + 1) * HD, :],
                                         parts_dram[1][part][bass.ds(row, HD), 0:LK]).then_inc(loaded[e], 16)

            @block.tensor
            def _(pe):
                pe.wait_ge(consts, 32)
                lead(pe, scored, turned, summed)

                def scores(i, u):
                    e, p0 = unit(u)
                    if u % NU == 0:
                        pe.wait_ge(loaded[e], i * LOADS + LOADS)
                    pe.wait_ge(exped, i * U + u + LEAD - 1)
                    for x in range(2):
                        (qr, qc), (kr, kc), kind = window_of(p0 + x)
                        out = s_ps[u % 2]
                        q = Q[e][:, (p0 + x) * PQ:(p0 + x + 1) * PQ]
                        k = image_of(K[e][:, 0:L])[:, kr:kr + KH, kc:kc + KW]
                        pe.matmul(out[:, x, 0:WKR], eye_b[:], mask[:, kind, :], start=True, stop=False)
                        pe.matmul(out[:, x, 0:WK].rearrange("p (h w) -> p h w", w=KW), q, k, start=False, stop=False)
                        mm = pe.matmul(out[:, x, WK:WKR], q, K[e][:, L:LK], start=False, stop=True)
                    mm.then_inc(scored, 1)

                def turn(i, u):
                    pe.wait_ge(exped, i * U + u + 1 + LEAD)
                    pe.wait_ge(evac_dve, i * U + u + LEAD)
                    pe.wait_ge(evac_act, i * U + u + LEAD)
                    for x in range(2):
                        for c, (r0, _) in enumerate(CUTS):
                            mm = pe.transpose(t_ps[0:ROWS[c], x, c, :], P[:, u % 2, x, r0 * KW:r0 * KW + ROWS[c]],
                                              eye[0:PQ, 0:PQ])
                    mm.then_inc(turned, 1)

                def values(b, j, i, u):
                    e, p0 = unit(u)
                    pe.wait_ge(evac_dve, i * U + u + 1 + LEAD)
                    pe.wait_ge(evac_act, i * U + u + 1 + LEAD)
                    pe.wait_ge(normed, i * U + u + LEAD - 1)
                    for x in range(2):
                        out = o_ps[u % 2][:, x * VE:(x + 1) * VE]
                        for c in range(len(CUTS)):
                            mm = pe.matmul(out, PT[0:ROWS[c], u % 2, x, c, :],
                                           V[0:ROWS[c], bass.ds(b, 1), p0 + x, c, bass.ds(j * HPB + e, 1), :],
                                           start=c == 0, stop=c == len(CUTS) - 1)
                    mm.then_inc(summed, 1)

                with pe.Fori(0, B) as b:
                    with pe.Fori(0, JB) as j:
                        i = pe.snap(b * JB + j)
                        scores(i, 0)
                        for u in range(U):
                            if u + 1 < U:
                                scores(i, u + 1)
                            turn(i, u)
                            if u >= 1:
                                values(b, j, i, u - 1)
                        values(b, j, i, U - 1)

            @block.vector
            def _(dve):
                lead(dve, maxed, evac_dve, inverted, normed)

                def top(i, u):
                    dve.wait_ge(scored, i * U + u + 1 + LEAD)
                    dve.wait_ge(exped, i * U + u + LEAD - 1)
                    dve.tensor_reduce(nmax[:, u % 2, :], s_ps[u % 2][:, :, 0:WKR], AX_X, ALU.max,
                                      negate=True).then_inc(maxed, 1)

                def take(i, u):
                    dve.wait_ge(turned, i * U + u + 1 + LEAD)
                    dve.wait_ge(summed, i * U + u + LEAD - 1)
                    evacuate(dve.tensor_copy, u, 0).then_inc(evac_dve, 1)

                def norm(b, j, i, u):
                    e, p0 = unit(u)
                    o = o_ps[u % 2][:, 0:2 * VE].rearrange("p (x d) -> p x d", x=2)
                    dve.wait_ge(summed, i * U + u + 1 + LEAD)
                    dve.reciprocal(rec[:, u % 2, :], o[:, :, HD]).then_inc(inverted, 1)
                    dve.wait_ge(inverted, i * U + u + 1 + LEAD)
                    dve.tensor_tensor(O[:, bass.ds(b * NPT + p0, 2), bass.ds((j * HPB + e) * HD, HD)],
                                      o[:, :, 0:HD], rec[:, u % 2, :].unsqueeze(2).to_broadcast([PQ, 2, HD]),
                                      ALU.mult).then_inc(normed, 1)

                with dve.Fori(0, B) as b:
                    with dve.Fori(0, JB) as j:
                        i = dve.snap(b * JB + j)
                        for u in range(U + 2):
                            if u < U:
                                top(i, u)
                            if 1 <= u <= U:
                                take(i, u - 1)
                            if u >= 2:
                                norm(b, j, i, u - 2)
                dve.wait_ge(normed, B * JB * U + LEAD)

            @block.scalar
            def _(act):
                lead(act, exped, evac_act)

                def exps(i, u):
                    act.wait_ge(maxed, i * U + u + 1 + LEAD)
                    act.wait_ge(turned, i * U + u + LEAD - 1)
                    for x in range(2):
                        last = act.activation(P[:, u % 2, x, :], s_ps[u % 2][:, x, 0:WKR], ACT.Exp,
                                              bias=nmax[:, u % 2, x:x + 1])
                    last.then_inc(exped, 1)

                def take(i, u):
                    act.wait_ge(turned, i * U + u + 1 + LEAD)
                    act.wait_ge(summed, i * U + u + LEAD - 1)
                    evacuate(lambda o, p: act.activation(o, p, ACT.Copy), u, 1).then_inc(evac_act, 1)

                with act.Fori(0, B * JB) as i:
                    for u in range(U + 1):
                        if u < U:
                            exps(i, u)
                        if u >= 1:
                            take(i, u - 1)


def turn_output(nc, name, O, OT, eye):
    with Scope(nc, name) as s:
        ps = [s.ps(f"t{i}", [CP, NPW, PH, PW]) for i in range(4)]
        turned, moved = s.sem("turned"), s.sem("moved")
        jobs = [(c, g) for g in range(B * NPH) for c in range(CC)]
        with s.block() as block:
            @block.tensor
            def _(pe):
                for n, (c, g) in enumerate(jobs):
                    if n >= 4:
                        pe.wait_ge(moved, n - 3)
                    for x in range(NPW):
                        mm = pe.transpose(ps[n % 4][:, x, :, :], O[:, g * NPW + x, c * CP:(c + 1) * CP], eye[:, :])
                    mm.then_inc(turned, 1)

            @block.scalar
            def _(act):
                for n, (c, g) in enumerate(jobs):
                    act.wait_ge(turned, n + 1)
                    strip = OT[:, c, g * PH * W:(g + 1) * PH * W].rearrange("p (h x w) -> p x h w", x=NPW, w=PW)
                    act.activation(strip, ps[n % 4][:], ACT.Copy).then_inc(moved, 1)
                act.wait_ge(moved, len(jobs))


def ssm_conv(nc, name, XN, t, pre, U, UT, z_dram):
    PADW = W + 2
    STRIP = PH * W
    with Scope(nc, name) as s:
        w_sb = s.sb("w", [CP, CC, 2 * DI])
        cw = s.sb("cw", [DI, 9])
        cb = s.sb("cb", [DI, 1])
        pad = s.sb("pad", [DI, B, H + 2, PADW])
        z = s.sb("z", [DI, 2, STRIP])
        conv = s.sb("conv", [DI, B, L])
        e = s.sb("e", [DI, B, L])
        acc = [s.ps(f"acc{i}", [DI, CH]) for i in range(4)]
        loaded, padded, ready, placed, z_moved, z_stored0, z_stored1 = (
            s.sem(n) for n in ("loaded", "padded", "ready", "placed", "z_moved", "z_stored0", "z_stored1"))
        z_stored = (z_stored0, z_stored1)
        convolved, own, exped, gated, turned = (s.sem(n) for n in ("convolved", "own", "exped", "gated", "turned"))
        strips = [(b, r) for b in range(B) for r in range(0, H, PH)]
        n_s = len(strips)
        with s.block() as block:
            @block.sync
            def _(sp):
                sp.dma_start(w_sb[:], t[pre + "in_wT"].rearrange("(k p) n -> p k n", p=CP)).then_inc(loaded, 16)
                sp.dma_start(cw[:], t[pre + "conv_w"]).then_inc(loaded, 16)
                sp.dma_start(cb[:], t[pre + "conv_b"]).then_inc(loaded, 16)
                for n, (b, r) in enumerate(strips):
                    sp.wait_ge(z_moved, n + 1)
                    at = b * L + r * W
                    sp.dma_start(z_dram[:, at:at + STRIP], z[:, n % 2, :]).then_inc(z_stored[n % 2], 16)
                for x in z_stored:
                    sp.wait_ge(x, 16 * n_s // 2)

            @block.tensor
            def _(pe):
                pe.wait_ge(loaded, 48)
                for n, (b, r) in enumerate(strips):
                    if n >= 2:
                        pe.wait_ge(placed, n - 1)
                        pe.wait_ge(z_moved, n - 1)
                    at = b * L + r * W
                    for half in range(2):
                        for k in range(CC):
                            mm = pe.matmul(acc[2 * (n % 2) + half][:, 0:STRIP], w_sb[:, k, half * DI:(half + 1) * DI],
                                           XN[:, k, at:at + STRIP], start=k == 0, stop=k == CC - 1)
                        mm.then_inc(ready, 1)

            @block.gpsimd
            def _(pool):
                pool.memset(pad[:], 0.0).then_inc(padded, 1)

            @block.scalar
            def _(act):
                act.wait_ge(padded, 1)
                for n, (b, r) in enumerate(strips):
                    act.wait_ge(ready, 2 * n + 1)
                    act.activation(pad[:, b, 1 + r:1 + r + PH, 1:1 + W],
                                   acc[2 * (n % 2)][:, 0:STRIP].rearrange("p (h w) -> p h w", w=W), ACT.Copy)\
                       .then_inc(placed, 1)
                    act.wait_ge(ready, 2 * n + 2)
                    if n >= 2:
                        act.wait_ge(z_stored[n % 2], 16 * (n // 2))
                    act.activation(z[:, n % 2, :], acc[2 * (n % 2) + 1][:, 0:STRIP], ACT.Copy).then_inc(z_moved, 1)
                for b in range(B):
                    act.wait_ge(convolved, b + 1)
                    act.activation(e[:, b, :], conv[:, b, :], ACT.Exp, scale=-1.0).then_inc(exped, 1)
                for b in range(B):
                    act.wait_ge(gated, b + 1)
                    act.activation(image_of(UT[:, b, :]), U[:, b, :].rearrange("p (h w) -> p w h", w=W), ACT.Copy)\
                       .then_inc(turned, 1)
                act.wait_ge(turned, B)

            @block.vector
            def _(dve):
                link = Chain(dve, own)
                dve.wait_ge(loaded, 48)
                for b in range(B):
                    dve.wait_ge(placed, n_s // B * (b + 1))
                    c = image_of(conv[:, b, :])
                    for k in range(9):
                        src = pad[:, b, k // 3:k // 3 + H, k % 3:k % 3 + W]
                        if k == 0:
                            link(dve.tensor_scalar(c, src, cw[:, 0:1], cb[:, 0:1], ALU.mult, ALU.add))
                        else:
                            link(dve.scalar_tensor_tensor(c, src, cw[:, k:k + 1], c, ALU.mult, ALU.add))
                    dve.sem_inc(convolved, 1)
                for b in range(B):
                    dve.wait_ge(exped, b + 1)
                    link(dve.tensor_scalar(e[:, b, :], e[:, b, :], 1.0, None, ALU.add))
                    link(dve.reciprocal(e[:, b, :], e[:, b, :]))
                    dve.tensor_tensor(U[:, b, :], conv[:, b, :], e[:, b, :], ALU.mult).then_inc(gated, 1)
                dve.wait_ge(gated, B)


def ssm_prepare(nc, name, t, pre, U, UT, dt_dram, du_dram, bc_dram, skip_dram):
    LEAD = 4
    XR = 80
    SR = XR
    with Scope(nc, name) as s:
        wx = s.sb("wx", [DI, ND, CP])
        wdt = s.sb("wdt", [DT_R, ND, DI])
        bdt = s.sb("bdt", [DI, ND])
        Dk = s.sb("dk", [DI, ND])
        dsum = s.sb("dsum", [DI, 1])
        skip = s.sb("skip", [DI, L])
        XD = s.sb("xd", [CP, 2, L])
        T = s.sb("t", [DI, 2, L])
        E = s.sb("e", [DI, 2, L])
        Wb = s.sb("wb", [DI, 2, L])
        parts = {k: s.sb(f"parts_{k}", [CP, 3, L], BF16) for k in ("x", "t", "u")}
        xd_ps = [s.ps(f"xd{i}", [CP, CH]) for i in range(2)]
        dt_ps = [s.ps(f"dt{i}", [DI, CH]) for i in range(2)]
        loaded = s.sem("loaded")
        xd_made, xd_taken, dt_made, dt_taken = (s.sem(n) for n in ("xd_made", "xd_taken", "dt_made", "dt_taken"))
        absed, exped, plus1, delta, logged, softed, dt_done, du_done, dt_held = (
            s.sem(n) for n in ("absed", "exped", "plus1", "delta", "logged", "softed", "dt_done", "du_done",
                               "dt_held"))
        hi = {k: s.sem(f"hi_{k}") for k in parts}
        rest = {k: s.sem(f"rest_{k}") for k in parts}
        mid = {k: s.sem(f"mid_{k}") for k in parts}
        low = {k: s.sem(f"low_{k}") for k in parts}
        stored = {k: s.sem(f"stored_{k}") for k in parts}
        skipped, skip_stored, skip_own = s.sem("skipped"), s.sem("skip_stored"), s.sem("skip_own")
        own_rows = {"x": XR, "t": DI, "u": DI}
        STORES = {"x": 2 * 16, "t": 9 * 16, "u": 9 * 16}

        def lead(eng, *sems):
            for x in sems:
                eng.sem_inc(x, LEAD)

        def whole(k, n):
            return {"x": XD, "t": T, "u": E}[k][0:own_rows[k], n % 2, :]

        def order(k):
            return [("make", 0)] + [x for n in range(1, ND) for x in (("make", n), ("split", n - 1))] + [("split", ND - 1)]

        def source(k, b):
            return (UT if k % 2 else U)[:, bass.ds(b, 1), :]

        with s.block() as block:
            @block.sync
            def _(sp):
                sp.dma_start(wx[:], t[pre + "xwT"].rearrange("k p n -> p k n")).then_inc(loaded, 16)
                sp.dma_start(wdt[:], t[pre + "dtwT"].rearrange("k p n -> p k n")).then_inc(loaded, 16)
                sp.dma_start(bdt[:], t[pre + "dtb"]).then_inc(loaded, 16)
                sp.dma_start(Dk[:], t[pre + "D"]).then_inc(loaded, 16)
                with sp.Fori(0, B) as b:
                    sp.wait_ge(skipped, b + 1 + LEAD)
                    sp.dma_start(skip_dram[bass.ds(b, 1), :, :].rearrange("a p l -> (a p) l"), skip[:])\
                      .then_inc(skip_stored, 16)
                    for k in range(ND):
                        n = b * ND + k
                        at = b * ND + (k % 2) * 2 + k // 2
                        sp.wait_ge(low["x"], n + 1 + LEAD)
                        for j, row in enumerate((32, 64)):
                            sp.dma_start(bc_dram[bass.ds(at * 2 + j, 1), :, :, :].rearrange("a c n l -> (a n) c l"),
                                         parts["x"][row:row + NS, :, :]).then_inc(stored["x"], 16)
                        for w, d in (("t", dt_dram), ("u", du_dram)):
                            sp.wait_ge(low[w], n + 1 + LEAD)
                            for c in range(3):
                                for tl in range(3):
                                    dst = d[bass.ds(at, 1), :, c, :, tl, :].rearrange("a g c l -> (a g) c l")
                                    sp.dma_start(dst, parts[w][tl * 32:(tl + 1) * 32, c, :]).then_inc(stored[w], 16)
                for w in parts:
                    sp.wait_ge(stored[w], STORES[w] * B * ND)
                sp.wait_ge(skip_stored, 16 * B)

            @block.tensor
            def _(pe):
                pe.wait_ge(loaded, 64)
                lead(pe, xd_made, dt_made)
                with pe.Fori(0, B) as b:
                    for k in range(ND):
                        n = b * ND + k
                        for c in range(len(LCH) + 1):
                            m = n * len(LCH) + c
                            if c < len(LCH):
                                at, w = LCH[c]
                                pe.wait_ge(xd_taken, m + LEAD - 1)
                                pe.matmul(xd_ps[c % 2][:, 0:w], wx[:, k, :], source(k, b)[:, :, at:at + w],
                                          start=True, stop=True).then_inc(xd_made, 1)
                            if c >= 1:
                                at, w = LCH[c - 1]
                                pe.wait_ge(xd_taken, m + LEAD)
                                pe.wait_ge(dt_taken, m - 1 + LEAD - 1)
                                pe.matmul(dt_ps[(c - 1) % 2][:, 0:w], wdt[:, k, :], XD[0:DT_R, k % 2, at:at + w],
                                          start=True, stop=True).then_inc(dt_made, 1)

            @block.scalar
            def _(act):
                act.wait_ge(loaded, 64)
                lead(act, xd_taken, dt_taken, absed, exped, logged, *hi.values(), *mid.values())

                def make(b, k):
                    n = b * ND + k
                    for w in ("x", "t"):
                        act.wait_ge(low[w], n + LEAD - 1)
                    act.wait_ge(low["u"], n + LEAD - 1)
                    for c in range(len(LCH) + 1):
                        m = n * len(LCH) + c
                        if c < len(LCH):
                            at, w = LCH[c]
                            act.wait_ge(xd_made, m + 1 + LEAD)
                            act.activation(XD[:, k % 2, at:at + w], xd_ps[c % 2][:, 0:w], ACT.Copy)\
                               .then_inc(xd_taken, 1)
                        if c >= 1:
                            at, w = LCH[c - 1]
                            act.wait_ge(dt_made, m + LEAD)
                            act.activation(T[:, k % 2, at:at + w], dt_ps[(c - 1) % 2][:, 0:w], ACT.Identity,
                                           bias=bdt[:, k:k + 1]).then_inc(dt_taken, 1)
                    act.wait_ge(dt_taken, (n + 1) * len(LCH) + LEAD)
                    act.activation(E[:, k % 2, :], T[:, k % 2, :], ACT.Abs).then_inc(absed, 1)
                    act.wait_ge(absed, n + 1 + LEAD)
                    act.activation(E[:, k % 2, :], E[:, k % 2, :], ACT.Exp, scale=-1.0).then_inc(exped, 1)
                    act.wait_ge(delta, n + 1 + LEAD)
                    act.activation(Wb[:, k % 2, :], Wb[:, k % 2, :], ACT.Ln).then_inc(logged, 1)

                def split(b, k):
                    n = b * ND + k
                    for w, done in (("x", None), ("t", dt_held), ("u", du_done)):
                        if done is not None:
                            act.wait_ge(done, n + 1 + LEAD)
                        act.wait_ge(stored[w], n * STORES[w])
                        r = own_rows[w]
                        act.activation(parts[w][0:r, 0, :], whole(w, k), ACT.Copy).then_inc(hi[w], 1)
                    for w in parts:
                        act.wait_ge(rest[w], n + 1 + LEAD)
                        r = own_rows[w]
                        act.activation(parts[w][0:r, 1, :], whole(w, k), ACT.Copy).then_inc(mid[w], 1)

                with act.Fori(0, B) as b:
                    for stage, k in order(0):
                        (make if stage == "make" else split)(b, k)

            @block.vector
            def _(dve):
                dve.wait_ge(loaded, 64)
                lead(dve, plus1, delta, dt_done, skipped, du_done, dt_held, *low.values())
                skip_link = Chain(dve, skip_own)
                skip_link(dve.tensor_reduce(dsum[:], Dk[:], AX_X, ALU.add))

                def make(b, k):
                    n = b * ND + k
                    if k == 0:
                        dve.wait_ge(skip_stored, b * 16)
                        dve.tensor_scalar(skip[:], U[:, bass.ds(b, 1), :], dsum[:, 0:1], None, ALU.mult)\
                           .then_inc(skipped, 1)
                    dve.wait_ge(exped, n + 1 + LEAD)
                    dve.tensor_scalar(Wb[:, k % 2, :], E[:, k % 2, :], 1.0, None, ALU.add).then_inc(plus1, 1)
                    dve.wait_ge(plus1, n + 1 + LEAD)
                    dve.scalar_tensor_tensor(E[:, k % 2, :], Wb[:, k % 2, :], 1.0, E[:, k % 2, :],
                                             ALU.subtract, ALU.subtract).then_inc(delta, 1)
                    dve.wait_ge(softed, n + 1 + LEAD)
                    dve.scalar_tensor_tensor(T[:, k % 2, :], T[:, k % 2, :], 0.0, Wb[:, k % 2, :],
                                             ALU.max, ALU.add).then_inc(dt_done, 1)
                    dve.wait_ge(dt_done, n + 1 + LEAD)
                    dve.tensor_tensor(E[:, k % 2, :], T[:, k % 2, :],
                                      source(k, b).rearrange("p a l -> p (a l)"), ALU.mult)\
                       .then_inc(du_done, 1)
                    dve.wait_ge(du_done, n + 1 + LEAD)
                    dve.tensor_scalar(T[:, k % 2, :], T[:, k % 2, :], DT_LEAST, None, ALU.max)\
                       .then_inc(dt_held, 1)

                def split(b, k):
                    n = b * ND + k
                    for w in parts:
                        r = own_rows[w]
                        dve.wait_ge(mid[w], n + 1 + LEAD)
                        dve.tensor_tensor(parts[w][0:r, 2, :], whole(w, k), parts[w][0:r, 1, :], ALU.subtract)\
                           .then_inc(low[w], 1)

                with dve.Fori(0, B) as b:
                    for stage, k in order(0):
                        (make if stage == "make" else split)(b, k)

            @block.gpsimd
            def _(pool):
                lead(pool, softed, *rest.values())

                def make(b, k):
                    n = b * ND + k
                    pool.wait_ge(logged, n + 1 + LEAD)
                    pool.tensor_tensor(Wb[:, k % 2, :], Wb[:, k % 2, :], E[:, k % 2, :], ALU.subtract)\
                        .then_inc(softed, 1)

                def split(b, k):
                    n = b * ND + k
                    for w in ("x", "t", "u"):
                        r = own_rows[w]
                        pool.wait_ge(hi[w], n + 1 + LEAD)
                        pool.tensor_tensor(whole(w, k), whole(w, k), parts[w][0:r, 0, :], ALU.subtract)\
                            .then_inc(rest[w], 1)

                with pool.Fori(0, B) as b:
                    for stage, k in order(0):
                        (make if stage == "make" else split)(b, k)


def ssm_scan(nc, name, t, pre, dt_dram, du_dram, bc_dram, y_dram):
    LEAD = 16
    NG, NT = 4, 3
    UN = 2 * NG * NT
    CW = 10 * W
    CHK = [(at, min(CW, L - at)) for at in range(0, L, CW)]
    NK = len(CHK)
    NB = 6
    with Scope(nc, name) as s:
        E4 = s.sb("e4", [128, 128], BF16)
        EN = s.sb("en", [3 * NS, 128], BF16)
        SUM = s.sb("sum", [128, NG, 32])
        A = s.sb("a", [128, ND * NG * NT])
        AO = s.sb("ao", [128, 2 * NG * NT])
        DT = s.sb("dt", [128, NT, L], BF16)
        DU = s.sb("du", [128, NT, L], BF16)
        BC = s.sb("bc", [3 * NS, 2, L], BF16)
        REP = [[s.sb(f"rep{d}{j}", [128, L]) for j in range(2)] for d in range(2)]
        dA = s.sb("da", [128, 2, L])
        S = s.sb("s", [128, NB, L])
        ystage = s.sb("ystage", [DI, L])
        ring = [s.ps(f"ring{i}", [128, CH]) for i in range(3)]
        y_ps = s.ps("y", [DI, NK, CH])
        consts = s.sem("consts")
        loaded = [s.sem(f"loaded{g}") for g in range(NG)]
        bc_loaded = s.sem("bc_loaded")
        a_capped, a_exped, a_turned = s.sem("a_capped"), s.sem("a_exped"), s.sem("a_turned")
        restored, act_took, dve_took = (s.sem(n) for n in ("restored", "act_took", "dve_took"))
        scanned, weighted, summed, y_taken, y_stored = (
            s.sem(n) for n in ("scanned", "weighted", "summed", "y_taken", "y_stored"))

        uses = []
        for d in range(2):
            for j in range(2):
                uses += [("bc", d, j, c) for c in range(NK)]
            for x in range(NG * NT):
                n = d * NG * NT + x
                uses += [("dt", d, n, c) for c in range(NK)] + [("du", d, n, c) for c in range(NK)]
        index = {u: r for r, u in enumerate(uses)}
        of_act = [u[0] != "du" for u in uses]
        PER_A, PER_V, R = sum(of_act), len(uses) - sum(of_act), len(uses)
        START = {restored: R, weighted: UN}

        def taken_by(r):
            a = sum(of_act[:r + 1])
            return a, r + 1 - a

        def place(n):
            d, x = divmod(n, NG * NT)
            return d, x // NT, x % NT

        def lead(eng, *sems):
            for x in sems:
                eng.sem_inc(x, START.get(x, LEAD))

        def way(ap, d):
            return ap[:, ::-1] if d else ap

        with s.block() as block:
            @block.sync
            def _(sp):
                sp.dma_start(E4[:], t["e4"]).then_inc(consts, 16)
                sp.dma_start(EN[:], t["en"]).then_inc(consts, 16)
                sp.dma_start(SUM[:], t["state_sum"]).then_inc(consts, 16)
                sp.dma_start(A[:], t[pre + "A"]).then_inc(consts, 16)
                with sp.Fori(0, B * 2) as i:
                    for d in range(2):
                        at = i * 2 + d
                        before = index["bc", 1 - d, 1, NK - 1] + 1 + (R if d else 0)
                        sp.wait_ge(restored, i * R + before)
                        for j in range(2):
                            sp.dma_start(BC[:, j, :], bc_dram[bass.ds(at * 2 + j, 1), :, :, :]
                                         .rearrange("a c n l -> (a c n) l")).then_inc(bc_loaded, 16)
                        for g in range(NG):
                            n = ((1 - d) * NG + g + 1) * NT - 1
                            before = index["du", 1 - d, n, NK - 1] + 1 + (R if d else 0)
                            sp.wait_ge(restored, i * R + before)
                            for dst, src in ((DT, dt_dram), (DU, du_dram)):
                                sp.dma_start(dst[32 * g:32 * g + 24, :, :].rearrange("p t l -> p (t l)"),
                                             src[bass.ds(at, 1), g, :, :, :, :].rearrange("a c e t l -> (a c e) (t l)"))\
                                  .then_inc(loaded[g], 16)
                    sp.wait_ge(y_taken, i * NK + NK + LEAD)
                    sp.dma_start(y_dram[bass.ds(i, 1), :, :].rearrange("a p l -> (a p) l"), ystage[:])\
                      .then_inc(y_stored, 16)
                sp.wait_ge(y_stored, 16 * B * 2)

            @block.tensor
            def _(pe):
                pe.wait_ge(consts, 64)
                lead(pe, restored, summed)

                def restore(i, use):
                    r = index[use]
                    kind, d, n, c = use
                    at, w = CHK[c]
                    back = r - 3
                    if back >= 0:
                        a, v = taken_by(back)
                        if of_act[back]:
                            pe.wait_ge(act_took, i * PER_A + a + LEAD)
                        else:
                            pe.wait_ge(dve_took, i * PER_V + v + LEAD)
                    elif r == 0:
                        pe.wait_ge(act_took, i * PER_A + LEAD)
                        pe.wait_ge(dve_took, i * PER_V + LEAD)
                    out = ring[r % 3][:, 0:w]
                    if kind == "bc":
                        mm = pe.matmul(out, EN[:], BC[:, n, at:at + w], start=True, stop=True)
                    else:
                        _, g, tl = place(n)
                        src = DT if kind == "dt" else DU
                        mm = pe.matmul(out, E4[32 * g:32 * g + 24, :], src[32 * g:32 * g + 24, tl, at:at + w],
                                       start=True, stop=True)
                    mm.then_inc(restored, 1)

                def sum_states(i, q):
                    d, g = divmod(q, NG)
                    pe.wait_ge(weighted, i * UN + (q + 1) * NT + UN)
                    if q == 0:
                        pe.wait_ge(y_taken, i * NK + LEAD)
                    for c, (at, w) in enumerate(CHK):
                        for tl in range(NT):
                            n = q * NT + tl
                            mm = pe.matmul(y_ps[32 * tl:32 * tl + 32, c, 0:w], SUM[:, g, :], S[:, n % NB, at:at + w],
                                           start=q == 0, stop=q == 2 * NG - 1)
                    mm.then_inc(summed, 1)

                with pe.Fori(0, B * 2) as i:
                    for n in range(UN):
                        d, g, tl = place(n)
                        if n % (NG * NT) == 0:
                            pe.wait_ge(bc_loaded, (i * 2 + d + 1) * 32)
                            for j in range(2):
                                for c in range(NK):
                                    restore(i, ("bc", d, j, c))
                        if tl == 0:
                            pe.wait_ge(loaded[g], (i * 2 + d + 1) * 32)
                        for c in range(NK):
                            restore(i, ("dt", d, n, c))
                        for c in range(NK):
                            restore(i, ("du", d, n, c))
                        if tl == NT - 1 and n >= 2 * NT - 1:
                            sum_states(i, n // NT - 1)
                    sum_states(i, 2 * NG - 1)

            @block.scalar
            def _(act):
                act.wait_ge(a_capped, 1)
                lead(act, act_took, y_taken)
                act.activation(A[:], A[:], ACT.Exp).then_inc(a_exped, 1)
                with act.Fori(0, B) as b:
                    with act.Fori(0, 2) as o:
                        i = act.snap(b * 2 + o)
                        act.wait_ge(act_took, i * PER_A + LEAD)
                        act.wait_ge(a_turned, 1)
                        act.activation(AO[:], A[:, bass.ds(o * UN, UN)], ACT.Copy).then_inc(a_exped, 1)
                        act.wait_ge(a_exped, i + 2)
                        for r, (kind, d, n, c) in enumerate(uses):
                            if kind == "du":
                                continue
                            at, w = CHK[c]
                            src = ring[r % 3][:, 0:w]
                            act.wait_ge(restored, i * R + r + 1 + R)
                            if kind == "bc":
                                if n == 0 and c == 0:
                                    act.wait_ge(weighted, i * UN + (d + 1) * NG * NT)
                                act.activation(REP[d][n][:, at:at + w], src, ACT.Copy).then_inc(act_took, 1)
                            else:
                                if c == 0:
                                    act.wait_ge(scanned, i * UN + n - 1 + LEAD)
                                act.activation(dA[:, n % 2, at:at + w], src, ACT.Exp, scale=AO[:, n:n + 1])\
                                   .then_inc(act_took, 1)
                        act.wait_ge(summed, i * 2 * NG + 2 * NG + LEAD)
                        act.wait_ge(y_stored, i * 16)
                        for c, (at, w) in enumerate(CHK):
                            act.activation(ystage[:, at:at + w], y_ps[:, c, 0:w], ACT.Copy).then_inc(y_taken, 1)

            @block.vector
            def _(dve):
                lead(dve, dve_took, scanned)
                dve.wait_ge(consts, 64)
                dve.tensor_scalar(A[:], A[:], 88.0, None, ALU.min).then_inc(a_capped, 1)
                dve.wait_ge(a_exped, 1)
                dve.tensor_scalar(A[:], A[:], A_MOST, -1.0, ALU.min, ALU.mult).then_inc(a_turned, 1)
                with dve.Fori(0, B * 2) as i:
                    for n in range(UN):
                        d, g, tl = place(n)
                        if n % (NG * NT) == 0:
                            a, _ = taken_by(index["bc", d, 1, NK - 1])
                            dve.wait_ge(act_took, i * PER_A + a + LEAD)
                        dve.wait_ge(summed, i * 2 * NG + n // NT - 1 + LEAD)
                        for c, (at, w) in enumerate(CHK):
                            r = index["du", d, n, c]
                            dve.wait_ge(restored, i * R + r + 1 + R)
                            dve.tensor_tensor(S[:, n % NB, at:at + w], ring[r % 3][:, 0:w],
                                              REP[d][0][:, at:at + w], ALU.mult).then_inc(dve_took, 1)
                        a, v = taken_by(index["du", d, n, NK - 1])
                        dve.wait_ge(act_took, i * PER_A + a + LEAD)
                        dve.wait_ge(dve_took, i * PER_V + v + LEAD)
                        dve.tensor_tensor_scan(way(S[:, n % NB, :], d), way(dA[:, n % 2, :], d),
                                               way(S[:, n % NB, :], d), 0.0, ALU.mult, ALU.add)\
                           .then_inc(scanned, 1)

            @block.gpsimd
            def _(pool):
                lead(pool, weighted)
                with pool.Fori(0, B * 2) as i:
                    for n in range(UN):
                        d, _, _ = place(n)
                        pool.wait_ge(scanned, i * UN + n + 1 + LEAD)
                        pool.tensor_tensor(S[:, n % NB, :], S[:, n % NB, :], REP[d][1][:], ALU.mult)\
                            .then_inc(weighted, 1)


def ssm_gate(nc, name, t, pre, ones_mean, y_dram, skip_dram, z_dram, YG):
    with Scope(nc, name) as s:
        y = s.sb("y", [DI, B, L])
        yt = s.sb("yt", [DI, B, L])
        sk = s.sb("sk", [DI, B, L])
        z = s.sb("z", [DI, B, L])
        g = s.sb("g", [DI, 1])
        bb = s.sb("b", [DI, 1])
        acc = [s.ps(f"acc{i}", [DI, CH]) for i in range(4)]
        var_ps = [s.ps(f"var{i}", [DI, CH]) for i in range(4)]
        loaded = [s.sem(f"loaded{b}") for b in range(B)]
        consts, zlink = s.sem("consts"), s.sem("zlink")
        joined, meaned, centred, squared, varied, eps_added, rooted, normed, scaled, zexp, zgate, done, own = (
            s.sem(n) for n in ("joined", "meaned", "centred", "squared", "varied", "eps_added", "rooted",
                               "normed", "scaled", "zexp", "zgate", "done", "own"))
        jobs = [(b, at, w) for b in range(B) for at, w in LCH]
        NJ = len(LCH)
        with s.block() as block:
            @block.sync
            def _(sp):
                for b in range(B):
                    for dst, src in ((y, y_dram[2 * b]), (yt, y_dram[2 * b + 1]), (sk, skip_dram[b]),
                                     (z, z_dram[:, b * L:(b + 1) * L])):
                        sp.dma_start(dst[:, b, :], src).then_inc(loaded[b], 16)
                sp.dma_start(g[:], t[pre + "norm_g"]).then_inc(consts, 16)
                sp.dma_start(bb[:], t[pre + "norm_b"]).then_inc(consts, 16)

            @block.gpsimd
            def _(pool):
                for b in range(B):
                    pool.wait_ge(loaded[b], 64)
                    pool.tensor_tensor(y[:, b, :], y[:, b, :], sk[:, b, :], ALU.add).then_inc(own, 1)
                for b in range(B):
                    pool.wait_ge(zexp, b + 1)
                    pool.wait_ge(scaled, NJ * (b + 1))
                    pool.wait_ge(zgate, b + 1)
                    pool.tensor_tensor(YG[:, 0, b * L:(b + 1) * L], yt[:, b, :], z[:, b, :], ALU.mult).then_inc(done, 1)
                pool.wait_ge(done, B)

            @block.tensor
            def _(pe):
                for n, (b, at, w) in enumerate(jobs):
                    pe.wait_ge(joined, b + 1)
                    if n >= 4:
                        pe.wait_ge(centred, n - 3)
                    pe.matmul(acc[n % 4][:, 0:w], ones_mean[:], y[:, b, at:at + w], start=True, stop=True)\
                      .then_inc(meaned, 1)
                for n, (b, at, w) in enumerate(jobs):
                    pe.wait_ge(squared, n + 1)
                    if n >= 4:
                        pe.wait_ge(eps_added, n - 3)
                    pe.matmul(var_ps[n % 4][:, 0:w], ones_mean[:], yt[:, b, at:at + w], start=True, stop=True)\
                      .then_inc(varied, 1)

            @block.scalar
            def _(act):
                act.wait_ge(consts, 32)
                for b in range(B):
                    act.wait_ge(loaded[b], 64)
                    act.wait_ge(own, b + 1)
                    act.activation(sk[:, b, :], z[:, b, :], ACT.Exp, scale=-1.0).then_inc(zexp, 1)
                for n, (b, at, w) in enumerate(jobs):
                    act.wait_ge(centred, n + 1)
                    act.activation(yt[:, b, at:at + w], y[:, b, at:at + w], ACT.Square).then_inc(squared, 1)
                for n, (b, at, w) in enumerate(jobs):
                    act.wait_ge(eps_added, n + 1)
                    act.activation(yt[:, b, at:at + w], yt[:, b, at:at + w], ACT.Ln).then_inc(rooted, 1)
                    act.wait_ge(rooted, 2 * n + 1)
                    act.activation(yt[:, b, at:at + w], yt[:, b, at:at + w], ACT.Exp, scale=-0.5).then_inc(rooted, 1)
                for n, (b, at, w) in enumerate(jobs):
                    act.wait_ge(normed, n + 1)
                    act.activation(yt[:, b, at:at + w], y[:, b, at:at + w], ACT.Identity, scale=g[:, 0:1],
                                   bias=bb[:, 0:1]).then_inc(scaled, 1)

            @block.vector
            def _(dve):
                for b in range(B):
                    dve.wait_ge(own, b + 1)
                    dve.tensor_tensor(image_of(y[:, b, :]), image_of(y[:, b, :]),
                                      yt[:, b, :].rearrange("p (w h) -> p h w", h=H), ALU.add).then_inc(joined, 1)
                for n, (b, at, w) in enumerate(jobs):
                    dve.wait_ge(meaned, n + 1)
                    dve.tensor_tensor(y[:, b, at:at + w], y[:, b, at:at + w], acc[n % 4][:, 0:w], ALU.subtract)\
                       .then_inc(centred, 1)
                for b in range(B):
                    dve.wait_ge(zexp, b + 1)
                    link = Chain(dve, zlink, 2 * b)
                    link(dve.tensor_scalar(sk[:, b, :], sk[:, b, :], 1.0, None, ALU.add))
                    link(dve.reciprocal(sk[:, b, :], sk[:, b, :]))
                    dve.tensor_tensor(z[:, b, :], z[:, b, :], sk[:, b, :], ALU.mult).then_inc(zgate, 1)
                for n, (b, at, w) in enumerate(jobs):
                    dve.wait_ge(varied, n + 1)
                    dve.tensor_scalar(yt[:, b, at:at + w], var_ps[n % 4][:, 0:w], 1e-5, None, ALU.add)\
                       .then_inc(eps_added, 1)
                for n, (b, at, w) in enumerate(jobs):
                    dve.wait_ge(rooted, 2 * n + 2)
                    dve.tensor_tensor(y[:, b, at:at + w], y[:, b, at:at + w], yt[:, b, at:at + w], ALU.mult)\
                       .then_inc(normed, 1)


def rel_terms(nc, name, QF, t, rel_dram):
    RG = 8
    LEAD = 16
    with Scope(nc, name) as s:
        table = s.sb("table", [CP, 2, HPC // 2, 2 * H - 1, 2])
        hi = s.sb("hi", [CP, 2, L], F16)
        lo = s.sb("lo", [CP, 2, L], F16)
        acc = [s.ps(f"acc{i}", [CP, CH]) for i in range(4)]
        loaded, ready, rounded, split = (s.sem(n) for n in ("loaded", "ready", "rounded", "split"))
        stored = [s.sem(f"stored{i}") for i in range(2)]
        rows = [(kind, c, p) for kind in range(2) for c in range(CC) for p in range(HPC // 2)]
        NR = len(rows)
        NGR = H // RG
        jobs = [(r, g) for r in range(NR) for g in range(NGR)]
        J = len(jobs)

        def lead(eng, *sems):
            for x in sems:
                eng.sem_inc(x, LEAD)

        def banked(n):
            return acc[n % 4][:, 0:RG * H].rearrange("p (a b) -> p a b", b=H)

        def home(n, buf):
            r, g = jobs[n]
            im = image_of(buf[:, r % 2, :])
            if rows[r][0] == 0:
                return im[:, g * RG:(g + 1) * RG, :]
            return im[:, :, g * RG:(g + 1) * RG].rearrange("p h w -> p w h")

        with s.block() as block:
            @block.sync
            def _(sp):
                sp.dma_start(table[:], t["l3_rel"]).then_inc(loaded, 16)
                with sp.Fori(0, B) as b:
                    for r, (kind, c, p) in enumerate(rows):
                        sp.wait_ge(split, b * J + (r + 1) * NGR + LEAD)
                        head = b * NH + c * HPC + 2 * p
                        for part, buf in enumerate((hi, lo)):
                            sp.dma_start(rel_dram[kind][part][bass.ds(head, 2), :, :].rearrange("e k l -> k e l"),
                                         buf[:, r % 2, :]).then_inc(stored[r % 2], 16)
                for x in stored:
                    sp.wait_ge(x, 16 * NR * B)

            @block.tensor
            def _(pe):
                pe.wait_ge(loaded, 16)
                lead(pe, ready)
                with pe.Fori(0, B) as b:
                    for n, (r, g) in enumerate(jobs):
                        kind, c, p = rows[r]
                        pe.wait_ge(split, b * J + n - 3 + LEAD)
                        for x in range(RG):
                            at = g * RG + x
                            q = QF[:, c, bass.ds(b * L, L)]
                            rhs = q[:, at * W:(at + 1) * W] if kind == 0 else \
                                q.rearrange("p (h w) -> p h w", w=W)[:, :, at]
                            lhs = table[:, kind, p, H - 1 - at:2 * H - 1 - at, :].rearrange("p k e -> p (k e)")
                            mm = pe.matmul(acc[n % 4][:, x * H:(x + 1) * H], lhs, rhs, start=True, stop=True)
                        mm.then_inc(ready, 1)

            @block.scalar
            def _(act):
                lead(act, rounded)
                with act.Fori(0, B) as b:
                    for n, (r, g) in enumerate(jobs):
                        act.wait_ge(ready, b * J + n + 1 + LEAD)
                        if g == 0:
                            act.wait_ge(stored[r % 2], b * 16 * NR + r // 2 * 32)
                        act.activation(home(n, hi), banked(n), ACT.Copy).then_inc(rounded, 1)

            @block.vector
            def _(dve):
                lead(dve, split)
                with dve.Fori(0, B) as b:
                    for n, (r, g) in enumerate(jobs):
                        dve.wait_ge(rounded, b * J + n + 1 + LEAD)
                        dve.tensor_tensor(home(n, lo), banked(n), home(n, hi), ALU.subtract).then_inc(split, 1)


def layer3_attention(nc, t, parts_dram, rel_dram, V, eye, o_dram):
    LEAD = 16
    KT = L // 128
    NQC = len(LCH)
    PAIRS = KT // 2
    SPH = NQC * PAIRS
    HPB = 2
    ST = SPH * HPB
    NMX = KT * NQC
    MX_FROM, MX_TO = 9, SPH - 5
    MT_AT = SPH - 3
    QUADS = [(qc, a, min(2, PAIRS - a)) for qc in range(NQC) for a in range(0, PAIRS, 2)]
    NQD = len(QUADS)
    ONE = 2 * HD
    ROW_SHIFT = 112
    with Scope(nc, "l3a") as s:
        QA = [s.sb(f"qa{i}", [128, L], F16) for i in range(2)]
        QB = [s.sb(f"qb{i}", [ROW_SHIFT + 1, L], F16) for i in range(2)]
        KA = [s.sb(f"ka{i}", [128, L], F16) for i in range(2)]
        KB = [s.sb(f"kb{i}", [ROW_SHIFT + 1, L], F16) for i in range(2)]
        VH = [s.sb(f"vh{i}", [128, KT, ONE]) for i in range(2)]
        P = s.sb("p", [128, 4, 2, CH])
        MX = s.sb("mx", [128, KT, NQC])
        M = s.sb("m", [128, KT])
        M16 = s.sb("m16", [KT, 128], F16)
        OS = s.sb("os", [128, 2, CH])
        RC = s.sb("rc", [HD, 2, CH])
        OUT = [s.sb(f"out{i}", [HD, L]) for i in range(2)]
        SEL = s.sb("sel", [128, 64])
        s_ps = [s.ps(f"s{i}", [128, 2, CH]) for i in range(2)]
        mx_ps = [s.ps(f"mx{i}", [128, CH]) for i in range(2)]
        o_ps = s.ps("o", [128, CH])
        misc = s.ps("misc", [128, CH])
        consts, ones_set = s.sem("consts"), s.sem("ones_set")
        loaded = [s.sem(f"loaded{i}") for i in range(2)]
        v_ready = [s.sem(f"v_ready{i}") for i in range(2)]
        shift_loaded = [s.sem(f"shift_loaded{i}") for i in range(2)]
        out_stored = [s.sem(f"out_stored{i}") for i in range(2)]
        scored, exped, summed, o_taken, misc_made, misc_taken, mx_made, mx_taken, m_made, m16_made, inverted = (
            s.sem(n) for n in ("scored", "exped", "summed", "o_taken", "misc_made", "misc_taken", "mx_made",
                               "mx_taken", "m_made", "m16_made", "inverted"))
        LOADS = 10 * 16
        START = {scored: ST, summed: 2 * NQD}

        quad_at, qc_end_at, mx_at = {}, {}, {}
        quad_of = {}
        for e in range(HPB):
            for q, (qc, a, n) in enumerate(QUADS):
                last = e * SPH + qc * PAIRS + a + n - 1
                for k in range(n):
                    quad_of[last - k] = e * NQD + q
                quad_at.setdefault(last + 2, []).append((e, q))
                if a + n == PAIRS:
                    qc_end_at.setdefault(last + 3, []).append((e, qc))
            span = MX_TO - MX_FROM
            for u in range(NMX):
                mx_at.setdefault(e * SPH + MX_FROM + u * span // NMX, []).append((e, u))
        MISC = NQC * HPB + HPB

        def misc_index(e, what):
            order = []
            for g in range(ST + 3):
                order += [x for x in qc_end_at.get(g, [])]
                if g < ST and g % SPH == MT_AT:
                    order.append((g // SPH, "m"))
            return order.index((e, what))

        def lead(eng, *sems):
            for x in sems:
                eng.sem_inc(x, START.get(x, LEAD))

        def load_head(sp, head, buf):
            row = head * HD
            qk = [(QA, 0, 0, 0), (QA, 112, 0, 0), (QB, 0, 0, 1), (KA, 0, 1, 0), (KA, 112, 1, 1), (KB, 0, 1, 0)]
            for dst, at, which, part in qk:
                sp.dma_start(dst[buf][at:at + HD, :], parts_dram[which][part][bass.ds(row, HD), :])\
                  .then_inc(loaded[buf], 16)
            for dst, part in ((QA, 0), (QB, 1)):
                for at, kind in ((16, 1), (64, 0)):
                    sp.dma_start(dst[buf][at:at + H, :],
                                 rel_dram[kind][part][bass.ds(head, 1), :, :].rearrange("a k l -> (a k) l"))\
                      .then_inc(loaded[buf], 16)

        def load_shift(sp, buf):
            sp.dma_start(QB[buf][ROW_SHIFT:ROW_SHIFT + 1, :].rearrange("a (t q) -> a t q", q=128), M16[:, :])\
              .then_inc(shift_loaded[buf], 16)

        with s.block() as block:
            @block.sync
            def _(sp):
                for i in range(2):
                    sp.dma_start(KA[i][16:112, :], t["l3_places"][0:96, :]).then_inc(consts, 16)
                    sp.dma_start(KB[i][16:113, :], t["l3_places"]).then_inc(consts, 16)
                sp.dma_start(SEL[:], t["l3_sel"]).then_inc(consts, 16)
                load_head(sp, 0, 0)
                sp.wait_ge(m16_made, 1 + LEAD)
                load_shift(sp, 0)
                with sp.Fori(0, BH // HPB) as i:
                    for e in range(HPB):
                        nxt = (i * HPB + e + 1) % BH if e == HPB - 1 else i * HPB + e + 1
                        sp.wait_ge(scored, i * ST + e * SPH + ST)
                        load_head(sp, nxt, 1 - e)
                        sp.wait_ge(m16_made, i * HPB + e + 2 + LEAD)
                        load_shift(sp, 1 - e)
                        sp.wait_ge(misc_taken, i * MISC + 1 + misc_index(e, NQC - 1) + 1 + LEAD)
                        row = i * (HPB * HD) + e * HD
                        sp.dma_start(o_dram[bass.ds(row, HD), :], OUT[e][:]).then_inc(out_stored[e], 16)
                for x in out_stored:
                    sp.wait_ge(x, 16 * BH // HPB)
                sp.wait_ge(shift_loaded[0], 16 * (BH // HPB + 1))

            @block.gpsimd
            def _(pool):
                for i in range(2):
                    pool.memset(VH[i][:, :, HD:ONE], 1.0).then_inc(ones_set, 1)

                with pool.Fori(0, B) as b:
                    with pool.Fori(0, NH // HPB) as j:
                        i = pool.snap(b * (NH // HPB) + j)
                        for e in range(HPB):
                            pool.wait_ge(summed, i * HPB * NQD + (e + 1) * NQD)
                            pool.wait_ge(ones_set, 2)
                            pool.tensor_copy(VH[e][:, :, 0:HD].unsqueeze(2),
                                             V[:, bass.ds(b * KT, KT), bass.ds(j * HPB + e, 1), :])\
                                .then_inc(v_ready[e], 1)

            @block.tensor
            def _(pe):
                pe.wait_ge(consts, 16 * 5)
                lead(pe, scored, summed, misc_made, mx_made)

                def mx_pass(buf, u, base):
                    qt, c = divmod(u, NQC)
                    at, w = LCH[c]
                    pe.wait_ge(mx_taken, base + u - 1 + LEAD)
                    pe.matmul(mx_ps[u % 2][:, 0:w], QA[buf][:, qt * 128:(qt + 1) * 128], KA[buf][:, at:at + w],
                              start=True, stop=True).then_inc(mx_made, 1)

                def turn_shift(count, uses):
                    pe.wait_ge(m_made, count + LEAD)
                    pe.wait_ge(misc_taken, uses + LEAD)
                    pe.transpose(misc[0:KT, 0:128], M[:], eye[:, :]).then_inc(misc_made, 1)

                def score(i, g):
                    e, x = divmod(g, SPH)
                    at, w = LCH[x // PAIRS]
                    if x == 0:
                        pe.wait_ge(shift_loaded[e], (i + 1) * 16)
                    pe.wait_ge(exped, i * ST + g - 1 + LEAD)
                    for y in range(2):
                        kt = 2 * (x % PAIRS) + y
                        out = s_ps[g % 2][:, y, 0:w]
                        keys = slice(kt * 128, (kt + 1) * 128)
                        pe.matmul(out, KA[e][:, keys], QA[e][:, at:at + w], start=True, stop=False)
                        mm = pe.matmul(out, KB[e][:, keys], QB[e][:, at:at + w], start=False, stop=True)
                    mm.then_inc(scored, 1)

                def values(i, e, q):
                    qc, a, n = QUADS[q]
                    w = LCH[qc][1]
                    last = e * SPH + qc * PAIRS + a + n - 1
                    pe.wait_ge(exped, i * ST + last + 1 + LEAD)
                    if q == 0:
                        pe.wait_ge(v_ready[e], i + 1)
                    if a == 0:
                        pe.wait_ge(o_taken, i * HPB * NQC + e * NQC + qc + LEAD)
                    for k in range(2 * n):
                        kt = 2 * a + k
                        g = e * SPH + qc * PAIRS + kt // 2
                        grp = kt % 4
                        mm = pe.matmul(o_ps[32 * grp:32 * grp + 32, 0:w], VH[e][:, kt, :], P[:, g % 4, kt % 2, 0:w],
                                       start=a == 0, stop=kt + 4 >= KT)
                    mm.then_inc(summed, 1)

                def add_groups(i, e, qc):
                    n = e * NQC + qc
                    w = LCH[qc][1]
                    pe.wait_ge(o_taken, i * HPB * NQC + n + 1 + LEAD)
                    pe.wait_ge(misc_taken, i * MISC + 1 + misc_index(e, qc) + LEAD)
                    pe.matmul(misc[0:64, 0:w], SEL[:], OS[:, n % 2, 0:w], start=True, stop=True).then_inc(misc_made, 1)

                pe.wait_ge(loaded[0], LOADS)
                for u in range(NMX):
                    mx_pass(0, u, 0)
                turn_shift(1, 0)
                with pe.Fori(0, BH // HPB) as i:
                    for g in range(ST + 4):
                        if g < ST:
                            score(i, g)
                        for e, q in quad_at.get(g, []):
                            values(i, e, q)
                        for e, qc in qc_end_at.get(g, []):
                            add_groups(i, e, qc)
                        for e, u in mx_at.get(g, []):
                            if u == 0:
                                pe.wait_ge(loaded[1 - e], (i + 1 + e) * LOADS)
                            mx_pass(1 - e, u, i * HPB * NMX + (e + 1) * NMX)
                        if g < ST and g % SPH == MT_AT:
                            e = g // SPH
                            turn_shift(i * HPB + e + 2, i * MISC + 1 + misc_index(e, "m"))

            @block.scalar
            def _(act):
                lead(act, exped)
                with act.Fori(0, BH // HPB) as i:
                    for g in range(ST):
                        w = LCH[g % SPH // PAIRS][1]
                        act.wait_ge(scored, i * ST + g + 1 + ST)
                        before = quad_of[g - 4] + 1 if g >= 4 else 0
                        act.wait_ge(summed, i * HPB * NQD + before + 2 * NQD)
                        act.activation(P[:, g % 4, :, 0:w], s_ps[g % 2][:, :, 0:w], ACT.Exp).then_inc(exped, 1)

            @block.vector
            def _(dve):
                lead(dve, o_taken, misc_taken, mx_taken, m_made, m16_made, inverted)

                def mx_take(u, base):
                    qt, c = divmod(u, NQC)
                    dve.wait_ge(mx_made, base + u + 1 + LEAD)
                    dve.tensor_reduce(MX[:, qt, c:c + 1], mx_ps[u % 2][:, 0:LCH[c][1]], AX_X, ALU.max)\
                       .then_inc(mx_taken, 1)

                def mx_join(base, count, uses):
                    dve.wait_ge(mx_taken, base + NMX + LEAD)
                    dve.wait_ge(misc_made, uses + LEAD)
                    dve.tensor_reduce(M[:], MX[:], AX_X, ALU.max).then_inc(m_made, 1)

                def m16(uses, shifts):
                    dve.wait_ge(misc_made, uses + LEAD)
                    for sem, n in shifts:
                        dve.wait_ge(sem, n)
                    dve.tensor_scalar(M16[:], misc[0:KT, 0:128], -1.0, None, ALU.mult).then_inc(m16_made, 1)

                def take_o(i, e, qc):
                    n = e * NQC + qc
                    w = LCH[qc][1]
                    dve.wait_ge(summed, i * HPB * NQD + e * NQD + (qc + 1) * (NQD // NQC) + 2 * NQD)
                    dve.tensor_copy(OS[:, n % 2, 0:w], o_ps[:, 0:w]).then_inc(o_taken, 1)

                def norm(i, e, qc):
                    n = e * NQC + qc
                    at, w = LCH[qc]
                    dve.wait_ge(misc_made, i * MISC + 1 + misc_index(e, qc) + 1 + LEAD)
                    dve.reciprocal(RC[:, n % 2, 0:w], misc[32:32 + HD, 0:w]).then_inc(inverted, 1)
                    if qc == 0:
                        dve.wait_ge(out_stored[e], i * 16)
                    dve.wait_ge(inverted, i * HPB * NQC + n + 1 + LEAD)
                    dve.tensor_tensor(OUT[e][:, at:at + w], misc[0:HD, 0:w], RC[:, n % 2, 0:w], ALU.mult)\
                       .then_inc(misc_taken, 1)

                for u in range(NMX):
                    mx_take(u, 0)
                mx_join(0, 1, 0)
                m16(1, [])
                dve.wait_ge(m16_made, 1 + LEAD)
                dve.sem_inc(misc_taken, 1)
                with dve.Fori(0, BH // HPB) as i:
                    for g in range(ST + 4):
                        for e, qc in qc_end_at.get(g, []):
                            norm(i, e, qc)
                        for e, q in quad_at.get(g, []):
                            if QUADS[q][1] + QUADS[q][2] == PAIRS:
                                take_o(i, e, QUADS[q][0])
                        for e, u in mx_at.get(g, []):
                            base = i * HPB * NMX + (e + 1) * NMX
                            mx_take(u, base)
                            if u == NMX - 1:
                                mx_join(base, 0, i * MISC + 1 + (misc_index(0, "m") + 1 if e else 0))
                        if g < ST and g % SPH == MT_AT:
                            e = g // SPH
                            uses = i * MISC + 1 + misc_index(e, "m") + 1
                            m16(uses, [(shift_loaded[e], (i + 1) * 16)])
                            dve.wait_ge(m16_made, i * HPB + e + 2 + LEAD)
                            dve.sem_inc(misc_taken, 1)


def load_output(nc, name, o_dram, OT):
    with Scope(nc, name) as s:
        loaded = s.sem("loaded")
        with s.block() as block:
            @block.sync
            def _(sp):
                for c in range(CC):
                    for b in range(B):
                        sp.dma_start(OT[:, c, b * L:(b + 1) * L],
                                     o_dram[b * C + c * CP:b * C + (c + 1) * CP, :]).then_inc(loaded, 16)
                sp.wait_ge(loaded, 16 * CC * B)


def build(nc, t, out, layers=4):
    with ExitStack() as outer:
        g = Scope(nc, "g")
        outer.enter_context(g)
        X = g.sb("x", [CP, CC, TOK])
        group_mean = g.sb("group_mean", [CP, CP])
        eye = g.sb("eye", [128, 128])
        ones_mean = g.sb("ones_mean", [DI, DI])
        scratch = {}

        def dram(name, shape, dtype):
            return nc.dram_tensor(name, shape, dtype, kind="Internal").ap()

        def load(sp, sem):
            for c in range(CC):
                for b in range(B):
                    sp.dma_start(X[:, c, b * L:(b + 1) * L], t["xT"][c * CP:(c + 1) * CP, b * L:(b + 1) * L])\
                      .then_inc(sem, 16)
            sp.dma_start(group_mean[:], t["group_mean"]).then_inc(sem, 16)
            sp.dma_start(eye[:], t["eye"]).then_inc(sem, 16)
            sp.dma_start(ones_mean[:], t["ones_mean"]).then_inc(sem, 16)
        load.total = 16 * (CC * B + 3)

        with Scope(nc, "l0") as s0:
            parts = [[dram(f"l0_{w}{p}", [B * C, LK], F16) for p in range(2)] for w in "qk"]
            v_dram = dram("l0_values", [TOK + 128, NH * VE], F32)
            V = s0.sb("v", [110, B, NPT, len(CUTS), NH, VE])
            v_stored, v_loaded = s0.sem("v_stored"), s0.sem("v_loaded")

            def load_patches(sp):
                n = 0
                reg_at = CUTS[-1][1] * KW
                for b in range(B):
                    for p in range(NPT):
                        _, (kr, kc), _ = window_of(p)
                        for c, (r0, nr) in enumerate(CUTS):
                            src = v_dram[b * L:(b + 1) * L, :].rearrange("(h w) e -> h w e", w=W)
                            sp.dma_start(V[0:nr * KW, b, p, c, :, :].rearrange("p h e -> p (h e)"),
                                         src[kr + r0:kr + r0 + nr, kc:kc + KW, :]).then_inc(v_loaded, 16)
                            n += 1
                        sp.dma_start(V[reg_at:reg_at + NREG, b, p, len(CUTS) - 1, :, :].rearrange("p h e -> p (h e)"),
                                     v_dram[TOK:TOK + NREG, :]).then_inc(v_loaded, 16)
                        n += 1
                return n

            with Scope(nc, "l0n") as sn:
                XN = sn.sb("xn", [CP, CC, TOK])
                group_norm(nc, "gn0", X, XN, group_mean, load)
                with Scope(nc, "l0vt") as sv:
                    VT = sv.sb("vt", [128, TOK // 128 + 1, NH, VE])
                    ones_set = sv.sem("ones_set")
                    with nc.Block() as block:
                        @block.vector
                        def _(dve):
                            dve.memset(VT[:, :, :, HD:VE], 1.0).then_inc(ones_set, 1)
                            dve.wait_ge(ones_set, 1)
                    v_projection(nc, "l0v", XN, t["l0_wT"], t["L0_conv_qkv_b"], VT, regs=t["l0_regsT"])
                    with nc.Block() as block:
                        @block.sync
                        def _(sp):
                            half = TOK // 256
                            for k in range(2):
                                sp.dma_start(
                                    v_dram[0:TOK, :].rearrange("(n p) e -> p n e", p=128)[:, k * half:(k + 1) * half, :],
                                    VT[:, k * half:(k + 1) * half, :, :].rearrange("p n h e -> p n (h e)"))\
                                  .then_inc(v_stored, 16)
                            sp.dma_start(v_dram[TOK:TOK + NREG, :],
                                         VT[0:NREG, TOK // 128, :, :].rearrange("p h e -> p (h e)")).then_inc(v_stored, 16)
                            sp.wait_ge(v_stored, 48)
                qk_projection(nc, "l0qk", XN, t["l0_wT"], t["L0_conv_qkv_b"], parts, regs=t["l0_regsT"],
                              early=load_patches, patches=True)
            with nc.Block() as block:
                @block.sync
                def _(sp):
                    sp.wait_ge(v_loaded, 16 * B * NPT * (len(CUTS) + 1))
            with Scope(nc, "l0o") as so:
                O = so.sb("o", [PH * PW, B * NPT, C])
                layer0_attention(nc, parts, O, V, t["l0_mask"], t["eye_bf"], eye)
                s0_ot = so.sb("ot", [CP, CC, TOK])
                turn_output(nc, "l0t", O, s0_ot, eye)
                out_projection(nc, "l0p", X, s0_ot, t["l0_owT"], t["L0_conv_out_b"], CP, CC)

        for layer in (1, 2):
            if layers <= layer:
                break
            pre = f"l{layer}_"
            z_dram = dram(pre + "z", [DI, TOK], F32)
            skip_dram = dram(pre + "skip", [B, DI, L], F32)
            dt_dram = dram(pre + "dtp", [B * ND, 4, 3, 8, 3, L], BF16)
            du_dram = dram(pre + "dup", [B * ND, 4, 3, 8, 3, L], BF16)
            bc_dram = dram(pre + "bcp", [B * ND * 2, 3, NS, L], BF16)
            y_dram = dram(pre + "y", [B * 2, DI, L], F32)
            with Scope(nc, pre + "u") as su:
                U = su.sb("u", [DI, B, L])
                UT = su.sb("ut", [DI, B, L])
                with Scope(nc, pre + "n") as sn:
                    XN = sn.sb("xn", [CP, CC, TOK])
                    group_norm(nc, f"gn{layer}", X, XN, group_mean)
                    ssm_conv(nc, pre + "conv", XN, t, pre, U, UT, z_dram)
                ssm_prepare(nc, pre + "prep", t, pre, U, UT, dt_dram, du_dram, bc_dram, skip_dram)
            ssm_scan(nc, pre + "scan", t, pre, dt_dram, du_dram, bc_dram, y_dram)
            with Scope(nc, pre + "o") as so:
                YG = so.sb("yg", [DI, 1, TOK])
                ssm_gate(nc, pre + "gate", t, pre, ones_mean, y_dram, skip_dram, z_dram, YG)
                out_projection(nc, pre + "proj", X, YG, t[pre + "owT"], None, DI, 1)

        if layers > 3:
            parts = [[dram(f"l3_{w}{p}", [B * C, L], F16) for p in range(2)] for w in "qk"]
            rel = [[dram(f"l3_rel{k}{p}", [BH, H, L], F16) for p in range(2)] for k in range(2)]
            o_dram = dram("l3_out", [B * C, L], F32)
            with Scope(nc, "l3") as s3:
                V = s3.sb("v", [128, TOK // 128, NH, HD])
                with Scope(nc, "l3q") as sq:
                    QF = sq.sb("qf", [CP, CC, TOK])
                    with Scope(nc, "l3n") as sn:
                        XN = sn.sb("xn", [CP, CC, TOK])
                        group_norm(nc, "gn3", X, XN, group_mean)
                        v_projection(nc, "l3v", XN, t["l3_wT"], t["l3_b"], V)
                        qk_projection(nc, "l3qk", XN, t["l3_wT"], t["l3_b"], parts, q_keep=QF)
                    rel_terms(nc, "l3r", QF, t, rel)
                layer3_attention(nc, t, parts, rel, V, eye, o_dram)
            with Scope(nc, "l3o") as so:
                OT = so.sb("ot", [CP, CC, TOK])
                load_output(nc, "l3l", o_dram, OT)
                out_projection(nc, "l3p", X, OT, t["l3_pwT"], t["l3_pb"], CP, CC)

        stored = g.sem("stored")
        with nc.Block() as block:
            @block.sync
            def _(sp):
                for c in range(CC):
                    sp.dma_start(out[c * CP:(c + 1) * CP, :], X[:, c, :]).then_inc(stored, 16)
                sp.wait_ge(stored, 16 * CC)


def shape_constants():
    bf16 = mybir.dt.np(BF16)
    k = {}
    p = np.arange(CP)
    k["group_mean"] = (p[:, None] // GC == p[None, :] // GC).astype(np.float32) / GC
    k["ones_mean"] = np.full((DI, DI), 1.0 / DI, np.float32)
    r, q = np.arange(128)[:, None], np.arange(128)[None]
    k["e4"] = ((r % 32 < 24) & (r % 32 % 8 == q // NS)).astype(bf16)
    k["en"] = (r[:3 * NS] % NS == q % NS).astype(bf16)
    col = np.arange(32)[None, None]
    k["state_sum"] = (col == 8 * np.arange(4)[None, :, None] + np.arange(128)[:, None, None] // NS).astype(np.float32)
    places = np.zeros((97, L), np.float16)
    places[np.arange(L) % W, np.arange(L)] = 1
    places[W + np.arange(L) // W, np.arange(L)] = 1
    places[96] = 1
    k["l3_places"] = places
    sel = np.zeros((128, 64), np.float32)
    for grp in range(4):
        for d in range(HD):
            sel[32 * grp + d, d] = sel[32 * grp + HD + d, 32 + d] = 1
    k["l3_sel"] = sel
    k["eye"] = np.eye(128, dtype=np.float32)
    k["eye_bf"] = np.eye(128).astype(bf16)
    mask = np.zeros((9, PH * PW, WK + NREG), np.float32)
    for p in range(NPT):
        (qr, qc), (kr, kc), kind = window_of(p)
        qh, qw = np.divmod(np.arange(PH * PW), PW)
        kh, kw = np.divmod(np.arange(WK), KW)
        sh = np.clip(qh + qr - WIN // 2, 0, H - WIN)[:, None]
        sw = np.clip(qw + qc - WIN // 2, 0, W - WIN)[:, None]
        kh, kw = (kh + kr)[None], (kw + kc)[None]
        seen = (kh >= sh) & (kh < sh + WIN) & (kw >= sw) & (kw < sw + WIN)
        mask[kind, :, :WK] = np.where(seen, 0.0, -1e30)
    k["l0_mask"] = mask.astype(bf16)
    return k


def kernel(**inputs):
    import concourse.bacc as bacc
    from concourse.bass_utils import run_bass_kernel_spmd

    a = {n: np.ascontiguousarray(v) for n, v in inputs.items()}
    turned = lambda m: np.ascontiguousarray(m.T)
    data = {
        "xT": turned(a["x"].reshape(TOK, C)),
        "l0_wT": turned(a["L0_conv_qkv_w"]), "l0_regsT": turned(a["L0_conv_registers"]),
        "L0_conv_qkv_b": a["L0_conv_qkv_b"], "l0_owT": turned(a["L0_conv_out_w"]),
        "L0_conv_out_b": a["L0_conv_out_b"],
        **shape_constants(),
    }
    w = {n[8:]: v for n, v in a.items() if n.startswith("L3_conv_")}
    data["l3_wT"], data["l3_b"], data["l3_pwT"], data["l3_pb"] = w["qkv_w"], w["qkv_b"], w["proj_w"], w["proj_b"]
    rel = np.zeros((CP, 2, HPC // 2, 2 * H - 1, 2), np.float32)
    for kind, n in enumerate(("rel_pos_h", "rel_pos_w")):
        rows = np.minimum(np.arange(2 * H - 2, -1, -1), len(w[n]) - 1)
        for head in range(HPC):
            rel[head * HD:(head + 1) * HD, kind, head // 2, :, head % 2] = w[n][rows].T
    data["l3_rel"] = rel
    for layer in (1, 2):
        w = {n[8:]: v for n, v in a.items() if n.startswith(f"L{layer}_conv_")}
        p = f"l{layer}_"
        data[p + "in_wT"] = turned(w["in_proj_w"])
        data[p + "conv_w"] = w["conv_w"].reshape(DI, 9)
        data[p + "conv_b"] = w["conv_b"].reshape(DI, 1)
        xw = np.zeros((ND, DI, CP), np.float32)
        xw[:, :, 0:DT_R] = w["x_proj_w"][:, 0:DT_R].transpose(0, 2, 1)
        xw[:, :, 32:32 + NS] = w["x_proj_w"][:, DT_R:DT_R + NS].transpose(0, 2, 1)
        xw[:, :, 64:64 + NS] = w["x_proj_w"][:, DT_R + NS:].transpose(0, 2, 1)
        data[p + "xwT"] = xw
        data[p + "dtwT"] = np.ascontiguousarray(w["dt_projs_w"].transpose(0, 2, 1))
        data[p + "dtb"] = turned(w["dt_projs_b"])
        data[p + "D"] = turned(w["Ds"].reshape(ND, DI))
        al = w["A_logs"].reshape(2, 2, 3, 4, 8, NS).transpose(4, 5, 1, 0, 3, 2)
        data[p + "A"] = np.ascontiguousarray(al.reshape(128, 48))
        data[p + "norm_g"] = w["out_norm_g"].reshape(DI, 1)
        data[p + "norm_b"] = w["out_norm_b"].reshape(DI, 1)
        data[p + "owT"] = turned(w["out_proj_w"])
    nc = bacc.Bacc("TRN2", target_bir_lowering=False, num_devices=1)
    t = {n: nc.dram_tensor(f"in_{n}", v.shape, mybir.dt.from_np(v.dtype), kind="ExternalInput").ap()
         for n, v in data.items()}
    out = nc.dram_tensor("out", (C, TOK), F32, kind="ExternalOutput").ap()
    build(nc, t, out)
    r = run_bass_kernel_spmd(nc, [{f"in_{n}": v for n, v in data.items()}], core_ids=[0])
    return np.ascontiguousarray(r.results[0]["out"].T).reshape(B, H, W, C)
```

```python
from contextlib import ExitStack

import numpy as np

import concourse.bass as bass
from concourse import mybir

F32 = mybir.dt.float32
F16 = mybir.dt.float16
BF16 = mybir.dt.bfloat16
ALU = mybir.AluOpType
ACT = mybir.ActivationFunctionType
AX_X = mybir.AxisListType.X

B, H, W, C = 2, 48, 48, 192
L = H * W
TOK = B * L
CP, CC = 96, 2
NH, HD = 12, 16
HPC = CP // HD
BH = B * NH
GROUPS = 32
GC = C // GROUPS
CH = 512
LCH = [(s, min(CH, L - s)) for s in range(0, L, CH)]
TCH = [(s, CH) for s in range(0, TOK, CH)]
NREG = 16
WIN = 7
PH, PW = 8, 16
NPH, NPW = H // PH, W // PW
NPT = NPH * NPW
KH, KW = PH + WIN - 1, PW + WIN - 1
CUTS = [(0, 5), (5, 5), (10, 4)]
WK = KH * KW
LK = L + NREG
DI, NS, DT_R, ND = 96, 16, 12, 4
QUARTER = HD ** -0.5
A_MOST, DT_LEAST = 2.0 ** 115, 2.0 ** -109


class Chain:

    def __init__(self, eng, sem, base=0):
        self.eng, self.sem, self.base, self.n = eng, sem, base, 0

    def __call__(self, ins):
        self.n += 1
        ins.then_inc(self.sem, 1)
        self.eng.wait_ge(self.sem, self.base + self.n)


class Scope:

    def __init__(self, nc, name):
        self.nc, self.name, self.stack, self.sems = nc, name, ExitStack(), []

    def __enter__(self):
        return self

    def __exit__(self, *a):
        if self.sems:
            self.nc.clear_and_free_semaphores(self.sems)
            self.nc.all_engine_barrier()
        return self.stack.__exit__(*a)

    def sb(self, name, shape, dtype=F32):
        return self.stack.enter_context(self.nc.sbuf_tensor(f"{self.name}_{name}", shape, dtype))

    def ps(self, name, shape, dtype=F32):
        return self.stack.enter_context(self.nc.psum_tensor(f"{self.name}_{name}", shape, dtype))

    def sem(self, name):
        self.sems.append(self.nc.alloc_semaphore(f"{self.name}_{name}"))
        return self.sems[-1]

    def block(self):
        return self.nc.Block()


def group_norm(nc, name, X, XN, group_mean, load=None):
    with Scope(nc, name) as s:
        stats = s.sb("stats", [CP, CC * B, len(LCH), 6])
        mv = s.sb("mv", [CP, CC * B, 2])
        gmean = s.sb("gmean", [CP, CC * B])
        dev = s.sb("dev", [CP, CC * B])
        spread = s.sb("spread", [CP, CC * B])
        sd = s.sb("sd", [CP, CC * B])
        rstd = s.sb("rstd", [CP, CC * B])
        shift = s.sb("shift", [CP, CC * B])
        gm_ps = s.ps("gm_ps", [CP, 512])
        gv_ps = s.ps("gv_ps", [CP, 512])
        loaded = s.sem("loaded")
        channel_ready, gm_ready, spread_ready, gv_ready = (
            s.sem(n) for n in ("channel", "gm", "spread", "gv"))
        var_ready, sd_ready, affine_ready, own = (s.sem(n) for n in ("var", "sd", "affine", "own"))
        xn_dve, xn_act = s.sem("xn_dve"), s.sem("xn_act")
        parts = [(c, b) for c in range(CC) for b in range(B)]
        with s.block() as block:
            if load is not None:
                @block.sync
                def _(sp):
                    load(sp, loaded)

            @block.vector
            def _(dve):
                link = Chain(dve, own)
                if load is not None:
                    dve.wait_ge(loaded, load.total)
                for n, (c, b) in enumerate(parts):
                    for k, (at, w) in enumerate(LCH):
                        last = dve.bn_stats(stats[:, n, k, :], X[:, c, b * L + at:b * L + at + w])
                link(last)
                for n in range(len(parts)):
                    last = dve.bn_aggr(mv[:, n, :], stats[:, n, :, :].rearrange("p k s -> p (k s)"))
                last.then_inc(channel_ready, 1)
                dve.wait_ge(gm_ready, 1)
                dve.tensor_copy(gmean[:], gm_ps[:, 0:CC * B]).then_inc(own, 1)
                link.n += 1
                link(dve.tensor_tensor(dev[:], mv[:, :, 0], gm_ps[:, 0:CC * B], ALU.subtract))
                link(dve.tensor_tensor(spread[:], dev[:], dev[:], ALU.mult))
                link(dve.tensor_tensor(spread[:], spread[:], mv[:, :, 1], ALU.add))
                dve.sem_inc(spread_ready, 1)
                dve.wait_ge(gv_ready, 1)
                dve.tensor_scalar(sd[:], gv_ps[:, 0:CC * B], 1e-5, None, ALU.add).then_inc(var_ready, 1)
                dve.wait_ge(sd_ready, 1)
                link(dve.reciprocal(rstd[:], sd[:]))
                dve.scalar_tensor_tensor(shift[:], gmean[:], -1.0, rstd[:], ALU.mult, ALU.mult)\
                   .then_inc(affine_ready, 1)
                dve.wait_ge(affine_ready, 1)
                for n, (c, b) in enumerate(parts):
                    if n % 2:
                        dve.tensor_scalar(XN[:, c, b * L:(b + 1) * L], X[:, c, b * L:(b + 1) * L],
                                          rstd[:, n:n + 1], shift[:, n:n + 1], ALU.mult, ALU.add)\
                           .then_inc(xn_dve, 1)
                dve.wait_ge(xn_dve, 2)

            @block.tensor
            def _(pe):
                pe.wait_ge(channel_ready, 1)
                pe.matmul(gm_ps[:, 0:CC * B], group_mean[:, :], mv[:, :, 0], start=True, stop=True)\
                  .then_inc(gm_ready, 1)
                pe.wait_ge(spread_ready, 1)
                pe.matmul(gv_ps[:, 0:CC * B], group_mean[:, :], spread[:], start=True, stop=True)\
                  .then_inc(gv_ready, 1)

            @block.scalar
            def _(act):
                act.wait_ge(var_ready, 1)
                act.activation(sd[:], sd[:], ACT.Sqrt).then_inc(sd_ready, 1)
                act.wait_ge(affine_ready, 1)
                for n, (c, b) in enumerate(parts):
                    if n % 2 == 0:
                        act.activation(XN[:, c, b * L:(b + 1) * L], X[:, c, b * L:(b + 1) * L],
                                       ACT.Identity, scale=rstd[:, n:n + 1], bias=shift[:, n:n + 1])\
                           .then_inc(xn_act, 1)
                act.wait_ge(xn_act, 2)


def out_projection(nc, name, X, OT, wT, bias_dram, rows, chunks):
    with Scope(nc, name) as s:
        w_sb = s.sb("w", [rows, chunks, C])
        b_sb = s.sb("b", [CP, CC])
        acc = [s.ps(f"acc{i}", [CP, CH]) for i in range(4)]
        loaded, ready, added = s.sem("loaded"), s.sem("ready"), s.sem("added")
        jobs = [(m, at, w) for m in range(CC) for at, w in TCH]
        with s.block() as block:
            @block.sync
            def _(sp):
                sp.dma_start(w_sb[:], wT.rearrange("(k p) n -> p k n", p=rows)).then_inc(loaded, 16)
                if bias_dram is not None:
                    with nc.allow_non_contiguous_dma(reason="a bias column"):
                        sp.dma_start(b_sb[:], bias_dram.rearrange("(c p) -> p c", p=CP)).then_inc(loaded, 16)
                sp.wait_ge(loaded, 32 if bias_dram is not None else 16)

            @block.tensor
            def _(pe):
                pe.wait_ge(loaded, 32 if bias_dram is not None else 16)
                for n, (m, at, w) in enumerate(jobs):
                    if n >= 4:
                        pe.wait_ge(added, n - 3)
                    for k in range(chunks):
                        mm = pe.matmul(acc[n % 4][:, 0:w], w_sb[:, k, m * CP:(m + 1) * CP],
                                       OT[:, k, at:at + w], start=k == 0, stop=k == chunks - 1)
                    mm.then_inc(ready, 1)

            @block.vector
            def _(dve):
                for n, (m, at, w) in enumerate(jobs):
                    dve.wait_ge(ready, n + 1)
                    x = X[:, m, at:at + w]
                    if bias_dram is not None:
                        dve.scalar_tensor_tensor(x, acc[n % 4][:, 0:w], b_sb[:, m:m + 1], x,
                                                 ALU.add, ALU.add).then_inc(added, 1)
                    else:
                        dve.tensor_tensor(x, acc[n % 4][:, 0:w], x, ALU.add).then_inc(added, 1)
                dve.wait_ge(added, len(jobs))


def qk_projection(nc, name, XN, wT, bias_dram, parts_dram, regs=None, q_keep=None, early=(),
                  patches=False):
    lch = [(at, PH * W) for at in range(0, L, PH * W)] if patches else LCH
    wide = L + (NREG if regs is not None else 0)
    with Scope(nc, name) as s:
        w_sb = s.sb("w", [CP, CC, 2 * C])
        b_sb = s.sb("b", [CP, 2 * CC])
        r_sb = s.sb("r", [CP, CC, NREG])
        val = s.sb("val", [CP, 4, CH])
        hi = s.sb("hi", [CP, 2, LK], F16)
        lo = s.sb("lo", [CP, 2, LK], F16)
        acc = [s.ps(f"acc{i}", [CP, CH]) for i in range(4)]
        loaded, ready, valued, rounded, split = (
            s.sem(n) for n in ("loaded", "ready", "valued", "rounded", "split"))
        stored = [s.sem(f"stored{i}") for i in range(2)]
        n_loads = 32 + (16 if regs is not None else 0)
        rows = [(q, c, b) for q in range(2) for c in range(CC) for b in range(B)]
        jobs = []
        for slot, (q, c, b) in enumerate(rows):
            for at, w in lch:
                jobs.append((slot, q, c, b, at, w, False))
            if regs is not None:
                jobs.append((slot, q, c, b, L, NREG, True))
        per = len(jobs) // len(rows)
        with s.block() as block:
            @block.sync
            def _(sp):
                sp.dma_start(w_sb[:], wT.rearrange("(k p) n -> p k n", p=CP)[:, :, 0:2 * C]).then_inc(loaded, 16)
                with nc.allow_non_contiguous_dma(reason="a bias column"):
                    sp.dma_start(b_sb[:], bias_dram[0:2 * C].rearrange("(c p) -> p c", p=CP))\
                      .then_inc(loaded, 16)
                if regs is not None:
                    sp.dma_start(r_sb[:], regs.rearrange("(k p) n -> p k n", p=CP)).then_inc(loaded, 16)
                for slot, (q, c, b) in enumerate(rows):
                    for load in early[slot::len(rows)]:
                        load(sp)
                    sp.wait_ge(split, per * (slot + 1))
                    at = b * C + c * CP
                    for part, t in enumerate((hi, lo)):
                        sp.dma_start(parts_dram[q][part][at:at + CP, :], t[:, slot % 2, 0:wide])\
                          .then_inc(stored[slot % 2], 16)
                for x in stored:
                    sp.wait_ge(x, 16 * len(rows))

            @block.tensor
            def _(pe):
                pe.wait_ge(loaded, n_loads)
                for n, (slot, q, c, b, at, w, is_reg) in enumerate(jobs):
                    if n >= 4:
                        pe.wait_ge(valued, n - 3)
                    for k in range(CC):
                        rhs = r_sb[:, k, :] if is_reg else XN[:, k, b * L + at:b * L + at + w]
                        mm = pe.matmul(acc[n % 4][:, 0:w], w_sb[:, k, q * C + c * CP:q * C + (c + 1) * CP],
                                       rhs, start=k == 0, stop=k == CC - 1)
                    mm.then_inc(ready, 1)

            def value(n):
                slot, q, c, b, at, w, is_reg = jobs[n]
                if q_keep is not None and q == 0:
                    return q_keep[:, c, b * L + at:b * L + at + w]
                return val[:, n % 4, 0:w]

            def home(n, ap):
                if patches and jobs[n][1] == 0 and not jobs[n][6]:
                    return ap.rearrange("p (h x w) -> p x h w", x=NPW, w=PW)
                return ap

            def stored_order(n, ap):
                if patches and jobs[n][1] == 0 and not jobs[n][6]:
                    return ap.rearrange("p (x h w) -> p x h w", h=PH, w=PW)
                return ap

            @block.vector
            def _(dve):
                dve.wait_ge(loaded, n_loads)
                for n in range(len(jobs) + 1):
                    if n < len(jobs):
                        slot, q, c, b, at, w, _ = jobs[n]
                        dve.wait_ge(ready, n + 1)
                        if n >= 4:
                            dve.wait_ge(rounded, n - 3)
                        dve.tensor_scalar(value(n), acc[n % 4][:, 0:w], b_sb[:, q * CC + c:q * CC + c + 1],
                                          QUARTER if q else 1.0, ALU.add, ALU.mult).then_inc(valued, 1)
                    if n >= 1:
                        slot, q, c, b, at, w, _ = jobs[n - 1]
                        dve.wait_ge(rounded, n)
                        dve.wait_ge(valued, n)
                        if slot >= 2:
                            dve.wait_ge(stored[slot % 2], 32 * (slot // 2))
                        dve.tensor_tensor(stored_order(n - 1, lo[:, slot % 2, at:at + w]), home(n - 1, value(n - 1)),
                                          stored_order(n - 1, hi[:, slot % 2, at:at + w]), ALU.subtract)\
                           .then_inc(split, 1)

            @block.scalar
            def _(act):
                for n, (slot, q, c, b, at, w, _) in enumerate(jobs):
                    act.wait_ge(valued, n + 1)
                    if slot >= 2:
                        act.wait_ge(stored[slot % 2], 32 * (slot // 2))
                    act.activation(stored_order(n, hi[:, slot % 2, at:at + w]), home(n, value(n)), ACT.Copy)\
                       .then_inc(rounded, 1)


def v_projection(nc, name, XN, wT, bias_dram, V, regs=None):
    with Scope(nc, name) as s:
        w_sb = s.sb("w", [CP, CC, C])
        bias = s.sb("bias", [128, C])
        r_sb = s.sb("r", [CP, CC, NREG])
        acc = [s.ps(f"acc{i}", [128, CH]) for i in range(4)]
        loaded, ready, done = s.sem("loaded"), s.sem("ready"), s.sem("done")
        n_loads = 32 + (16 if regs is not None else 0)
        jobs = [(n, 128) for n in range(TOK // 128)] + ([(TOK // 128, NREG)] if regs is not None else [])
        with s.block() as block:
            @block.sync
            def _(sp):
                sp.dma_start(w_sb[:], wT.rearrange("(k p) n -> p k n", p=CP)[:, :, 2 * C:3 * C]).then_inc(loaded, 16)
                sp.dma_start(bias[:], bias_dram[2 * C:3 * C].rearrange("(a n) -> a n", a=1).to_broadcast([128, C]))\
                  .then_inc(loaded, 16)
                if regs is not None:
                    sp.dma_start(r_sb[:], regs.rearrange("(k p) n -> p k n", p=CP)).then_inc(loaded, 16)
                sp.wait_ge(loaded, n_loads)

            @block.tensor
            def _(pe):
                pe.wait_ge(loaded, n_loads)
                for n, (tile, rows) in enumerate(jobs):
                    if n >= 4:
                        pe.wait_ge(done, n - 3)
                    for k in range(CC):
                        src = XN[:, k, tile * 128:(tile + 1) * 128] if rows == 128 else r_sb[:, k, :]
                        mm = pe.matmul(acc[n % 4][0:rows, 0:C], src, w_sb[:, k, :], start=k == 0, stop=k == CC - 1)
                    mm.then_inc(ready, 1)

            @block.vector
            def _(dve):
                dve.wait_ge(loaded, n_loads)
                for n, (tile, rows) in enumerate(jobs):
                    dve.wait_ge(ready, n + 1)
                    dve.tensor_tensor(V[0:rows, tile, :, 0:HD], acc[n % 4][0:rows, 0:C].rearrange("p (h d) -> p h d", d=HD),
                                      bias[0:rows, :].rearrange("p (h d) -> p h d", d=HD), ALU.add)\
                       .then_inc(done, 1)
                dve.wait_ge(done, len(jobs))


def window_of(p):
    r, c = divmod(p, NPW)
    kr = min(max(r * PH - WIN // 2, 0), H - KH)
    kc = min(max(c * PW - WIN // 2, 0), W - KW)
    kind = 3 * (0 if r == 0 else 2 if r == NPH - 1 else 1) + (0 if c == 0 else 2 if c == NPW - 1 else 1)
    return (r * PH, c * PW), (kr, kc), kind


def image_of(ap):
    return ap.rearrange("p (h w) -> p h w", w=W)


def layer0_attention(nc, parts_dram, V, mask_d, eye_bf_d, eye, o_dram, sum_dram):
    HPB = 4
    UP = NPT
    U = 2 * UP
    NQ = U // 2
    QP = NQ // 2
    WKR = WK + NREG
    PQ = PH * PW
    VO = HD + 1
    ROWS = [n * KW + (NREG if k == len(CUTS) - 1 else 0) for k, (_, n) in enumerate(CUTS)]
    LEAD = U
    JB = NH // HPB
    LOADS, STORES = 6 * 16, 8 * 16
    with Scope(nc, "l0a") as s:
        Q = [s.sb(f"q{i}", [3 * HD, L], F16) for i in range(HPB)]
        K = [s.sb(f"k{i}", [3 * HD, LK], F16) for i in range(HPB)]
        VH = [s.sb(f"vh{i}", [110, NPT, len(CUTS), VO]) for i in range(HPB)]
        mask = s.sb("mask", [PQ, 9, WKR], BF16)
        eye_b = s.sb("eye_b", [PQ, PQ], BF16)
        nmax = s.sb("nmax", [PQ, 2, 2])
        P = s.sb("p", [PQ, 2, 2, WKR])
        PT = s.sb("pt", [128, 4, 2, len(CUTS), PQ])
        OS = [s.sb(f"os{i}", [128, QP, PQ]) for i in range(2)]
        s_ps = [s.ps(f"s{i}", [PQ, 2, CH]) for i in range(2)]
        t_ps = s.ps("t", [128, 2, 4, PQ])
        o_ps = [s.ps(f"o{i}", [128, CH]) for i in range(2)]
        consts, ones_set, cleared = s.sem("consts"), s.sem("ones_set"), s.sem("cleared")
        loaded = [s.sem(f"loaded{i}") for i in range(HPB)]
        v_ready = [s.sem(f"v_ready{i}") for i in range(HPB)]
        stored = [s.sem(f"stored{i}") for i in range(2)]
        scored, maxed, exped, evac_dve, evac_act, summed, o_taken = (
            s.sem(n) for n in ("scored", "maxed", "exped", "evac_dve", "evac_act", "summed", "o_taken"))
        turned = [s.sem(f"turned{x}") for x in range(2)]

        def lead(eng, *sems):
            for x in sems:
                eng.sem_inc(x, LEAD)

        def unit(u):
            pair, v = divmod(u, UP)
            return 2 * pair + v % 2, 2 * (v // 2)

        def evacuate(copy, u, x):
            copy(PT[0:ROWS[0], u % 4, x, 0:2, :], t_ps[0:ROWS[0], x, 0:2, :])
            return copy(PT[0:ROWS[2], u % 4, x, 2, :], t_ps[0:ROWS[2], x, 2, :])

        with s.block() as block:
            @block.sync
            def _(sp):
                def load_pair(r, pair):
                    for e in (2 * pair, 2 * pair + 1):
                        row = r * (HPB * HD) + e * HD
                        for j, part in enumerate((0, 0, 1)):
                            sp.dma_start(Q[e][j * HD:(j + 1) * HD, :],
                                         parts_dram[0][part][bass.ds(row, HD), 0:L]).then_inc(loaded[e], 16)
                        for j, part in enumerate((0, 1, 0)):
                            sp.dma_start(K[e][j * HD:(j + 1) * HD, :],
                                         parts_dram[1][part][bass.ds(row, HD), 0:LK]).then_inc(loaded[e], 16)

                for pair in range(2):
                    load_pair(0, pair)
                sp.dma_start(mask[:], mask_d.rearrange("k q w -> q k w")).then_inc(consts, 16)
                sp.dma_start(eye_b[:], eye_bf_d[0:PQ, 0:PQ]).then_inc(consts, 16)
                with sp.Fori(0, B * JB) as i:
                    for pair in range(2):
                        sp.wait_ge(scored, i * U + (pair + 1) * UP + LEAD)
                        load_pair((i + 1) % (B * JB), pair)
                        sp.wait_ge(o_taken, i * NQ + (pair + 1) * QP + LEAD)
                        for g in range(4):
                            e, x = 2 * pair + g // 2, g % 2
                            for dst, at, n in ((o_dram[bass.ds(i * (HPB * HD) + e * HD, HD), :], 0, HD),
                                               (sum_dram[bass.ds(i * HPB + e, 1), :], HD, 1)):
                                sp.dma_start(dst.rearrange("r (q x t) -> r q x t", x=2, t=PQ)[:, :, x, :],
                                             OS[pair][32 * g + at:32 * g + at + n, :, :]).then_inc(stored[pair], 16)
                for x in stored:
                    sp.wait_ge(x, STORES * B * JB + 1)
                for x in loaded:
                    sp.wait_ge(x, LOADS * (B * JB + 1))

            @block.gpsimd
            def _(pool):
                for e in range(HPB):
                    pool.memset(VH[e][:, :, :, HD:VO], 1.0).then_inc(ones_set, 1)
                with pool.Fori(0, B) as b:
                    with pool.Fori(0, JB) as j:
                        i = pool.snap(b * JB + j)
                        for e in range(HPB):
                            pool.wait_ge(summed, i * NQ + (e // 2 + 1) * QP + LEAD - NQ)
                            for c, rows in enumerate(ROWS):
                                pool.wait_ge(ones_set, HPB)
                                pool.tensor_copy(VH[e][0:rows, :, c, 0:HD].unsqueeze(2),
                                                 V[0:rows, bass.ds(b * NPT, NPT), c, bass.ds(j * HPB + e, 1), :])\
                                    .then_inc(v_ready[e], 1)

            @block.tensor
            def _(pe):
                lead(pe, scored, summed, *turned)
                pe.wait_ge(consts, 32)
                pe.wait_ge(cleared, 2)

                def scores(i, u):
                    e, p0 = unit(u)
                    if u % UP < 2:
                        pe.wait_ge(loaded[e], i * LOADS + LOADS)
                    pe.wait_ge(exped, i * U + u + LEAD - 1)
                    for x in range(2):
                        (qr, qc), (kr, kc), kind = window_of(p0 + x)
                        out = s_ps[u % 2]
                        q = Q[e][:, (p0 + x) * PQ:(p0 + x + 1) * PQ]
                        k = image_of(K[e][:, 0:L])[:, kr:kr + KH, kc:kc + KW]
                        pe.matmul(out[:, x, 0:WKR], eye_b[:], mask[:, kind, :], start=True, stop=False)
                        pe.matmul(out[:, x, 0:WK].rearrange("p (h w) -> p h w", w=KW), q, k, start=False, stop=False)
                        mm = pe.matmul(out[:, x, WK:WKR], q, K[e][:, L:LK], start=False, stop=True)
                    mm.then_inc(scored, 1)

                def turn(i, u):
                    pe.wait_ge(exped, i * U + u + 1 + LEAD)
                    for x, evacuated in enumerate((evac_dve, evac_act)):
                        pe.wait_ge(evacuated, i * U + u + LEAD)
                        for c, (r0, _) in enumerate(CUTS):
                            mm = pe.transpose(t_ps[0:ROWS[c], x, c, :], P[:, u % 2, x, r0 * KW:r0 * KW + ROWS[c]],
                                              eye[0:PQ, 0:PQ])
                        mm.then_inc(turned[x], 1)

                def values(i, n):
                    pe.wait_ge(evac_dve, i * U + 2 * n + 2 + LEAD)
                    pe.wait_ge(evac_act, i * U + 2 * n + 2 + LEAD)
                    pe.wait_ge(o_taken, i * NQ + n - 1 + LEAD)
                    for c in range(len(CUTS)):
                        for g in range(4):
                            u, x = 2 * n + g // 2, g % 2
                            e, p0 = unit(u)
                            if n % QP == 0 and c == 0:
                                pe.wait_ge(v_ready[e], (i + 1) * len(CUTS))
                            mm = pe.matmul(o_ps[n % 2][32 * g:32 * g + VO, 0:PQ], VH[e][0:ROWS[c], p0 + x, c, :],
                                           PT[0:ROWS[c], u % 4, x, c, :], start=c == 0, stop=c == len(CUTS) - 1)
                    mm.then_inc(summed, 1)

                with pe.Fori(0, B * JB) as i:
                    scores(i, 0)
                    for u in range(U + 1):
                        if u + 1 < U:
                            scores(i, u + 1)
                        if u % 2 == 0 and u >= 2:
                            values(i, u // 2 - 1)
                        if u < U:
                            turn(i, u)

            @block.vector
            def _(dve):
                for x in o_ps:
                    dve.memset(x[:], 0.0).then_inc(cleared, 1)
                lead(dve, maxed, evac_dve, o_taken)
                for x in stored:
                    dve.sem_inc(x, 1)

                def top(i, u):
                    dve.wait_ge(scored, i * U + u + 1 + LEAD)
                    dve.wait_ge(exped, i * U + u + LEAD - 1)
                    dve.tensor_reduce(nmax[:, u % 2, :], s_ps[u % 2][:, :, 0:WKR], AX_X, ALU.max,
                                      negate=True).then_inc(maxed, 1)

                def take(i, u):
                    dve.wait_ge(turned[0], i * U + u + 1 + LEAD)
                    dve.wait_ge(summed, i * NQ + u // 2 - 1 + LEAD)
                    evacuate(dve.tensor_copy, u, 0).then_inc(evac_dve, 1)

                def take_quad(i, n):
                    if n % QP == 0:
                        dve.wait_ge(stored[n // QP], i * STORES + 1)
                    dve.wait_ge(summed, i * NQ + n + 1 + LEAD)
                    dve.tensor_copy(OS[n // QP][:, n % QP, :], o_ps[n % 2][:, 0:PQ]).then_inc(o_taken, 1)

                with dve.Fori(0, B * JB) as i:
                    for u in range(U + 2):
                        if u < U:
                            top(i, u)
                        if u % 2 == 1 and u >= 3:
                            take_quad(i, (u - 3) // 2)
                        if 1 <= u <= U:
                            take(i, u - 1)

            @block.scalar
            def _(act):
                lead(act, exped, evac_act)

                def exps(i, u):
                    act.wait_ge(maxed, i * U + u + 1 + LEAD)
                    for x in turned:
                        act.wait_ge(x, i * U + u + LEAD - 1)
                    for x in range(2):
                        last = act.activation(P[:, u % 2, x, :], s_ps[u % 2][:, x, 0:WKR], ACT.Exp,
                                              bias=nmax[:, u % 2, x:x + 1])
                    last.then_inc(exped, 1)

                def take(i, u):
                    act.wait_ge(turned[1], i * U + u + 1 + LEAD)
                    act.wait_ge(summed, i * NQ + u // 2 - 1 + LEAD)
                    evacuate(lambda o, p: act.activation(o, p, ACT.Copy), u, 1).then_inc(evac_act, 1)

                with act.Fori(0, B * JB) as i:
                    for u in range(U + 1):
                        if u < U:
                            exps(i, u)
                        if u >= 1:
                            take(i, u - 1)


def ssm_conv(nc, name, XN, t, pre, U, UT, z_dram):
    PADW = W + 2
    STRIP = PH * W
    with Scope(nc, name) as s:
        w_sb = s.sb("w", [CP, CC, 2 * DI])
        cw = s.sb("cw", [DI, 9])
        cb = s.sb("cb", [DI, 1])
        pad = s.sb("pad", [DI, B, H + 2, PADW])
        z = s.sb("z", [DI, 2, STRIP])
        conv = s.sb("conv", [DI, B, L])
        e = s.sb("e", [DI, B, L])
        acc = [s.ps(f"acc{i}", [DI, CH]) for i in range(4)]
        loaded, padded, ready, placed, z_moved, z_stored0, z_stored1 = (
            s.sem(n) for n in ("loaded", "padded", "ready", "placed", "z_moved", "z_stored0", "z_stored1"))
        z_stored = (z_stored0, z_stored1)
        convolved, own, exped, gated, turned = (s.sem(n) for n in ("convolved", "own", "exped", "gated", "turned"))
        strips = [(b, r) for b in range(B) for r in range(0, H, PH)]
        n_s = len(strips)
        with s.block() as block:
            @block.sync
            def _(sp):
                sp.dma_start(w_sb[:], t[pre + "in_wT"].rearrange("(k p) n -> p k n", p=CP)).then_inc(loaded, 16)
                sp.dma_start(cw[:], t[pre + "conv_w"]).then_inc(loaded, 16)
                sp.dma_start(cb[:], t[pre + "conv_b"]).then_inc(loaded, 16)
                for n, (b, r) in enumerate(strips):
                    sp.wait_ge(z_moved, n + 1)
                    at = b * L + r * W
                    sp.dma_start(z_dram[:, at:at + STRIP], z[:, n % 2, :]).then_inc(z_stored[n % 2], 16)
                for x in z_stored:
                    sp.wait_ge(x, 16 * n_s // 2)

            @block.tensor
            def _(pe):
                pe.wait_ge(loaded, 48)
                for n, (b, r) in enumerate(strips):
                    if n >= 2:
                        pe.wait_ge(placed, n - 1)
                        pe.wait_ge(z_moved, n - 1)
                    at = b * L + r * W
                    for half in range(2):
                        for k in range(CC):
                            mm = pe.matmul(acc[2 * (n % 2) + half][:, 0:STRIP], w_sb[:, k, half * DI:(half + 1) * DI],
                                           XN[:, k, at:at + STRIP], start=k == 0, stop=k == CC - 1)
                        mm.then_inc(ready, 1)

            @block.gpsimd
            def _(pool):
                pool.memset(pad[:], 0.0).then_inc(padded, 1)

            @block.scalar
            def _(act):
                act.wait_ge(padded, 1)
                for n, (b, r) in enumerate(strips):
                    act.wait_ge(ready, 2 * n + 1)
                    act.activation(pad[:, b, 1 + r:1 + r + PH, 1:1 + W],
                                   acc[2 * (n % 2)][:, 0:STRIP].rearrange("p (h w) -> p h w", w=W), ACT.Copy)\
                       .then_inc(placed, 1)
                    act.wait_ge(ready, 2 * n + 2)
                    if n >= 2:
                        act.wait_ge(z_stored[n % 2], 16 * (n // 2))
                    act.activation(z[:, n % 2, :], acc[2 * (n % 2) + 1][:, 0:STRIP], ACT.Copy).then_inc(z_moved, 1)
                for b in range(B):
                    act.wait_ge(convolved, b + 1)
                    act.activation(e[:, b, :], conv[:, b, :], ACT.Exp, scale=-1.0).then_inc(exped, 1)
                for b in range(B):
                    act.wait_ge(gated, b + 1)
                    act.activation(image_of(UT[:, b, :]), U[:, b, :].rearrange("p (h w) -> p w h", w=W), ACT.Copy)\
                       .then_inc(turned, 1)
                act.wait_ge(turned, B)

            @block.vector
            def _(dve):
                link = Chain(dve, own)
                dve.wait_ge(loaded, 48)
                for b in range(B):
                    dve.wait_ge(placed, n_s // B * (b + 1))
                    c = image_of(conv[:, b, :])
                    for k in range(9):
                        src = pad[:, b, k // 3:k // 3 + H, k % 3:k % 3 + W]
                        if k == 0:
                            link(dve.tensor_scalar(c, src, cw[:, 0:1], cb[:, 0:1], ALU.mult, ALU.add))
                        else:
                            link(dve.scalar_tensor_tensor(c, src, cw[:, k:k + 1], c, ALU.mult, ALU.add))
                    dve.sem_inc(convolved, 1)
                for b in range(B):
                    dve.wait_ge(exped, b + 1)
                    link(dve.tensor_scalar(e[:, b, :], e[:, b, :], 1.0, None, ALU.add))
                    link(dve.reciprocal(e[:, b, :], e[:, b, :]))
                    dve.tensor_tensor(U[:, b, :], conv[:, b, :], e[:, b, :], ALU.mult).then_inc(gated, 1)
                dve.wait_ge(gated, B)


def ssm_prepare(nc, name, t, pre, U, UT, dt_dram, du_dram, bc_dram, skip_dram):
    LEAD = 4
    XR = 80
    with Scope(nc, name) as s:
        wx = s.sb("wx", [DI, ND, CP])
        wdt = s.sb("wdt", [DT_R, ND, DI])
        bdt = s.sb("bdt", [DI, ND])
        Dk = s.sb("dk", [DI, ND])
        dsum = s.sb("dsum", [DI, 1])
        skip = s.sb("skip", [DI, L])
        XD = s.sb("xd", [CP, 2, L])
        T = s.sb("t", [DI, 2, L])
        E = s.sb("e", [DI, 2, L])
        Wb = s.sb("wb", [DI, 2, L])
        parts = {k: s.sb(f"parts_{k}", [CP, 3, L], BF16) for k in ("x", "t", "u")}
        xd_ps = [s.ps(f"xd{i}", [CP, CH]) for i in range(4)]
        dt_ps = [s.ps(f"dt{i}", [DI, CH]) for i in range(4)]
        loaded = s.sem("loaded")
        xd_made, xd_taken, dt_made, dt_taken = (s.sem(n) for n in ("xd_made", "xd_taken", "dt_made", "dt_taken"))
        absed, exped, plus1, delta, logged, softed, dt_done, du_done, dt_held = (
            s.sem(n) for n in ("absed", "exped", "plus1", "delta", "logged", "softed", "dt_done", "du_done",
                               "dt_held"))
        hi = {k: s.sem(f"hi_{k}") for k in parts}
        rest = {k: s.sem(f"rest_{k}") for k in parts}
        mid = {k: s.sem(f"mid_{k}") for k in parts}
        low = {k: s.sem(f"low_{k}") for k in parts}
        stored = {k: s.sem(f"stored_{k}") for k in parts}
        skipped, skip_stored, skip_own = s.sem("skipped"), s.sem("skip_stored"), s.sem("skip_own")
        own_rows = {"x": XR, "t": DI, "u": DI}
        STORES = {"x": 2 * 16, "t": 9 * 16, "u": 9 * 16}

        def lead(eng, *sems):
            for x in sems:
                eng.sem_inc(x, LEAD)

        def whole(k, n):
            return {"x": XD, "t": T, "u": E}[k][0:own_rows[k], n % 2, :]

        SPLITS = ("x", "u", "t")

        PRODUCTS = [("xd", c) for c in range(4)] + [("dt", 0), ("xd", 4)] + [("dt", c) for c in range(1, 5)]

        def source(k, b):
            return (UT if k % 2 else U)[:, bass.ds(b, 1), :]

        with s.block() as block:
            @block.sync
            def _(sp):
                sp.dma_start(wx[:], t[pre + "xwT"].rearrange("k p n -> p k n")).then_inc(loaded, 16)
                sp.dma_start(wdt[:], t[pre + "dtwT"].rearrange("k p n -> p k n")).then_inc(loaded, 16)
                sp.dma_start(bdt[:], t[pre + "dtb"]).then_inc(loaded, 16)
                sp.dma_start(Dk[:], t[pre + "D"]).then_inc(loaded, 16)
                with sp.Fori(0, B) as b:
                    sp.wait_ge(skipped, b + 1 + LEAD)
                    sp.dma_start(skip_dram[bass.ds(b, 1), :, :].rearrange("a p l -> (a p) l"), skip[:])\
                      .then_inc(skip_stored, 16)
                    for k in range(ND):
                        n = b * ND + k
                        at = b * ND + (k % 2) * 2 + k // 2
                        sp.wait_ge(low["x"], n + 1 + LEAD)
                        for j, row in enumerate((32, 64)):
                            sp.dma_start(bc_dram[bass.ds(at * 2 + j, 1), :, :, :].rearrange("a c n l -> (a n) c l"),
                                         parts["x"][row:row + NS, :, :]).then_inc(stored["x"], 16)
                        for w, d in (("u", du_dram), ("t", dt_dram)):
                            sp.wait_ge(low[w], n + 1 + LEAD)
                            for c in range(3):
                                for tl in range(3):
                                    dst = d[bass.ds(at, 1), :, c, :, tl, :].rearrange("a g c l -> (a g) c l")
                                    sp.dma_start(dst, parts[w][tl * 32:(tl + 1) * 32, c, :]).then_inc(stored[w], 16)
                for w in parts:
                    sp.wait_ge(stored[w], STORES[w] * B * ND + 1)
                sp.wait_ge(skip_stored, 16 * B + 1)

            @block.tensor
            def _(pe):
                pe.wait_ge(loaded, 64)
                lead(pe, xd_made, dt_made)
                with pe.Fori(0, B) as b:
                    for k in range(ND):
                        n = b * ND + k
                        for what, c in PRODUCTS:
                            m = n * len(LCH) + c
                            bank = (k * len(LCH) + c) % 4
                            at, w = LCH[c]
                            if what == "xd":
                                pe.wait_ge(xd_taken, m + LEAD - 3)
                                pe.matmul(xd_ps[bank][:, 0:w], wx[:, k, :], source(k, b)[:, :, at:at + w],
                                          start=True, stop=True).then_inc(xd_made, 1)
                            else:
                                pe.wait_ge(xd_taken, m + 1 + LEAD)
                                pe.wait_ge(dt_taken, m + LEAD - 3)
                                pe.matmul(dt_ps[bank][:, 0:w], wdt[:, k, :], XD[0:DT_R, k % 2, at:at + w],
                                          start=True, stop=True).then_inc(dt_made, 1)

            @block.scalar
            def _(act):
                act.wait_ge(loaded, 64)
                lead(act, xd_taken, dt_taken, absed, exped, logged, *hi.values(), *mid.values())
                for x in stored.values():
                    act.sem_inc(x, 1)

                def project(b, k):
                    n = b * ND + k
                    act.wait_ge(low["x"], n + LEAD - 1)
                    for c in range(len(LCH) + 1):
                        m = n * len(LCH) + c
                        if c < len(LCH):
                            at, w = LCH[c]
                            act.wait_ge(xd_made, m + 1 + LEAD)
                            act.activation(XD[:, k % 2, at:at + w], xd_ps[(k * len(LCH) + c) % 4][:, 0:w], ACT.Copy)\
                               .then_inc(xd_taken, 1)
                        if c >= 1:
                            at, w = LCH[c - 1]
                            if c == 1:
                                act.wait_ge(low["t"], n + LEAD - 1)
                            act.wait_ge(dt_made, m + LEAD)
                            act.activation(T[:, k % 2, at:at + w], dt_ps[(k * len(LCH) + c - 1) % 4][:, 0:w], ACT.Identity,
                                           bias=bdt[:, k:k + 1]).then_inc(dt_taken, 1)

                def soften(b, k):
                    n = b * ND + k
                    act.wait_ge(low["u"], n + LEAD - 1)
                    act.wait_ge(dt_taken, (n + 1) * len(LCH) + LEAD)
                    act.activation(E[:, k % 2, :], T[:, k % 2, :], ACT.Abs).then_inc(absed, 1)
                    act.wait_ge(absed, n + 1 + LEAD)
                    act.activation(E[:, k % 2, :], E[:, k % 2, :], ACT.Exp, scale=-1.0).then_inc(exped, 1)

                def take_log(b, k):
                    n = b * ND + k
                    act.wait_ge(delta, n + 1 + LEAD)
                    act.activation(Wb[:, k % 2, :], Wb[:, k % 2, :], ACT.Ln).then_inc(logged, 1)

                def high_parts(b, k):
                    n = b * ND + k
                    for w, done in (("x", None), ("u", du_done), ("t", dt_held)):
                        if done is not None:
                            act.wait_ge(done, n + 1 + LEAD)
                        act.wait_ge(stored[w], n * STORES[w] + 1)
                        r = own_rows[w]
                        act.activation(parts[w][0:r, 0, :], whole(w, k), ACT.Copy).then_inc(hi[w], 1)

                def middle_parts(b, k):
                    n = b * ND + k
                    for w in SPLITS:
                        act.wait_ge(rest[w], n + 1 + LEAD)
                        r = own_rows[w]
                        act.activation(parts[w][0:r, 1, :], whole(w, k), ACT.Copy).then_inc(mid[w], 1)

                with act.Fori(0, B) as b:
                    for k in range(ND + 1):
                        if k < ND:
                            project(b, k)
                            soften(b, k)
                        if k >= 1:
                            high_parts(b, k - 1)
                        if k < ND:
                            take_log(b, k)
                        if k >= 1:
                            middle_parts(b, k - 1)

            @block.vector
            def _(dve):
                dve.wait_ge(loaded, 64)
                lead(dve, plus1, delta, dt_done, skipped, du_done, dt_held, *low.values())
                dve.sem_inc(skip_stored, 1)
                skip_link = Chain(dve, skip_own)
                skip_link(dve.tensor_reduce(dsum[:], Dk[:], AX_X, ALU.add))

                def soften(b, k):
                    n = b * ND + k
                    if k == 0:
                        dve.wait_ge(skip_stored, b * 16 + 1)
                        dve.tensor_scalar(skip[:], U[:, bass.ds(b, 1), :], dsum[:, 0:1], None, ALU.mult)\
                           .then_inc(skipped, 1)
                    dve.wait_ge(exped, n + 1 + LEAD)
                    dve.tensor_scalar(Wb[:, k % 2, :], E[:, k % 2, :], 1.0, None, ALU.add).then_inc(plus1, 1)
                    dve.wait_ge(plus1, n + 1 + LEAD)
                    dve.scalar_tensor_tensor(E[:, k % 2, :], Wb[:, k % 2, :], 1.0, E[:, k % 2, :],
                                             ALU.subtract, ALU.subtract).then_inc(delta, 1)

                def finish(b, k):
                    n = b * ND + k
                    dve.wait_ge(softed, n + 1 + LEAD)
                    dve.scalar_tensor_tensor(T[:, k % 2, :], T[:, k % 2, :], 0.0, Wb[:, k % 2, :],
                                             ALU.max, ALU.add).then_inc(dt_done, 1)
                    dve.wait_ge(dt_done, n + 1 + LEAD)
                    dve.tensor_tensor(E[:, k % 2, :], T[:, k % 2, :],
                                      source(k, b).rearrange("p a l -> p (a l)"), ALU.mult)\
                       .then_inc(du_done, 1)
                    dve.wait_ge(du_done, n + 1 + LEAD)
                    dve.tensor_scalar(T[:, k % 2, :], T[:, k % 2, :], DT_LEAST, None, ALU.max)\
                       .then_inc(dt_held, 1)

                def low_parts(b, k):
                    n = b * ND + k
                    for w in SPLITS:
                        r = own_rows[w]
                        dve.wait_ge(mid[w], n + 1 + LEAD)
                        dve.tensor_tensor(parts[w][0:r, 2, :], whole(w, k), parts[w][0:r, 1, :], ALU.subtract)\
                           .then_inc(low[w], 1)

                with dve.Fori(0, B) as b:
                    for k in range(ND + 1):
                        if k < ND:
                            soften(b, k)
                        if k >= 1:
                            low_parts(b, k - 1)
                        if k < ND:
                            finish(b, k)

            @block.gpsimd
            def _(pool):
                lead(pool, softed, *rest.values())

                def soften(b, k):
                    n = b * ND + k
                    pool.wait_ge(logged, n + 1 + LEAD)
                    pool.tensor_tensor(Wb[:, k % 2, :], Wb[:, k % 2, :], E[:, k % 2, :], ALU.subtract)\
                        .then_inc(softed, 1)

                def rests(b, k, which):
                    n = b * ND + k
                    for w in which:
                        r = own_rows[w]
                        pool.wait_ge(hi[w], n + 1 + LEAD)
                        pool.tensor_tensor(whole(w, k), whole(w, k), parts[w][0:r, 0, :], ALU.subtract)\
                            .then_inc(rest[w], 1)

                with pool.Fori(0, B) as b:
                    for k in range(ND + 1):
                        if k >= 1:
                            rests(b, k - 1, SPLITS)
                        if k < ND:
                            soften(b, k)


def ssm_scan(nc, name, t, pre, dt_dram, du_dram, bc_dram, y_dram):
    LEAD = 16
    NG, NT = 4, 3
    UN = 2 * NG * NT
    CW = 10 * W
    CHK = [(at, min(CW, L - at)) for at in range(0, L, CW)]
    NK = len(CHK)
    NB = 6
    with Scope(nc, name) as s:
        E4 = s.sb("e4", [128, 128], BF16)
        EN = s.sb("en", [3 * NS, 128], BF16)
        SUM = s.sb("sum", [128, NG, 32])
        A = s.sb("a", [128, ND * NG * NT])
        AO = s.sb("ao", [128, 2 * NG * NT])
        DT = s.sb("dt", [128, NT, L], BF16)
        DU = s.sb("du", [128, NT, L], BF16)
        BC = s.sb("bc", [3 * NS, 2, L], BF16)
        REP = [[s.sb(f"rep{d}{j}", [128, L]) for j in range(2)] for d in range(2)]
        dA = s.sb("da", [128, 2, L])
        S = s.sb("s", [128, NB, L])
        ystage = s.sb("ystage", [DI, L])
        ring = [s.ps(f"ring{i}", [128, CH]) for i in range(3)]
        y_ps = s.ps("y", [DI, NK, CH])
        consts = s.sem("consts")
        loaded = [s.sem(f"loaded{g}") for g in range(NG)]
        bc_loaded, cleared = s.sem("bc_loaded"), s.sem("cleared")
        a_capped, a_exped, a_turned = s.sem("a_capped"), s.sem("a_exped"), s.sem("a_turned")
        restored, act_took, dve_took = (s.sem(n) for n in ("restored", "act_took", "dve_took"))
        scanned, weighted, summed, y_taken, y_stored = (
            s.sem(n) for n in ("scanned", "weighted", "summed", "y_taken", "y_stored"))

        BC_FROM = 2
        uses = []
        for n in range(UN):
            d, x = divmod(n, NG * NT)
            uses += [("dt", d, n, c) for c in range(NK)] + [("du", d, n, c) for c in range(NK)]
            if BC_FROM <= x < BC_FROM + 2 * NK:
                uses.append(("bc", 1 - d) + divmod(x - BC_FROM, NK))
        ahead = [(j, c) for j in range(2) for c in range(NK)]
        sum_places = {(4, ("du", 4)): 0, (5, ("dt", 1)): 1, (5, ("dt", 4)): 2, (5, ("du", 1)): 3, (5, ("du", 4)): 4}
        index = {u: r for r, u in enumerate(uses)}
        of_act = [u[0] != "du" for u in uses]
        PER_A, PER_V, R = sum(of_act), len(uses) - sum(of_act), len(uses)
        START = {restored: R - len(ahead), weighted: UN, act_took: LEAD - len(ahead)}

        def taken_by(r):
            a = sum(of_act[:r + 1])
            return a, r + 1 - a

        def place(n):
            d, x = divmod(n, NG * NT)
            return d, x // NT, x % NT

        def lead(eng, *sems):
            for x in sems:
                eng.sem_inc(x, START.get(x, LEAD))

        def way(ap, d):
            return ap[:, ::-1] if d else ap

        with s.block() as block:
            @block.sync
            def _(sp):
                sp.dma_start(E4[:], t["e4"]).then_inc(consts, 16)
                sp.dma_start(EN[:], t["en"]).then_inc(consts, 16)
                sp.dma_start(SUM[:], t["state_sum"]).then_inc(consts, 16)
                sp.dma_start(A[:], t[pre + "A"]).then_inc(consts, 16)

                def load_bc(at):
                    for j in range(2):
                        sp.dma_start(BC[:, j, :], bc_dram[bass.ds(at * 2 + j, 1), :, :, :]
                                     .rearrange("a c n l -> (a c n) l")).then_inc(bc_loaded, 16)

                def store_y(i):
                    sp.wait_ge(y_taken, i * NK + NK + LEAD)
                    sp.dma_start(y_dram[bass.ds(i, 1), :, :].rearrange("a p l -> (a p) l"), ystage[:])\
                      .then_inc(y_stored, 16)

                load_bc(0)
                with sp.Fori(0, B * 2) as i:
                    for d in range(2):
                        at = i * 2 + d
                        for g in range(NG):
                            n = ((1 - d) * NG + g + 1) * NT - 1
                            before = index["du", 1 - d, n, NK - 1] + 1 + (R if d else 0)
                            sp.wait_ge(restored, i * R + before)
                            for dst, src in ((DT, dt_dram), (DU, du_dram)):
                                sp.dma_start(dst[32 * g:32 * g + 24, :, :].rearrange("p t l -> p (t l)"),
                                             src[bass.ds(at, 1), g, :, :, :, :].rearrange("a c e t l -> (a c e) (t l)"))\
                                  .then_inc(loaded[g], 16)
                        sp.wait_ge(restored, i * R + R + (index["bc", 1, 1, NK - 1] + 1 if d else 0))
                        load_bc((at + 1) % (B * ND))
                        if d == 0:
                            store_y(i)
                store_y(B * 2)
                sp.wait_ge(y_stored, 16 * (B * 2 + 1) + 1)
                sp.wait_ge(bc_loaded, 32 * (B * ND + 1))

            @block.tensor
            def _(pe):
                pe.wait_ge(consts, 64)
                lead(pe, restored, summed)

                def restore(i, use):
                    r = index[use]
                    kind, d, n, c = use
                    at, w = CHK[c]
                    back = r - 3
                    if back >= 0:
                        a, v = taken_by(back)
                        if of_act[back]:
                            pe.wait_ge(act_took, i * PER_A + a + LEAD)
                        else:
                            pe.wait_ge(dve_took, i * PER_V + v + LEAD)
                    elif r == 0:
                        pe.wait_ge(act_took, i * PER_A + LEAD)
                        pe.wait_ge(dve_took, i * PER_V + LEAD)
                    out = ring[r % 3][:, 0:w]
                    if kind == "bc":
                        mm = pe.matmul(out, EN[:], BC[:, n, at:at + w], start=True, stop=True)
                    else:
                        _, g, tl = place(n)
                        src = DT if kind == "dt" else DU
                        mm = pe.matmul(out, E4[32 * g:32 * g + 24, :], src[32 * g:32 * g + 24, tl, at:at + w],
                                       start=True, stop=True)
                    mm.then_inc(restored, 1)

                def sum_states(i, q, c):
                    at, w = CHK[c]
                    if c == 0:
                        pe.wait_ge(weighted, i * UN + (q + 1) * NT + UN)
                    if q == 0:
                        pe.wait_ge(y_taken, i * NK + c + 1 + LEAD)
                    for tl in range(NT):
                        mm = pe.matmul(y_ps[32 * tl:32 * tl + 32, c, 0:w], SUM[:, q % NG, :],
                                       S[:, (q * NT + tl) % NB, at:at + w],
                                       start=q == 0, stop=q % (2 * NG) == 2 * NG - 1)
                    if c == NK - 1:
                        mm.then_inc(summed, 1)

                pe.wait_ge(cleared, 1)
                for c, (at, w) in enumerate(CHK):
                    for tl in range(NT):
                        pe.matmul(y_ps[32 * tl:32 * tl + 32, c, 0:w], SUM[:, 0, :], S[:, NB - NT, at:at + w],
                                  start=True, stop=False)
                pe.wait_ge(bc_loaded, 32)
                for p, (j, c) in enumerate(ahead):
                    if p >= 3:
                        pe.wait_ge(act_took, p - 2 + LEAD - len(ahead))
                    at, w = CHK[c]
                    pe.matmul(ring[p % 3][:, 0:w], EN[:], BC[:, j, at:at + w], start=True, stop=True)\
                      .then_inc(restored, 1)
                with pe.Fori(0, B * 2) as i:
                    for use in uses:
                        kind, d, n, c = use
                        if kind == "bc":
                            if (n, c) == (0, 0):
                                pe.wait_ge(bc_loaded, (i * 2 + (1 - d) + 2) * 32)
                            restore(i, use)
                            continue
                        if kind == "dt" and c == 0 and n % NT == 0:
                            pe.wait_ge(loaded[place(n)[1]], (i * 2 + d + 1) * 32)
                        restore(i, use)
                        for (off, after), chunk in sum_places.items():
                            if after == (kind, c) and (n - off) % NT == 0:
                                q = (n - off) // NT
                                if q >= -1:
                                    sum_states(i, q, chunk)
                for c in range(NK):
                    sum_states(B * 2, -1, c)

            @block.scalar
            def _(act):
                act.wait_ge(a_capped, 1)
                lead(act, act_took, y_taken)
                act.sem_inc(y_stored, 1)
                act.activation(A[:], A[:], ACT.Exp).then_inc(a_exped, 1)

                def take_y(chunks):
                    for c in chunks:
                        at, w = CHK[c]
                        act.activation(ystage[:, at:at + w], y_ps[:, c, 0:w], ACT.Copy).then_inc(y_taken, 1)

                for p, (j, c) in enumerate(ahead):
                    at, w = CHK[c]
                    act.wait_ge(restored, R - len(ahead) + p + 1)
                    act.activation(REP[0][j][:, at:at + w], ring[p % 3][:, 0:w], ACT.Copy).then_inc(act_took, 1)
                with act.Fori(0, B) as b:
                    with act.Fori(0, 2) as o:
                        i = act.snap(b * 2 + o)
                        act.wait_ge(act_took, i * PER_A + LEAD)
                        act.wait_ge(a_turned, 1)
                        act.activation(AO[:], A[:, bass.ds(o * UN, UN)], ACT.Copy).then_inc(a_exped, 1)
                        act.wait_ge(a_exped, i + 2)
                        for r, (kind, d, n, c) in enumerate(uses):
                            if kind == "du":
                                continue
                            at, w = CHK[c]
                            src = ring[r % 3][:, 0:w]
                            act.wait_ge(restored, i * R + r + 1 + R)
                            if kind == "bc":
                                if n == 0 and c == 0:
                                    act.wait_ge(weighted, i * UN + UN + (0 if d else NG * NT))
                                act.activation(REP[d][n][:, at:at + w], src, ACT.Copy).then_inc(act_took, 1)
                            else:
                                if c == 0:
                                    act.wait_ge(scanned, i * UN + n - 1 + LEAD)
                                act.activation(dA[:, n % 2, at:at + w], src, ACT.Exp, scale=AO[:, n:n + 1])\
                                   .then_inc(act_took, 1)
                                if c == NK - 1 and n == 3:
                                    act.wait_ge(summed, i * 2 * NG + 1 + LEAD)
                                    act.wait_ge(y_stored, i * 16 + 1)
                                    take_y(range(0, 3))
                                if c == NK - 1 and n == 4:
                                    take_y(range(3, NK))
                act.wait_ge(summed, B * 2 * 2 * NG + 1 + LEAD)
                act.wait_ge(y_stored, B * 2 * 16 + 1)
                take_y(range(NK))

            @block.vector
            def _(dve):
                lead(dve, dve_took, scanned)
                dve.memset(S[:, NB - NT:NB, :], 0.0).then_inc(cleared, 1)
                dve.wait_ge(cleared, 1)
                dve.wait_ge(consts, 64)
                dve.tensor_scalar(A[:], A[:], 88.0, None, ALU.min).then_inc(a_capped, 1)
                dve.wait_ge(a_exped, 1)
                dve.tensor_scalar(A[:], A[:], A_MOST, -1.0, ALU.min, ALU.mult).then_inc(a_turned, 1)
                with dve.Fori(0, B * 2) as i:
                    for n in range(UN):
                        d, g, tl = place(n)
                        if n % (NG * NT) == 0:
                            a = taken_by(index["bc", 1, 1, NK - 1])[0] if d else 0
                            dve.wait_ge(act_took, i * PER_A + a + LEAD)
                        dve.wait_ge(summed, i * 2 * NG + n // NT + LEAD)
                        for c, (at, w) in enumerate(CHK):
                            r = index["du", d, n, c]
                            dve.wait_ge(restored, i * R + r + 1 + R)
                            dve.tensor_tensor(S[:, n % NB, at:at + w], ring[r % 3][:, 0:w],
                                              REP[d][0][:, at:at + w], ALU.mult).then_inc(dve_took, 1)
                        a, v = taken_by(index["du", d, n, NK - 1])
                        dve.wait_ge(act_took, i * PER_A + a + LEAD)
                        dve.wait_ge(dve_took, i * PER_V + v + LEAD)
                        dve.tensor_tensor_scan(way(S[:, n % NB, :], d), way(dA[:, n % 2, :], d),
                                               way(S[:, n % NB, :], d), 0.0, ALU.mult, ALU.add)\
                           .then_inc(scanned, 1)

            @block.gpsimd
            def _(pool):
                lead(pool, weighted)
                with pool.Fori(0, B * 2) as i:
                    for n in range(UN):
                        d, _, _ = place(n)
                        pool.wait_ge(scanned, i * UN + n + 1 + LEAD)
                        pool.tensor_tensor(S[:, n % NB, :], S[:, n % NB, :], REP[d][1][:], ALU.mult)\
                            .then_inc(weighted, 1)


def ssm_gate(nc, name, t, pre, ones_mean, y_dram, skip_dram, z_dram, YG):
    with Scope(nc, name) as s:
        y = s.sb("y", [DI, B, L])
        yt = s.sb("yt", [DI, B, L])
        sk = s.sb("sk", [DI, B, L])
        z = s.sb("z", [DI, B, L])
        g = s.sb("g", [DI, 1])
        bb = s.sb("b", [DI, 1])
        acc = [s.ps(f"acc{i}", [DI, CH]) for i in range(4)]
        var_ps = [s.ps(f"var{i}", [DI, CH]) for i in range(4)]
        loaded = [s.sem(f"loaded{b}") for b in range(B)]
        consts, zlink = s.sem("consts"), s.sem("zlink")
        joined, meaned, centred, squared, varied, eps_added, rooted, normed, scaled, zexp, zgate, done, own = (
            s.sem(n) for n in ("joined", "meaned", "centred", "squared", "varied", "eps_added", "rooted",
                               "normed", "scaled", "zexp", "zgate", "done", "own"))
        jobs = [(b, at, w) for b in range(B) for at, w in LCH]
        NJ = len(LCH)
        with s.block() as block:
            @block.sync
            def _(sp):
                for b in range(B):
                    for dst, src in ((y, y_dram[2 * b + 1]), (yt, y_dram[2 * b + 2]), (sk, skip_dram[b]),
                                     (z, z_dram[:, b * L:(b + 1) * L])):
                        sp.dma_start(dst[:, b, :], src).then_inc(loaded[b], 16)
                sp.dma_start(g[:], t[pre + "norm_g"]).then_inc(consts, 16)
                sp.dma_start(bb[:], t[pre + "norm_b"]).then_inc(consts, 16)

            @block.gpsimd
            def _(pool):
                for b in range(B):
                    pool.wait_ge(loaded[b], 64)
                    pool.tensor_tensor(y[:, b, :], y[:, b, :], sk[:, b, :], ALU.add).then_inc(own, 1)
                for b in range(B):
                    pool.wait_ge(zexp, b + 1)
                    pool.wait_ge(scaled, NJ * (b + 1))
                    pool.wait_ge(zgate, b + 1)
                    pool.tensor_tensor(YG[:, 0, b * L:(b + 1) * L], yt[:, b, :], z[:, b, :], ALU.mult).then_inc(done, 1)
                pool.wait_ge(done, B)

            @block.tensor
            def _(pe):
                for n, (b, at, w) in enumerate(jobs):
                    pe.wait_ge(joined, b + 1)
                    if n >= 4:
                        pe.wait_ge(centred, n - 3)
                    pe.matmul(acc[n % 4][:, 0:w], ones_mean[:], y[:, b, at:at + w], start=True, stop=True)\
                      .then_inc(meaned, 1)
                for n, (b, at, w) in enumerate(jobs):
                    pe.wait_ge(squared, n + 1)
                    if n >= 4:
                        pe.wait_ge(eps_added, n - 3)
                    pe.matmul(var_ps[n % 4][:, 0:w], ones_mean[:], yt[:, b, at:at + w], start=True, stop=True)\
                      .then_inc(varied, 1)

            @block.scalar
            def _(act):
                act.wait_ge(consts, 32)
                for b in range(B):
                    act.wait_ge(loaded[b], 64)
                    act.wait_ge(own, b + 1)
                    act.activation(sk[:, b, :], z[:, b, :], ACT.Exp, scale=-1.0).then_inc(zexp, 1)
                for n, (b, at, w) in enumerate(jobs):
                    act.wait_ge(centred, n + 1)
                    act.activation(yt[:, b, at:at + w], y[:, b, at:at + w], ACT.Square).then_inc(squared, 1)
                for n, (b, at, w) in enumerate(jobs):
                    act.wait_ge(eps_added, n + 1)
                    act.activation(yt[:, b, at:at + w], yt[:, b, at:at + w], ACT.Ln).then_inc(rooted, 1)
                    act.wait_ge(rooted, 2 * n + 1)
                    act.activation(yt[:, b, at:at + w], yt[:, b, at:at + w], ACT.Exp, scale=-0.5).then_inc(rooted, 1)
                for n, (b, at, w) in enumerate(jobs):
                    act.wait_ge(normed, n + 1)
                    act.activation(yt[:, b, at:at + w], y[:, b, at:at + w], ACT.Identity, scale=g[:, 0:1],
                                   bias=bb[:, 0:1]).then_inc(scaled, 1)

            @block.vector
            def _(dve):
                for b in range(B):
                    dve.wait_ge(own, b + 1)
                    dve.tensor_tensor(image_of(y[:, b, :]), image_of(y[:, b, :]),
                                      yt[:, b, :].rearrange("p (w h) -> p h w", h=H), ALU.add).then_inc(joined, 1)
                for n, (b, at, w) in enumerate(jobs):
                    dve.wait_ge(meaned, n + 1)
                    dve.tensor_tensor(y[:, b, at:at + w], y[:, b, at:at + w], acc[n % 4][:, 0:w], ALU.subtract)\
                       .then_inc(centred, 1)
                for b in range(B):
                    dve.wait_ge(zexp, b + 1)
                    link = Chain(dve, zlink, 2 * b)
                    link(dve.tensor_scalar(sk[:, b, :], sk[:, b, :], 1.0, None, ALU.add))
                    link(dve.reciprocal(sk[:, b, :], sk[:, b, :]))
                    dve.tensor_tensor(z[:, b, :], z[:, b, :], sk[:, b, :], ALU.mult).then_inc(zgate, 1)
                for n, (b, at, w) in enumerate(jobs):
                    dve.wait_ge(varied, n + 1)
                    dve.tensor_scalar(yt[:, b, at:at + w], var_ps[n % 4][:, 0:w], 1e-5, None, ALU.add)\
                       .then_inc(eps_added, 1)
                for n, (b, at, w) in enumerate(jobs):
                    dve.wait_ge(rooted, 2 * n + 2)
                    dve.tensor_tensor(y[:, b, at:at + w], y[:, b, at:at + w], yt[:, b, at:at + w], ALU.mult)\
                       .then_inc(normed, 1)


def rel_terms(nc, name, QF, t, rel_dram):
    RG = 4
    LEAD = 16
    with Scope(nc, name) as s:
        table = s.sb("table", [CP, 2, HPC // 2, 2 * H - 1, 2])
        hi = s.sb("hi", [CP, 2, B, L], F16)
        lo = s.sb("lo", [CP, 2, B, L], F16)
        acc = [s.ps(f"acc{i}", [CP, CH]) for i in range(4)]
        loaded, ready, rounded, split = (s.sem(n) for n in ("loaded", "ready", "rounded", "split"))
        stored = [s.sem(f"stored{i}") for i in range(2)]
        rows = [(kind, p) for kind in range(2) for p in range(HPC // 2)]
        NR = len(rows)
        STORES = 16 * 2 * B
        NGR = H // RG
        jobs = [(r, g) for r in range(NR) for g in range(NGR)]
        J = len(jobs)

        def lead(eng, *sems):
            for x in sems:
                eng.sem_inc(x, LEAD)

        def banked(n):
            return acc[n % 4][:, 0:RG * B * H].rearrange("p (x b k) -> p x b k", b=B, k=H)

        def home(n, buf):
            r, g = jobs[n]
            im = buf[:, r % 2, :, :].rearrange("p b (h w) -> p b h w", w=W)
            if rows[r][0] == 0:
                return im[:, :, g * RG:(g + 1) * RG, :].rearrange("p b h w -> p h b w")
            return im[:, :, :, g * RG:(g + 1) * RG].rearrange("p b h w -> p w b h")

        with s.block() as block:
            @block.sync
            def _(sp):
                sp.dma_start(table[:], t["l3_rel"]).then_inc(loaded, 16)
                with sp.Fori(0, CC) as c:
                    for r, (kind, p) in enumerate(rows):
                        sp.wait_ge(split, c * J + (r + 1) * NGR + LEAD)
                        for b in range(B):
                            head = c * HPC + b * NH + 2 * p
                            for part, buf in enumerate((hi, lo)):
                                sp.dma_start(rel_dram[kind][part][bass.ds(head, 2), :, :].rearrange("e k l -> k e l"),
                                             buf[:, r % 2, b, :]).then_inc(stored[r % 2], 16)
                for x in stored:
                    sp.wait_ge(x, STORES * NR // 2 * CC + 1)

            @block.tensor
            def _(pe):
                pe.wait_ge(loaded, 16)
                lead(pe, ready)
                with pe.Fori(0, CC) as c:
                    for n, (r, g) in enumerate(jobs):
                        kind, p = rows[r]
                        q = QF[:, bass.ds(c, 1), :].rearrange("p a (b h w) -> p (a b) h w", b=B, w=W)
                        pe.wait_ge(split, c * J + n - 3 + LEAD)
                        for x in range(RG):
                            at = g * RG + x
                            rhs = q[:, :, at, :] if kind == 0 else q[:, :, :, at]
                            lhs = table[:, kind, p, H - 1 - at:2 * H - 1 - at, :].rearrange("p k e -> p (k e)")
                            mm = pe.matmul(acc[n % 4][:, x * B * H:(x + 1) * B * H], lhs, rhs, start=True, stop=True)
                        mm.then_inc(ready, 1)

            @block.scalar
            def _(act):
                lead(act, rounded)
                for x in stored:
                    act.sem_inc(x, 1)
                with act.Fori(0, CC) as c:
                    for n, (r, g) in enumerate(jobs):
                        act.wait_ge(ready, c * J + n + 1 + LEAD)
                        if g == 0:
                            act.wait_ge(stored[r % 2], c * (STORES * NR // 2) + r // 2 * STORES + 1)
                        act.activation(home(n, hi), banked(n), ACT.Copy).then_inc(rounded, 1)

            @block.vector
            def _(dve):
                lead(dve, split)
                with dve.Fori(0, CC) as c:
                    for n, (r, g) in enumerate(jobs):
                        dve.wait_ge(rounded, c * J + n + 1 + LEAD)
                        dve.tensor_tensor(home(n, lo), banked(n), home(n, hi), ALU.subtract).then_inc(split, 1)


def layer3_attention(nc, t, parts_dram, rel_dram, V, eye, o_dram, sum_dram):
    LEAD = 16
    KT = L // 128
    NQC = len(LCH)
    PAIRS = KT // 2
    SPH = NQC * PAIRS
    HPB = 2
    ST = SPH * HPB
    NMX = KT * NQC
    MX_FROM, MX_TO = 6, SPH - 5
    MT_AT = SPH - 3
    QUADS = [(qc, a, min(2, PAIRS - a)) for qc in range(NQC) for a in range(0, PAIRS, 2)]
    NQD = len(QUADS)
    ONE = 2 * HD
    ROW_SHIFT = 112
    with Scope(nc, "l3a") as s:
        QA = [s.sb(f"qa{i}", [128, L], F16) for i in range(2)]
        QB = [s.sb(f"qb{i}", [ROW_SHIFT + 1, L], F16) for i in range(2)]
        KA = [s.sb(f"ka{i}", [128, L], F16) for i in range(2)]
        KB = [s.sb(f"kb{i}", [ROW_SHIFT + 1, L], F16) for i in range(2)]
        VH = [s.sb(f"vh{i}", [128, KT, ONE]) for i in range(2)]
        P = s.sb("p", [128, 4, 2, CH])
        MX = s.sb("mx", [128, KT, NQC])
        M = s.sb("m", [128, KT])
        M16 = s.sb("m16", [KT, 128], F16)
        OS = s.sb("os", [128, 2, CH])
        OUT = [s.sb(f"out{i}", [HD + 1, L]) for i in range(2)]
        SEL = s.sb("sel", [128, HD + 1])
        s_ps = [s.ps(f"s{i}", [128, 2, CH]) for i in range(2)]
        mx_ps = [s.ps(f"mx{i}", [128, CH]) for i in range(2)]
        o_ps = s.ps("o", [128, CH])
        misc = s.ps("misc", [128, CH])
        consts, ones_set = s.sem("consts"), s.sem("ones_set")
        loaded = [s.sem(f"loaded{i}") for i in range(2)]
        v_ready = [s.sem(f"v_ready{i}") for i in range(2)]
        shift_loaded = [s.sem(f"shift_loaded{i}") for i in range(2)]
        out_stored = [s.sem(f"out_stored{i}") for i in range(2)]
        scored, exped, summed, o_taken, misc_made, misc_taken, mx_made, mx_taken, m_made, m16_made = (
            s.sem(n) for n in ("scored", "exped", "summed", "o_taken", "misc_made", "misc_taken", "mx_made",
                               "mx_taken", "m_made", "m16_made"))
        LOADS = 10 * 16
        START = {scored: ST, summed: 2 * NQD}

        quad_at, qc_end_at, mx_at = {}, {}, {}
        quad_of = {}
        for e in range(HPB):
            for q, (qc, a, n) in enumerate(QUADS):
                last = e * SPH + qc * PAIRS + a + n - 1
                for k in range(n):
                    quad_of[last - k] = e * NQD + q
                quad_at.setdefault(last + 2, []).append((e, q))
                if a + n == PAIRS:
                    qc_end_at.setdefault(last + 3, []).append((e, qc))
            places = [(e * SPH + x, place) for x in range(MX_FROM, MX_TO) for place in range(3)]
            for u in range(NMX):
                mx_at.setdefault(places[u * len(places) // NMX], []).append((e, u))
        MISC = NQC * HPB + HPB

        def misc_index(e, what):
            order = []
            for g in range(ST + 3):
                order += [x for x in qc_end_at.get(g, [])]
                if g < ST and g % SPH == MT_AT:
                    order.append((g // SPH, "m"))
            return order.index((e, what))

        def lead(eng, *sems):
            for x in sems:
                eng.sem_inc(x, START.get(x, LEAD))

        def load_head(sp, head, buf):
            row = head * HD
            qk = [(QA, 0, 0, 0), (QA, 112, 0, 0), (QB, 0, 0, 1), (KA, 0, 1, 0), (KA, 112, 1, 1), (KB, 0, 1, 0)]
            for dst, at, which, part in qk:
                sp.dma_start(dst[buf][at:at + HD, :], parts_dram[which][part][bass.ds(row, HD), :])\
                  .then_inc(loaded[buf], 16)
            for dst, part in ((QA, 0), (QB, 1)):
                for at, kind in ((16, 1), (64, 0)):
                    sp.dma_start(dst[buf][at:at + H, :],
                                 rel_dram[kind][part][bass.ds(head, 1), :, :].rearrange("a k l -> (a k) l"))\
                      .then_inc(loaded[buf], 16)

        def load_shift(sp, buf):
            sp.dma_start(QB[buf][ROW_SHIFT:ROW_SHIFT + 1, :].rearrange("a (t q) -> a t q", q=128), M16[:, :])\
              .then_inc(shift_loaded[buf], 16)

        with s.block() as block:
            @block.sync
            def _(sp):
                for i in range(2):
                    sp.dma_start(KA[i][16:112, :], t["l3_places"][0:96, :]).then_inc(consts, 16)
                    sp.dma_start(KB[i][16:113, :], t["l3_places"]).then_inc(consts, 16)
                sp.dma_start(SEL[:], t["l3_sel"]).then_inc(consts, 16)
                load_head(sp, 0, 0)
                sp.wait_ge(m16_made, 1 + LEAD)
                load_shift(sp, 0)
                with sp.Fori(0, BH // HPB) as i:
                    for e in range(HPB):
                        nxt = (i * HPB + e + 1) % BH if e == HPB - 1 else i * HPB + e + 1
                        sp.wait_ge(scored, i * ST + e * SPH + ST)
                        load_head(sp, nxt, 1 - e)
                        sp.wait_ge(m16_made, i * HPB + e + 2 + LEAD)
                        load_shift(sp, 1 - e)
                        sp.wait_ge(misc_taken, i * MISC + 1 + misc_index(e, NQC - 1) + 1 + LEAD)
                        row = i * (HPB * HD) + e * HD
                        sp.dma_start(o_dram[bass.ds(row, HD), :], OUT[e][0:HD, :]).then_inc(out_stored[e], 16)
                        sp.dma_start(sum_dram[bass.ds(i * HPB + e, 1), :], OUT[e][HD:HD + 1, :])\
                          .then_inc(out_stored[e], 16)
                for x in out_stored:
                    sp.wait_ge(x, 32 * BH // HPB + 1)
                sp.wait_ge(shift_loaded[0], 16 * (BH // HPB + 1))

            @block.gpsimd
            def _(pool):
                for i in range(2):
                    pool.memset(VH[i][:, :, HD:ONE], 1.0).then_inc(ones_set, 1)

                with pool.Fori(0, B) as b:
                    with pool.Fori(0, NH // HPB) as j:
                        i = pool.snap(b * (NH // HPB) + j)
                        for e in range(HPB):
                            pool.wait_ge(summed, i * HPB * NQD + (e + 1) * NQD)
                            pool.wait_ge(ones_set, 2)
                            pool.tensor_copy(VH[e][:, :, 0:HD].unsqueeze(2),
                                             V[:, bass.ds(b * KT, KT), bass.ds(j * HPB + e, 1), :])\
                                .then_inc(v_ready[e], 1)

            @block.tensor
            def _(pe):
                pe.wait_ge(consts, 16 * 5)
                lead(pe, scored, summed, misc_made, mx_made)

                def mx_pass(buf, u, base):
                    qt, c = divmod(u, NQC)
                    at, w = LCH[c]
                    pe.wait_ge(mx_taken, base + u - 1 + LEAD)
                    pe.matmul(mx_ps[u % 2][:, 0:w], QA[buf][:, qt * 128:(qt + 1) * 128], KA[buf][:, at:at + w],
                              start=True, stop=True).then_inc(mx_made, 1)

                def turn_shift(count, uses):
                    pe.wait_ge(m_made, count + LEAD)
                    pe.wait_ge(misc_taken, uses + LEAD)
                    pe.transpose(misc[0:KT, 0:128], M[:], eye[:, :]).then_inc(misc_made, 1)

                def score(i, g, y):
                    e, x = divmod(g, SPH)
                    at, w = LCH[x // PAIRS]
                    if y == 0:
                        if x == 0:
                            pe.wait_ge(shift_loaded[e], (i + 1) * 16)
                        pe.wait_ge(exped, i * ST + g - 1 + LEAD)
                    kt = 2 * (x % PAIRS) + y
                    out = s_ps[g % 2][:, y, 0:w]
                    keys = slice(kt * 128, (kt + 1) * 128)
                    pe.matmul(out, KA[e][:, keys], QA[e][:, at:at + w], start=True, stop=False)
                    mm = pe.matmul(out, KB[e][:, keys], QB[e][:, at:at + w], start=False, stop=True)
                    if y == 1:
                        mm.then_inc(scored, 1)

                def maxima(i, g, place):
                    for e, u in mx_at.get((g, place), []):
                        if u == 0:
                            pe.wait_ge(loaded[1 - e], (i + 1 + e) * LOADS)
                        mx_pass(1 - e, u, i * HPB * NMX + (e + 1) * NMX)

                def values(i, e, q):
                    qc, a, n = QUADS[q]
                    w = LCH[qc][1]
                    last = e * SPH + qc * PAIRS + a + n - 1
                    pe.wait_ge(exped, i * ST + last + 1 + LEAD)
                    if q == 0:
                        pe.wait_ge(v_ready[e], i + 1)
                    if a == 0:
                        pe.wait_ge(o_taken, i * HPB * NQC + e * NQC + qc + LEAD)
                    for k in range(2 * n):
                        kt = 2 * a + k
                        g = e * SPH + qc * PAIRS + kt // 2
                        grp = kt % 4
                        mm = pe.matmul(o_ps[32 * grp:32 * grp + 32, 0:w], VH[e][:, kt, :], P[:, g % 4, kt % 2, 0:w],
                                       start=a == 0, stop=kt + 4 >= KT)
                    mm.then_inc(summed, 1)

                def add_groups(i, e, qc):
                    n = e * NQC + qc
                    w = LCH[qc][1]
                    pe.wait_ge(o_taken, i * HPB * NQC + n + 1 + LEAD)
                    pe.wait_ge(misc_taken, i * MISC + 1 + misc_index(e, qc) + LEAD)
                    pe.matmul(misc[0:HD + 1, 0:w], SEL[:], OS[:, n % 2, 0:w], start=True, stop=True).then_inc(misc_made, 1)

                pe.wait_ge(loaded[0], LOADS)
                for u in range(NMX):
                    mx_pass(0, u, 0)
                turn_shift(1, 0)
                with pe.Fori(0, BH // HPB) as i:
                    for g in range(ST + 4):
                        if g < ST:
                            score(i, g, 0)
                            maxima(i, g, 0)
                            score(i, g, 1)
                            maxima(i, g, 1)
                        for e, q in quad_at.get(g, []):
                            values(i, e, q)
                        for e, qc in qc_end_at.get(g, []):
                            add_groups(i, e, qc)
                        maxima(i, g, 2)
                        if g < ST and g % SPH == MT_AT:
                            e = g // SPH
                            turn_shift(i * HPB + e + 2, i * MISC + 1 + misc_index(e, "m"))

            @block.scalar
            def _(act):
                lead(act, exped)
                with act.Fori(0, BH // HPB) as i:
                    for g in range(ST):
                        w = LCH[g % SPH // PAIRS][1]
                        act.wait_ge(scored, i * ST + g + 1 + ST)
                        before = quad_of[g - 4] + 1 if g >= 4 else 0
                        act.wait_ge(summed, i * HPB * NQD + before + 2 * NQD)
                        act.activation(P[:, g % 4, :, 0:w], s_ps[g % 2][:, :, 0:w], ACT.Exp).then_inc(exped, 1)

            @block.vector
            def _(dve):
                lead(dve, o_taken, misc_taken, mx_taken, m_made, m16_made)
                for x in out_stored:
                    dve.sem_inc(x, 1)

                def mx_take(u, base):
                    qt, c = divmod(u, NQC)
                    dve.wait_ge(mx_made, base + u + 1 + LEAD)
                    dve.tensor_reduce(MX[:, qt, c:c + 1], mx_ps[u % 2][:, 0:LCH[c][1]], AX_X, ALU.max)\
                       .then_inc(mx_taken, 1)

                def mx_join(base, count, uses):
                    dve.wait_ge(mx_taken, base + NMX + LEAD)
                    dve.wait_ge(misc_made, uses + LEAD)
                    dve.tensor_reduce(M[:], MX[:], AX_X, ALU.max).then_inc(m_made, 1)

                def m16(uses, shifts):
                    dve.wait_ge(misc_made, uses + LEAD)
                    for sem, n in shifts:
                        dve.wait_ge(sem, n)
                    dve.tensor_scalar(M16[:], misc[0:KT, 0:128], -1.0, None, ALU.mult).then_inc(m16_made, 1)

                def take_o(i, e, qc):
                    n = e * NQC + qc
                    w = LCH[qc][1]
                    dve.wait_ge(summed, i * HPB * NQD + e * NQD + (qc + 1) * (NQD // NQC) + 2 * NQD)
                    dve.tensor_copy(OS[:, n % 2, 0:w], o_ps[:, 0:w]).then_inc(o_taken, 1)

                def take_sums(i, e, qc):
                    at, w = LCH[qc]
                    dve.wait_ge(misc_made, i * MISC + 1 + misc_index(e, qc) + 1 + LEAD)
                    if qc == 0:
                        dve.wait_ge(out_stored[e], i * 32 + 1)
                    dve.tensor_copy(OUT[e][:, at:at + w], misc[0:HD + 1, 0:w]).then_inc(misc_taken, 1)

                def maxima(i, g, place):
                    for e, u in mx_at.get((g, place), []):
                        base = i * HPB * NMX + (e + 1) * NMX
                        mx_take(u, base)
                        if u == NMX - 1:
                            mx_join(base, 0, i * MISC + 1 + (misc_index(0, "m") + 1 if e else 0))

                for u in range(NMX):
                    mx_take(u, 0)
                mx_join(0, 1, 0)
                m16(1, [])
                dve.wait_ge(m16_made, 1 + LEAD)
                dve.sem_inc(misc_taken, 1)
                with dve.Fori(0, BH // HPB) as i:
                    for g in range(ST + 4):
                        maxima(i, g, 0)
                        maxima(i, g, 1)
                        for e, q in quad_at.get(g, []):
                            if QUADS[q][1] + QUADS[q][2] == PAIRS:
                                take_o(i, e, QUADS[q][0])
                        for e, qc in qc_end_at.get(g, []):
                            take_sums(i, e, qc)
                        maxima(i, g, 2)
                        if g < ST and g % SPH == MT_AT:
                            e = g // SPH
                            uses = i * MISC + 1 + misc_index(e, "m") + 1
                            m16(uses, [(shift_loaded[e], (i + 1) * 16)])
                            dve.wait_ge(m16_made, i * HPB + e + 2 + LEAD)
                            dve.sem_inc(misc_taken, 1)


def load_output(nc, name, o_dram, sum_dram, inv_dram, OT, patches=False):
    with Scope(nc, name) as s:
        SUMS = s.sb("sums", [128, BH * L // 128])
        INV = s.sb("inv", [128, BH * L // 128])
        SPREAD = s.sb("spread", [CP, CC, TOK])
        RAW = s.sb("raw", [CP, CC, TOK]) if patches else OT
        sums_loaded, inverted, inv_stored, divided = (s.sem(n) for n in (
            "sums_loaded", "inverted", "inv_stored", "divided"))
        rows = [(c, b) for c in range(CC) for b in range(B)]
        loaded = [s.sem(f"loaded{i}") for i in range(len(rows))]
        spread = [s.sem(f"spread{i}") for i in range(len(rows))]
        flat = lambda d: d[:, :].rearrange("a l -> (a l)").rearrange("(p n) -> p n", p=128)
        with s.block() as block:
            @block.sync
            def _(sp):
                sp.dma_start(SUMS[:], flat(sum_dram)).then_inc(sums_loaded, 16)
                for r, (c, b) in enumerate(rows):
                    sp.dma_start(RAW[:, c, b * L:(b + 1) * L],
                                 o_dram[b * C + c * CP:b * C + (c + 1) * CP, :]).then_inc(loaded[r], 16)
                sp.wait_ge(inverted, 1)
                sp.dma_start(flat(inv_dram), INV[:]).then_inc(inv_stored, 16)
                sp.wait_ge(inv_stored, 16)
                for r, (c, b) in enumerate(rows):
                    for h in range(HPC):
                        head = b * NH + c * HPC + h
                        sp.dma_start(SPREAD[h * HD:(h + 1) * HD, c, b * L:(b + 1) * L],
                                     inv_dram[head:head + 1, :].to_broadcast([HD, L])).then_inc(spread[r], 16)

            @block.vector
            def _(dve):
                dve.wait_ge(sums_loaded, 16)
                dve.reciprocal(INV[:], SUMS[:]).then_inc(inverted, 1)
                for r, (c, b) in enumerate(rows):
                    dve.wait_ge(loaded[r], 16)
                    dve.wait_ge(spread[r], 16 * HPC)
                    strips = NPH if patches else 1
                    for g in range(strips):
                        tokens = slice(b * L + g * (L // strips), b * L + (g + 1) * (L // strips))
                        home, raw, inv = OT[:, c, tokens], RAW[:, c, tokens], SPREAD[:, c, tokens]
                        if patches:
                            home = home.rearrange("p (h x w) -> p x h w", x=NPW, w=PW)
                            raw, inv = (m.rearrange("p (x h w) -> p x h w", x=NPW, w=PW) for m in (raw, inv))
                        dve.tensor_tensor(home, raw, inv, ALU.mult).then_inc(divided, 1)
                dve.wait_ge(divided, len(rows) * (NPH if patches else 1))


def build(nc, t, out):
    with ExitStack() as outer:
        g = Scope(nc, "g")
        outer.enter_context(g)
        X = g.sb("x", [CP, CC, TOK])
        group_mean = g.sb("group_mean", [CP, CP])
        eye = g.sb("eye", [128, 128])
        ones_mean = g.sb("ones_mean", [DI, DI])

        def dram(name, shape, dtype):
            return nc.dram_tensor(name, shape, dtype, kind="Internal").ap()

        def load(sp, sem):
            for c in range(CC):
                for b in range(B):
                    sp.dma_start(X[:, c, b * L:(b + 1) * L], t["xT"][c * CP:(c + 1) * CP, b * L:(b + 1) * L])\
                      .then_inc(sem, 16)
            sp.dma_start(group_mean[:], t["group_mean"]).then_inc(sem, 16)
            sp.dma_start(eye[:], t["eye"]).then_inc(sem, 16)
            sp.dma_start(ones_mean[:], t["ones_mean"]).then_inc(sem, 16)
        load.total = 16 * (CC * B + 3)

        with Scope(nc, "l0") as s0:
            parts = [[dram(f"l0_{w}{p}", [B * C, LK], F16) for p in range(2)] for w in "qk"]
            v_dram = dram("l0_values", [TOK + 128, C], F32)
            o_dram = dram("l0_out", [B * C, L], F32)
            sum_dram = dram("l0_sums", [BH, L], F32)
            inv_dram = dram("l0_inverses", [BH, L], F32)
            V = s0.sb("v", [110, B * NPT, len(CUTS), NH, HD])
            v_stored, v_loaded = s0.sem("v_stored"), s0.sem("v_loaded")

            def patch_loads():
                def transfer(dst, src):
                    return lambda sp: sp.dma_start(dst.rearrange("p h e -> p (h e)"), src).then_inc(v_loaded, 16)

                loads = []
                reg_at = CUTS[-1][1] * KW
                for b in range(B):
                    for p in range(NPT):
                        _, (kr, kc), _ = window_of(p)
                        for c, (r0, nr) in enumerate(CUTS):
                            src = v_dram[b * L:(b + 1) * L, :].rearrange("(h w) e -> h w e", w=W)
                            loads.append(transfer(V[0:nr * KW, b * NPT + p, c, :, :],
                                                  src[kr + r0:kr + r0 + nr, kc:kc + KW, :]))
                        loads.append(transfer(V[reg_at:reg_at + NREG, b * NPT + p, len(CUTS) - 1, :, :],
                                              v_dram[TOK:TOK + NREG, :]))
                return loads

            with Scope(nc, "l0n") as sn:
                XN = sn.sb("xn", [CP, CC, TOK])
                group_norm(nc, "gn0", X, XN, group_mean, load)
                with Scope(nc, "l0vt") as sv:
                    VT = sv.sb("vt", [128, TOK // 128 + 1, NH, HD])
                    v_projection(nc, "l0v", XN, t["l0_wT"], t["L0_conv_qkv_b"], VT, regs=t["l0_regsT"])
                    with nc.Block() as block:
                        @block.sync
                        def _(sp):
                            half = TOK // 256
                            for k in range(2):
                                sp.dma_start(
                                    v_dram[0:TOK, :].rearrange("(n p) e -> p n e", p=128)[:, k * half:(k + 1) * half, :],
                                    VT[:, k * half:(k + 1) * half, :, :].rearrange("p n h e -> p n (h e)"))\
                                  .then_inc(v_stored, 16)
                            sp.dma_start(v_dram[TOK:TOK + NREG, :],
                                         VT[0:NREG, TOK // 128, :, :].rearrange("p h e -> p (h e)")).then_inc(v_stored, 16)
                            sp.wait_ge(v_stored, 48)
                qk_projection(nc, "l0qk", XN, t["l0_wT"], t["L0_conv_qkv_b"], parts, regs=t["l0_regsT"],
                              early=patch_loads(), patches=True)
            with nc.Block() as block:
                @block.sync
                def _(sp):
                    sp.wait_ge(v_loaded, 16 * B * NPT * (len(CUTS) + 1))
            layer0_attention(nc, parts, V, t["l0_mask"], t["eye_bf"], eye, o_dram, sum_dram)
        with Scope(nc, "l0o") as so:
            OT = so.sb("ot", [CP, CC, TOK])
            load_output(nc, "l0t", o_dram, sum_dram, inv_dram, OT, patches=True)
            out_projection(nc, "l0p", X, OT, t["l0_owT"], t["L0_conv_out_b"], CP, CC)

        for layer in (1, 2):
            pre = f"l{layer}_"
            z_dram = dram(pre + "z", [DI, TOK], F32)
            skip_dram = dram(pre + "skip", [B, DI, L], F32)
            dt_dram = dram(pre + "dtp", [B * ND, 4, 3, 8, 3, L], BF16)
            du_dram = dram(pre + "dup", [B * ND, 4, 3, 8, 3, L], BF16)
            bc_dram = dram(pre + "bcp", [B * ND * 2, 3, NS, L], BF16)
            y_dram = dram(pre + "y", [B * 2 + 1, DI, L], F32)
            with Scope(nc, pre + "u") as su:
                U = su.sb("u", [DI, B, L])
                UT = su.sb("ut", [DI, B, L])
                with Scope(nc, pre + "n") as sn:
                    XN = sn.sb("xn", [CP, CC, TOK])
                    group_norm(nc, f"gn{layer}", X, XN, group_mean)
                    ssm_conv(nc, pre + "conv", XN, t, pre, U, UT, z_dram)
                ssm_prepare(nc, pre + "prep", t, pre, U, UT, dt_dram, du_dram, bc_dram, skip_dram)
            ssm_scan(nc, pre + "scan", t, pre, dt_dram, du_dram, bc_dram, y_dram)
            with Scope(nc, pre + "o") as so:
                YG = so.sb("yg", [DI, 1, TOK])
                ssm_gate(nc, pre + "gate", t, pre, ones_mean, y_dram, skip_dram, z_dram, YG)
                out_projection(nc, pre + "proj", X, YG, t[pre + "owT"], None, DI, 1)

        parts = [[dram(f"l3_{w}{p}", [B * C, L], F16) for p in range(2)] for w in "qk"]
        rel = [[dram(f"l3_rel{k}{p}", [BH, H, L], F16) for p in range(2)] for k in range(2)]
        o_dram = dram("l3_out", [B * C, L], F32)
        sum_dram = dram("l3_sums", [BH, L], F32)
        inv_dram = dram("l3_inverses", [BH, L], F32)
        with Scope(nc, "l3") as s3:
            V = s3.sb("v", [128, TOK // 128, NH, HD])
            with Scope(nc, "l3q") as sq:
                QF = sq.sb("qf", [CP, CC, TOK])
                with Scope(nc, "l3n") as sn:
                    XN = sn.sb("xn", [CP, CC, TOK])
                    group_norm(nc, "gn3", X, XN, group_mean)
                    v_projection(nc, "l3v", XN, t["l3_wT"], t["l3_b"], V)
                    qk_projection(nc, "l3qk", XN, t["l3_wT"], t["l3_b"], parts, q_keep=QF)
                rel_terms(nc, "l3r", QF, t, rel)
            layer3_attention(nc, t, parts, rel, V, eye, o_dram, sum_dram)
        with Scope(nc, "l3o") as so:
            OT = so.sb("ot", [CP, CC, TOK])
            load_output(nc, "l3l", o_dram, sum_dram, inv_dram, OT)
            out_projection(nc, "l3p", X, OT, t["l3_pwT"], t["l3_pb"], CP, CC)

        stored = g.sem("stored")
        with nc.Block() as block:
            @block.sync
            def _(sp):
                for c in range(CC):
                    sp.dma_start(out[c * CP:(c + 1) * CP, :], X[:, c, :]).then_inc(stored, 16)
                sp.wait_ge(stored, 16 * CC)


def shape_constants():
    bf16 = mybir.dt.np(BF16)
    k = {}
    p = np.arange(CP)
    k["group_mean"] = (p[:, None] // GC == p[None, :] // GC).astype(np.float32) / GC
    k["ones_mean"] = np.full((DI, DI), 1.0 / DI, np.float32)
    r, q = np.arange(128)[:, None], np.arange(128)[None]
    k["e4"] = ((r % 32 < 24) & (r % 32 % 8 == q // NS)).astype(bf16)
    k["en"] = (r[:3 * NS] % NS == q % NS).astype(bf16)
    col = np.arange(32)[None, None]
    k["state_sum"] = (col == 8 * np.arange(4)[None, :, None] + np.arange(128)[:, None, None] // NS).astype(np.float32)
    places = np.zeros((97, L), np.float16)
    places[np.arange(L) % W, np.arange(L)] = 1
    places[W + np.arange(L) // W, np.arange(L)] = 1
    places[96] = 1
    k["l3_places"] = places
    sel = np.zeros((128, HD + 1), np.float32)
    for grp in range(4):
        for d in range(HD + 1):
            sel[32 * grp + d, d] = 1
    k["l3_sel"] = sel
    k["eye"] = np.eye(128, dtype=np.float32)
    k["eye_bf"] = np.eye(128).astype(bf16)
    mask = np.zeros((9, PH * PW, WK + NREG), np.float32)
    for p in range(NPT):
        (qr, qc), (kr, kc), kind = window_of(p)
        qh, qw = np.divmod(np.arange(PH * PW), PW)
        kh, kw = np.divmod(np.arange(WK), KW)
        sh = np.clip(qh + qr - WIN // 2, 0, H - WIN)[:, None]
        sw = np.clip(qw + qc - WIN // 2, 0, W - WIN)[:, None]
        kh, kw = (kh + kr)[None], (kw + kc)[None]
        seen = (kh >= sh) & (kh < sh + WIN) & (kw >= sw) & (kw < sw + WIN)
        mask[kind, :, :WK] = np.where(seen, 0.0, -1e30)
    k["l0_mask"] = mask.astype(bf16)
    return k


def kernel(**inputs):
    import concourse.bacc as bacc
    from concourse.bass_utils import run_bass_kernel_spmd

    a = {n: np.ascontiguousarray(v) for n, v in inputs.items()}
    turned = lambda m: np.ascontiguousarray(m.T)
    data = {
        "xT": turned(a["x"].reshape(TOK, C)),
        "l0_wT": turned(a["L0_conv_qkv_w"]), "l0_regsT": turned(a["L0_conv_registers"]),
        "L0_conv_qkv_b": a["L0_conv_qkv_b"], "l0_owT": turned(a["L0_conv_out_w"]),
        "L0_conv_out_b": a["L0_conv_out_b"],
        **shape_constants(),
    }
    w = {n[8:]: v for n, v in a.items() if n.startswith("L3_conv_")}
    data["l3_wT"], data["l3_b"], data["l3_pwT"], data["l3_pb"] = w["qkv_w"], w["qkv_b"], w["proj_w"], w["proj_b"]
    rel = np.zeros((CP, 2, HPC // 2, 2 * H - 1, 2), np.float32)
    for kind, n in enumerate(("rel_pos_h", "rel_pos_w")):
        rows = np.minimum(np.arange(2 * H - 2, -1, -1), len(w[n]) - 1)
        for head in range(HPC):
            rel[head * HD:(head + 1) * HD, kind, head // 2, :, head % 2] = w[n][rows].T
    data["l3_rel"] = rel
    for layer in (1, 2):
        w = {n[8:]: v for n, v in a.items() if n.startswith(f"L{layer}_conv_")}
        p = f"l{layer}_"
        data[p + "in_wT"] = turned(w["in_proj_w"])
        data[p + "conv_w"] = w["conv_w"].reshape(DI, 9)
        data[p + "conv_b"] = w["conv_b"].reshape(DI, 1)
        xw = np.zeros((ND, DI, CP), np.float32)
        xw[:, :, 0:DT_R] = w["x_proj_w"][:, 0:DT_R].transpose(0, 2, 1)
        xw[:, :, 32:32 + NS] = w["x_proj_w"][:, DT_R:DT_R + NS].transpose(0, 2, 1)
        xw[:, :, 64:64 + NS] = w["x_proj_w"][:, DT_R + NS:].transpose(0, 2, 1)
        data[p + "xwT"] = xw
        data[p + "dtwT"] = np.ascontiguousarray(w["dt_projs_w"].transpose(0, 2, 1))
        data[p + "dtb"] = turned(w["dt_projs_b"])
        data[p + "D"] = turned(w["Ds"].reshape(ND, DI))
        al = w["A_logs"].reshape(2, 2, 3, 4, 8, NS).transpose(4, 5, 1, 0, 3, 2)
        data[p + "A"] = np.ascontiguousarray(al.reshape(128, 48))
        data[p + "norm_g"] = w["out_norm_g"].reshape(DI, 1)
        data[p + "norm_b"] = w["out_norm_b"].reshape(DI, 1)
        data[p + "owT"] = turned(w["out_proj_w"])
    nc = bacc.Bacc("TRN2", target_bir_lowering=False, num_devices=1)
    t = {n: nc.dram_tensor(f"in_{n}", v.shape, mybir.dt.from_np(v.dtype), kind="ExternalInput").ap()
         for n, v in data.items()}
    out = nc.dram_tensor("out", (C, TOK), F32, kind="ExternalOutput").ap()
    build(nc, t, out)
    r = run_bass_kernel_spmd(nc, [{f"in_{n}": v for n, v in data.items()}], core_ids=[0])
    return np.ascontiguousarray(r.results[0]["out"].T).reshape(B, H, W, C)
```
